# Optimizing a Trainium2 kernel written in Bass

```python
import numpy as np
import jax
import jax.numpy as jnp

def _softmax(x, axis=-1):
    return jax.nn.softmax(x, axis=axis)

def _gelu(x):
    return jax.nn.gelu(x, approximate=True)

def _silu(x):
    return jax.nn.silu(x)

def _sigmoid(x):
    return jax.nn.sigmoid(x)

def _layernorm(x, axis=-1, eps=1e-05):
    m = jnp.mean(x, axis=axis, keepdims=True)
    v = jnp.var(x, axis=axis, keepdims=True)
    return (x - m) / jnp.sqrt(v + eps)

def _scatter_add(tgt, idx, src, axis=0):
    return tgt.at[idx].add(src)

def _segment_sum(src, seg, n):
    return jax.ops.segment_sum(src, seg, n)
kernel_name = 'mk_seq_preln_d2_jaxref_r8_831427'

def setup_inputs(seed: int=0):
    np.random.seed(seed)
    _w = jnp.asarray

    def _L0_attn_setup():
        import jax, jax.numpy as jnp
        import numpy as np
        DIM = 128
        N_HEADS = 16
        HEAD_DIM = DIM // N_HEADS
        HIDDEN = 352
        WINDOW_PER_SIDE = 128
        EPS = 1e-05
        THETA = 10000.0

        def rope_cos_sin(seqlen, head_dim):
            freqs = 1.0 / THETA ** (jnp.arange(0, head_dim, 2, dtype=jnp.float32) / head_dim)
            t = jnp.arange(seqlen, dtype=jnp.float32)
            ang = jnp.outer(t, freqs)
            return (jnp.cos(ang), jnp.sin(ang))

        def apply_rope(x, cos, sin):
            xr = x[..., 0::2]
            xi = x[..., 1::2]
            c = cos[None, :, None, :]
            s = sin[None, :, None, :]
            or_ = xr * c - xi * s
            oi_ = xr * s + xi * c
            return jnp.stack([or_, oi_], axis=-1).reshape(x.shape)

        def layernorm(x, g, b):
            mu = jnp.mean(x, axis=-1, keepdims=True)
            var = jnp.mean(jnp.square(x - mu), axis=-1, keepdims=True)
            return (x - mu) * jax.lax.rsqrt(var + EPS) * g + b

        def attention(x, wq, wk, wv, wo):
            b, s, _ = x.shape
            scale = HEAD_DIM ** (-0.5)
            q = (x @ wq).reshape(b, s, N_HEADS, HEAD_DIM)
            k = (x @ wk).reshape(b, s, N_HEADS, HEAD_DIM)
            v = (x @ wv).reshape(b, s, N_HEADS, HEAD_DIM)
            cos, sin = rope_cos_sin(s, HEAD_DIM)
            q = apply_rope(q, cos, sin)
            k = apply_rope(k, cos, sin)
            i = jnp.arange(s)[:, None]
            j = jnp.arange(s)[None, :]
            mask = (j <= i) & (i - j <= WINDOW_PER_SIDE)
            scores = jnp.einsum('bqhd,bkhd->bhqk', q, k) * scale
            scores = jnp.where(mask[None, None], scores, jnp.finfo(scores.dtype).min)
            probs = jax.nn.softmax(scores, axis=-1)
            out = jnp.einsum('bhqk,bkhd->bqhd', probs, v).reshape(b, s, -1)
            return out @ wo

        def ffn(x, w1, w2, w3):
            return jax.nn.silu(x @ w1) * (x @ w3) @ w2
        key = jax.random.key(seed)
        ks = jax.random.split(key, 9)
        sd = 0.02
        x = jax.random.normal(ks[0], (4, 256, DIM), dtype=jnp.float32)
        wq = jax.random.normal(ks[1], (DIM, DIM), dtype=jnp.float32) * sd
        wk = jax.random.normal(ks[2], (DIM, DIM), dtype=jnp.float32) * sd
        wv = jax.random.normal(ks[3], (DIM, DIM), dtype=jnp.float32) * sd
        wo = jax.random.normal(ks[4], (DIM, DIM), dtype=jnp.float32) * sd
        w1 = jax.random.normal(ks[5], (DIM, HIDDEN), dtype=jnp.float32) * sd
        w2 = jax.random.normal(ks[6], (HIDDEN, DIM), dtype=jnp.float32) * sd
        w3 = jax.random.normal(ks[7], (DIM, HIDDEN), dtype=jnp.float32) * sd
        ln1_g = jnp.ones((DIM,), jnp.float32)
        ln1_b = jnp.zeros((DIM,), jnp.float32)
        ln2_g = jnp.ones((DIM,), jnp.float32)
        ln2_b = jnp.zeros((DIM,), jnp.float32)
        return dict(x=x, wq=wq, wk=wk, wv=wv, wo=wo, w1=w1, w2=w2, w3=w3, ln1_g=ln1_g, ln1_b=ln1_b, ln2_g=ln2_g, ln2_b=ln2_b)
    _L0_attn_in = _L0_attn_setup()

    def _L0_ffn_setup():
        import jax, jax.numpy as jnp
        import numpy as np
        EPS = 1e-09
        key = jax.random.key(seed)
        k0, k1, k2, k3 = jax.random.split(key, 4)
        B, S, H, F, E = (4, 256, 128, 256, 8)
        return {'hidden_states': jax.random.normal(k0, (B, S, H), dtype=jnp.float32), 'router_w': jax.random.normal(k1, (H, E), dtype=jnp.float32) * 0.02, 'w1': jax.random.normal(k2, (E, H, F), dtype=jnp.float32) * 0.02, 'w2': jax.random.normal(k3, (E, F, H), dtype=jnp.float32) * 0.02}
    _L0_ffn_in = _L0_ffn_setup()

    def _L1_attn_setup():
        import jax, jax.numpy as jnp
        import numpy as np
        HEADS = 16
        WINDOW = 128
        key = jax.random.key(seed)
        k1, k2, k3, k4 = jax.random.split(key, 4)
        B, N, C = (2, 256, 128)
        x = jax.random.normal(k1, (B, N, C), dtype=jnp.float32)
        w_qkv = jax.random.normal(k2, (3 * C, C), dtype=jnp.float32) * C ** (-0.5)
        w_out = jax.random.normal(k3, (C, C), dtype=jnp.float32) * C ** (-0.5)
        b_out = jax.random.normal(k4, (C,), dtype=jnp.float32) * 0.01
        return {'x': x, 'w_qkv': w_qkv, 'w_out': w_out, 'b_out': b_out}
    _L1_attn_in = _L1_attn_setup()

    def _L1_ffn_setup():
        import jax, jax.numpy as jnp
        import numpy as np
        B, S, D = (4, 256, 128)
        O = 128
        E = 8
        K = 2
        key = jax.random.key(seed)
        k1, k2, k3, k4, k5 = jax.random.split(key, 5)
        scale = 1.0 / np.sqrt(D)
        x = jax.random.normal(k1, (B, S, D), dtype=jnp.float32)
        We = jax.random.uniform(k2, (E, D, O), dtype=jnp.float32, minval=-scale, maxval=scale)
        be = jax.random.uniform(k3, (E, O), dtype=jnp.float32, minval=-scale, maxval=scale)
        Wg = jax.random.uniform(k4, (D, E), dtype=jnp.float32, minval=-scale, maxval=scale)
        bg = jax.random.uniform(k5, (E,), dtype=jnp.float32, minval=-scale, maxval=scale)
        return {'x': x, 'We': We, 'be': be, 'Wg': Wg, 'bg': bg}
    _L1_ffn_in = _L1_ffn_setup()
    _d = {'L0_attn_x': _L0_attn_in['x'], 'L0_attn_wq': _L0_attn_in['wq'], 'L0_attn_wk': _L0_attn_in['wk'], 'L0_attn_wv': _L0_attn_in['wv'], 'L0_attn_wo': _L0_attn_in['wo'], 'L0_attn_w1': _L0_attn_in['w1'], 'L0_attn_w2': _L0_attn_in['w2'], 'L0_attn_w3': _L0_attn_in['w3'], 'L0_attn_ln1_g': _L0_attn_in['ln1_g'], 'L0_attn_ln1_b': _L0_attn_in['ln1_b'], 'L0_attn_ln2_g': _L0_attn_in['ln2_g'], 'L0_attn_ln2_b': _L0_attn_in['ln2_b'], 'L0_ffn_router_w': _L0_ffn_in['router_w'], 'L0_ffn_w1': _L0_ffn_in['w1'], 'L0_ffn_w2': _L0_ffn_in['w2'], 'L1_attn_w_qkv': _L1_attn_in['w_qkv'], 'L1_attn_w_out': _L1_attn_in['w_out'], 'L1_attn_b_out': _L1_attn_in['b_out'], 'L1_ffn_We': _L1_ffn_in['We'], 'L1_ffn_be': _L1_ffn_in['be'], 'L1_ffn_Wg': _L1_ffn_in['Wg'], 'L1_ffn_bg': _L1_ffn_in['bg']}
    _x0 = _d['L0_attn_x']
    _d['L0_attn_x'] = jax.random.normal(jax.random.fold_in(jax.random.key(seed), 1), (8, 512, 128), dtype=_x0.dtype)
    del _x0
    return _d

def reference(L0_attn_x, L0_attn_wq, L0_attn_wk, L0_attn_wv, L0_attn_wo, L0_attn_w1, L0_attn_w2, L0_attn_w3, L0_attn_ln1_g, L0_attn_ln1_b, L0_attn_ln2_g, L0_attn_ln2_b, L0_ffn_router_w, L0_ffn_w1, L0_ffn_w2, L1_attn_w_qkv, L1_attn_w_out, L1_attn_b_out, L1_ffn_We, L1_ffn_be, L1_ffn_Wg, L1_ffn_bg):

    def _L0_attn_ref(x, wq, wk, wv, wo, w1, w2, w3, ln1_g, ln1_b, ln2_g, ln2_b):
        import jax, jax.numpy as jnp
        import numpy as np
        DIM = 128
        N_HEADS = 16
        HEAD_DIM = DIM // N_HEADS
        HIDDEN = 352
        WINDOW_PER_SIDE = 128
        EPS = 1e-05
        THETA = 10000.0

        def rope_cos_sin(seqlen, head_dim):
            freqs = 1.0 / THETA ** (jnp.arange(0, head_dim, 2, dtype=jnp.float32) / head_dim)
            t = jnp.arange(seqlen, dtype=jnp.float32)
            ang = jnp.outer(t, freqs)
            return (jnp.cos(ang), jnp.sin(ang))

        def apply_rope(x, cos, sin):
            xr = x[..., 0::2]
            xi = x[..., 1::2]
            c = cos[None, :, None, :]
            s = sin[None, :, None, :]
            or_ = xr * c - xi * s
            oi_ = xr * s + xi * c
            return jnp.stack([or_, oi_], axis=-1).reshape(x.shape)

        def layernorm(x, g, b):
            mu = jnp.mean(x, axis=-1, keepdims=True)
            var = jnp.mean(jnp.square(x - mu), axis=-1, keepdims=True)
            return (x - mu) * jax.lax.rsqrt(var + EPS) * g + b

        def attention(x, wq, wk, wv, wo):
            b, s, _ = x.shape
            scale = HEAD_DIM ** (-0.5)
            q = (x @ wq).reshape(b, s, N_HEADS, HEAD_DIM)
            k = (x @ wk).reshape(b, s, N_HEADS, HEAD_DIM)
            v = (x @ wv).reshape(b, s, N_HEADS, HEAD_DIM)
            cos, sin = rope_cos_sin(s, HEAD_DIM)
            q = apply_rope(q, cos, sin)
            k = apply_rope(k, cos, sin)
            i = jnp.arange(s)[:, None]
            j = jnp.arange(s)[None, :]
            mask = (j <= i) & (i - j <= WINDOW_PER_SIDE)
            scores = jnp.einsum('bqhd,bkhd->bhqk', q, k) * scale
            scores = jnp.where(mask[None, None], scores, jnp.finfo(scores.dtype).min)
            probs = jax.nn.softmax(scores, axis=-1)
            out = jnp.einsum('bhqk,bkhd->bqhd', probs, v).reshape(b, s, -1)
            return out @ wo

        def ffn(x, w1, w2, w3):
            return jax.nn.silu(x @ w1) * (x @ w3) @ w2
        h = x + attention(layernorm(x, ln1_g, ln1_b), wq, wk, wv, wo)
        out = h + ffn(layernorm(h, ln2_g, ln2_b), w1, w2, w3)
        return out

    def _L0_ffn_ref(hidden_states, router_w, w1, w2):
        import jax, jax.numpy as jnp
        import numpy as np
        EPS = 1e-09
        TOP_K = 2
        orig_shape = hidden_states.shape
        H = orig_shape[-1]
        E = router_w.shape[-1]
        flat = hidden_states.reshape(-1, H)
        T = flat.shape[0]
        gate_logits = flat @ router_w
        gate_probs = jax.nn.softmax(gate_logits, axis=-1)
        topk_w, topk_idx = jax.lax.top_k(gate_probs, TOP_K)
        topk_w = topk_w / jnp.clip(topk_w.sum(-1, keepdims=True), EPS)
        cw = jnp.zeros((T, E), dtype=flat.dtype).at[jnp.arange(T)[:, None], topk_idx].add(topk_w)
        h = jax.nn.silu(jnp.einsum('td,edf->etf', flat, w1))
        y = jnp.einsum('etf,efd->etd', h, w2)
        out = jnp.einsum('etd,te->td', y, cw)
        return out.reshape(orig_shape)

    def _L1_attn_ref(x, w_qkv, w_out, b_out):
        import jax, jax.numpy as jnp
        import numpy as np
        HEADS = 16
        WINDOW = 128
        B, N, C = x.shape
        H, Dh = (HEADS, C // HEADS)
        scale = Dh ** (-0.5)
        qkv = (x @ w_qkv.T).reshape(B, N, 3, H, Dh)
        q = jnp.transpose(qkv[:, :, 0], (0, 2, 1, 3))
        k = jnp.transpose(qkv[:, :, 1], (0, 2, 1, 3))
        v = jnp.transpose(qkv[:, :, 2], (0, 2, 1, 3))
        scores = jnp.einsum('bhnd,bhmd->bhnm', q, k) * scale
        i = jnp.arange(N)[:, None]
        j = jnp.arange(N)[None, :]
        local_mask = (j <= i) & (jnp.abs(i - j) <= WINDOW)
        attn_local = jax.nn.softmax(jnp.where(local_mask[None, None], scores, -jnp.inf), axis=-1)
        out_local = jnp.einsum('bhnm,bhmd->bhnd', attn_local, v)
        stride = WINDOW
        k_g = k[:, :, ::stride]
        v_g = v[:, :, ::stride]
        scores_g = jnp.einsum('bhnd,bhmd->bhnm', q, k_g) * scale
        attn_g = jax.nn.softmax(scores_g, axis=-1)
        out_g = jnp.einsum('bhnm,bhmd->bhnd', attn_g, v_g)
        out = (out_local + out_g).transpose(0, 2, 1, 3).reshape(B, N, C)
        return out @ w_out.T + b_out

    def _L1_ffn_ref(x, We, be, Wg, bg):
        import jax, jax.numpy as jnp
        import numpy as np
        B, S, D = (4, 256, 128)
        O = 128
        E = 8
        K = 2
        b, s, d = x.shape
        x_flat = x.reshape(-1, d)
        gates = jax.nn.softmax(x_flat @ Wg + bg, axis=-1)
        topk_gates, topk_idx = jax.lax.top_k(gates, K)
        topk_gates = topk_gates / jnp.sum(topk_gates, axis=1, keepdims=True)
        expert_out = jnp.einsum('nd,edo->neo', x_flat, We) + be
        selected = jnp.take_along_axis(expert_out, topk_idx[:, :, None], axis=1)
        out = jnp.sum(selected * topk_gates[:, :, None], axis=1)
        return out.reshape(b, s, -1)
    x = L0_attn_x
    x = x + _L0_attn_ref(_layernorm(x, axis=-1), L0_attn_wq, L0_attn_wk, L0_attn_wv, L0_attn_wo, L0_attn_w1, L0_attn_w2, L0_attn_w3, L0_attn_ln1_g, L0_attn_ln1_b, L0_attn_ln2_g, L0_attn_ln2_b)
    x = x + _L0_ffn_ref(_layernorm(x, axis=-1), L0_ffn_router_w, L0_ffn_w1, L0_ffn_w2)
    x = x + _L1_attn_ref(_layernorm(x, axis=-1), L1_attn_w_qkv, L1_attn_w_out, L1_attn_b_out)
    x = x + _L1_ffn_ref(_layernorm(x, axis=-1), L1_ffn_We, L1_ffn_be, L1_ffn_Wg, L1_ffn_bg)
    return x

_drawn_inputs = setup_inputs


def setup_inputs(seed=0):
    import zlib

    import numpy as np

    out = dict(_drawn_inputs(seed))
    spreads = {'L0_attn_ln1_g': (1.0, 0.6),
     'L0_attn_ln1_b': (0.0, 0.8),
     'L0_attn_ln2_g': (1.0, 0.6),
     'L0_attn_ln2_b': (0.0, 0.8)}
    factors = {'L0_attn_wq': 8.0,
     'L0_attn_wk': 8.0,
     'L0_attn_wv': 4.17,
     'L0_attn_wo': 3.832,
     'L0_attn_w1': 4.137,
     'L0_attn_w2': 4.41,
     'L0_attn_w3': 4.366,
     'L0_ffn_router_w': 17.441,
     'L1_attn_b_out': 18.077,
     'L1_ffn_be': 3.281,
     'L0_ffn_w1': 5.828,
     'L0_ffn_w2': 5.885}
    for name, (base, spread) in spreads.items():
        noise = np.random.default_rng([zlib.crc32(name.encode()), seed]).standard_normal(out[name].shape)
        drawn = base * np.exp(spread * noise) if base else spread * noise
        out[name] = jnp.asarray(drawn.astype(out[name].dtype))
    for name, factor in factors.items():
        out[name] = (out[name] * factor).astype(out[name].dtype)
    return out
```

```python
from contextlib import ExitStack

import numpy as np

import concourse.bass as bass
from concourse import mybir

F32 = mybir.dt.float32
F16 = mybir.dt.float16
BF16 = mybir.dt.bfloat16
ALU = mybir.AluOpType
ACT = mybir.ActivationFunctionType
AX = mybir.AxisListType

P = 128
D = 128
SEQS, T = 8, 512
NJ = T // P
HEADS, HD = 16, 8
HG = 4
KB = 32
NB = T // KB
WINDOW = 128
PADB = WINDOW // KB
WIN = WINDOW + KB
HID = 352
HT = (128, 128, 96)
E = 8
FE = 256
STRIDE = 128
NG = T // STRIDE
EPS = 1e-5
SCALE = HD ** -0.5
MSCALE = 1024.0
PAIR = 3 * KB
ROWS = PAIR + 8
BIG = -1.0e30
PB = 3

MAX_FILLS = [list(range(w, min(w + PB, NJ * HEADS))) for w in range(0, NJ * HEADS, PB)]


def exp_fills():
    full = [(kb, hg) for kb in range(NB - 4) for hg in range(HG)]
    fills = [[(kb, hg, n * WIN, WIN) for n, (kb, hg) in enumerate(full[i:i + PB])]
             for i in range(0, len(full), PB)]
    for kbs in ((NB - 4,), (NB - 3,), (NB - 2, NB - 1)):
        at, tiles = 0, []
        for kb in kbs:
            n = T - KB * kb
            for hg in range(HG):
                tiles.append((kb, hg, at, n))
                at += n
        fills.append(tiles)
    return fills


EXP_FILLS = exp_fills()
NMF, NEF = len(MAX_FILLS), len(EXP_FILLS)


def at(s, per, k):
    return s * per + k


def pass_on(eng, passed):
    eng.sem_inc(passed, 1)


class Steps:

    def __init__(self, eng, sem, per):
        self.eng, self.sem, self.per, self.n, self.s = eng, sem, per, 0, 0

    def begin(self, s):
        self.s, self.n = s, 0

    def mark(self, ins):
        ins.then_inc(self.sem, 1)
        self.n += 1
        return self.n

    def wait(self, n=None):
        self.eng.wait_ge(self.sem, at(self.s, self.per, self.n if n is None else n))

    def link(self, ins):
        self.mark(ins)
        self.wait()

    def end(self):
        assert self.n == self.per, (self.sem, self.n)


DVE_A, DVE_B = 14, 58
POOL_A, POOL_B = 3, 11
ACT_B = 1


def model_kernel(nc, x, out, w, c, indicator):
    x_v = x.rearrange("(s j p) d -> s p j d", p=P, j=NJ)
    out_v = out.rearrange("(s j p) d -> s p j d", p=P, j=NJ)
    ctx = ExitStack()
    with ctx:
        def sb(name, shape, dt=F32):
            return ctx.enter_context(nc.sbuf_tensor(name, shape, dt))

        def sem(name):
            return ctx.enter_context(nc.semaphore(name))

        W = {n: sb(f"w_{n}", list(a.shape), a.dtype) for n, a in w.items()}
        C = {n: sb(f"c_{n}", list(a.shape), a.dtype) for n, a in c.items()}
        s_w = sem("weights_in")
        s_c = sem("constants_in")
        s_init = sem("buffers_cleared")
        n_w, n_c = 16 * len(w), 16 * len(c)

        class Thread:

            def __init__(self, t):
                self.t = t
                self.bank = [ctx.enter_context(nc.psum_tensor(f"{t}_bank{i}", [P, 512], F32)) for i in range(4)]
                self.st = sb(f"{t}_st", [P, NJ, 6])
                self.mv = sb(f"{t}_mv", [P, NJ, 2])
                self.ve = sb(f"{t}_ve", [P, 2, NJ])
                self.rs = sb(f"{t}_rs", [P, 2, NJ])
                self.nrm = sb(f"{t}_nrm", [P, NJ, D])
                self.ft = sb(f"{t}_ft", [D, T])
                self.q32 = sb(f"{t}_q32", [D, T])
                self.k32 = sb(f"{t}_k32", [D, T])
                self.ot, self.rden = self.q32, self.k32
                self.hl = sb(f"{t}_hl", [D, 4, T], F16)
                self.scr = nc.dram_tensor(f"{t}_scr", (4, D, T), F16, kind="Internal").ap()
                self.qr = sb(f"{t}_qr", [P, HG, T], F16)
                self.kr = self.hl
                self.kd = sb(f"{t}_kd", [P, HG, PADB + NB, 4, KB], F16)
                self.vb = sb(f"{t}_vb", [P, NB, HG, 4, HD])
                self.m = sb(f"{t}_m", [P, NJ * HEADS])
                self.mhl = sb(f"{t}_mhl", [P, NJ, HG, 2, 4], F16)
                self.mt = sb(f"{t}_mt", [HG * 8, T], F16)
                self.p = sb(f"{t}_p", [P, 3, 512])
                self.s_mv = sem(f"{t}_stats_ready")
                self.s_rs = sem(f"{t}_rstd_ready")
                self.s_nrm = sem(f"{t}_normed")
                self.s_tps = sem(f"{t}_transposed")
                self.s_ft = sem(f"{t}_features_ready")
                self.s_qk = sem(f"{t}_qk_projected")
                self.s_hl = sem(f"{t}_pairs_split")
                self.s_hi = sem(f"{t}_high_parts")
                self.s_vps = sem(f"{t}_v_projected")
                self.s_vb = sem(f"{t}_v_placed")
                self.s_scr = sem(f"{t}_pairs_out")
                self.s_rep = sem(f"{t}_pairs_spread")
                self.s_kd = sem(f"{t}_k_in_blocks")
                self.s_mfill = sem(f"{t}_max_scores")
                self.s_mdone = sem(f"{t}_max_taken")
                self.s_mhl = sem(f"{t}_max_split")
                self.s_mtp = sem(f"{t}_max_transposed")
                self.s_mt = sem(f"{t}_max_rows")
                self.s_shift = sem(f"{t}_max_placed")
                self.s_sfill = sem(f"{t}_scores")
                self.s_exp = sem(f"{t}_exp_done")
                self.s_pv = sem(f"{t}_pv_done")
                self.s_ot = sem(f"{t}_attended")
                self.s_ops = sem(f"{t}_attn_projected")
                self.s_h = sem(f"{t}_residual_added")
                self.s_dve = sem(f"{t}_dve_steps")
                self.s_pool = sem(f"{t}_pool_steps")

        A, B = Thread("a"), Thread("b")
        s_passed = {n: sem(f"{n}_passed") for n in ("pe", "dve", "pool")}

        xin = sb("xin", [P, NJ, D])
        xres = sb("xres", [P, NJ, D])
        a0 = sb("a0", [P, NJ, D])
        rope_t = sb("rope_t", [D, 4, T])
        h0 = sb("h0", [P, NJ, D])
        xh = sb("xh", [P, NJ, D])
        tanh_t, sg = rope_t[:, 0:2], rope_t[:, 2:4]
        gt = sb("gt", [P, 3, T])
        x1 = sb("x1", [P, NJ, D])
        s_xin = sem("x_in")
        s_xfree = sem("x_copied")
        s_rope = sem("rope_products")
        s_q32 = sem("rope_summed")
        s_hh = sem("h_plus_x")
        s_up = sem("ffn_up")
        s_th = sem("ffn_tanh")
        s_g = sem("ffn_gated")
        s_dn = sem("ffn_down")
        s_x1 = sem("x1_ready")

        acc = sb("acc", [P, NJ, D])
        lg = sb("lg", [P, 10, NJ, E])
        red = sb("red", [P, 8, NJ])
        cw = sb("cw", [P, NJ, E])
        mth = sb("mth", [P, 2, T])
        hs = sb("hs", [P, 2, 2, T])
        yc = sb("yc", [P, 2, NJ, D])
        gkd = sb("gkd", [D, HEADS, NG])
        gft = sb("gft", [D, HEADS * NG])
        gs = sb("gs", [P, NJ, HEADS, NG])
        gp = sb("gp", [P, NJ, HEADS, NG])
        gred = sb("gred", [P, 3, NJ, HEADS])
        gpt = sb("gpt", [HEADS * NG, T])
        gv = sb("gv", [HEADS * NG, D])
        ogt = sb("ogt", [D, T])
        x2b = sb("x2b", [P, NJ, D])
        x3 = sb("x3", [P, NJ, D])
        cwt = sb("cwt", [E, T])
        yce = hs
        fold = sb("fold", [P, 2, 4 * D])
        x3b = x2b
        fsum = acc
        xout = sb("xout", [P, NJ, D])
        s_lg = sem("logits")
        s_le = sem("gate_exp")
        s_ls = sem("gate_shifted")
        s_cw = sem("gates_ready")
        s_mup = sem("moe_up")
        s_mth = sem("moe_tanh")
        s_hs = sem("moe_hidden")
        s_y = sem("moe_down")
        s_yc = sem("moe_gated")
        s_acc = sem("moe_summed")
        s_k32 = sem("k_copied")
        s_gkd = sem("global_keys")
        s_gsh = sem("global_shifted")
        s_ge = sem("global_exp")
        s_gp = sem("global_probs")
        s_gpp = sem("global_probs_transposed")
        s_gpt = sem("global_probs_rows")
        s_gvp = sem("global_v_projected")
        s_gv = sem("global_v_placed")
        s_ogp = sem("global_out")
        s_ogt = sem("global_out_copied")
        s_x2b = sem("x2_plus_bias")
        s_cwp = sem("gates_transposed")
        s_cwt = sem("gates_rows")
        s_ye = sem("expert_out")
        s_yce = sem("expert_gated")
        s_fold = sem("expert_folded")
        s_bp = sem("expert_bias")
        s_x3b = sem("x3_plus_biases")
        s_ind = sem("indicator_rows_in")
        s_xo = sem("x_out_ready")
        s_out = sem("x_stored")

        block = ctx.enter_context(nc.Block())

        @block.sync
        def _(sp):
            def load(s):
                sp.wait_ge(s_xfree, at(s, 2, 2))
                sp.dma_start(xin[:], x_v[s]).then_inc(s_xin, 16)

            def spread(th, s):
                sp.wait_ge(th.s_hl, at(s, 2, 2))
                sp.dma_start(th.scr.rearrange("c p n -> p c n"), th.hl[:]).then_inc(th.s_scr, 16)
                sp.wait_ge(th.s_scr, at(s, 16, 16))
                sp.wait_ge(th.s_pv, at(s, NEF, NEF))
                rows = th.scr.rearrange("c (g r) n -> c r g n", g=HG)
                for part, of in ((0, 0), (1, 1), (2, 0)):
                    sp.dma_start(th.qr[KB * part:KB * (part + 1), :, :], rows[of]).then_inc(th.s_rep, 16)
                for part, of in ((0, 2), (1, 2), (2, 3)):
                    sp.dma_start(th.kr[KB * part:KB * (part + 1), :, :], rows[of]).then_inc(th.s_rep, 16)

            def shift(th, s):
                sp.wait_ge(th.s_mt, at(s, 1, 1))
                for g in range(HG):
                    sp.dma_start(th.qr[PAIR:ROWS, g, :], th.mt[8 * g:8 * g + 8, :]).then_inc(th.s_shift, 16)

            def store(s):
                sp.wait_ge(s_xo, at(s, 1, 1))
                sp.dma_start(out_v[s], xout[:]).then_inc(s_out, 16)

            for n, a in w.items():
                sp.dma_start(W[n][:], a).then_inc(s_w, 16)

            sp.wait_ge(s_init, 1)
            for th in (A, B):
                sp.dma_start(th.kd[PAIR:ROWS].rearrange("p g b h k -> p (g b h k)"), indicator).then_inc(s_ind, 16)

            def trip(sa, sb_):
                if sa is not None:
                    load(sa)
                    spread(A, sa)
                    shift(A, sa)
                if sb_ is not None:
                    spread(B, sb_)
                    shift(B, sb_)
                    store(sb_)
            trip(0, None)
            with sp.Fori(1, SEQS) as i:
                trip(i, i - 1)
            trip(None, SEQS - 1)
            sp.wait_ge(s_out, 16 * SEQS + 16)

        @block.tensor
        def _(pe):
            def transposes(th, s, k, per, bank, src):
                pe.wait_ge(th.s_nrm, at(s, per, k))
                for j in range(NJ):
                    mm = pe.transpose(bank[:, P * j:P * (j + 1)], src[:, j, :], C["ident"][:])
                mm.then_inc(th.s_tps, 1)

            def project(th, bank, wt, m=P):
                return pe.matmul(bank[0:m, :], wt, th.ft[:], start=True, stop=True)

            def v_blocks(th, s, bank, wv):
                for kb in range(NB):
                    for h in range(4):
                        mm = pe.matmul(bank[KB * h:KB * (h + 1), KB * kb:KB * (kb + 1)],
                                       th.ft[:, KB * kb:KB * (kb + 1)], wv[:, h, :],
                                       start=(kb == 0), stop=(kb == NB - 1), skip_group_check=True)
                mm.then_inc(th.s_vps, 1)

            def max_fill(th, s, f):
                bank = th.bank[f % 2]
                if f == 0:
                    pe.wait_ge(th.s_rep, at(s, 96, 96))
                    pe.wait_ge(th.s_kd, at(s, 1, 1))
                if f == 1:
                    pe.wait_ge(th.s_vb, at(s, 1, 1))
                if f >= 2:
                    pe.wait_ge(th.s_mdone, at(s, NMF, f - 1))
                ws = MAX_FILLS[f]
                runs = []
                for n, wd in enumerate(ws):
                    key = (wd // HEADS, wd % HEADS // 4)
                    if runs and runs[-1][0] == key:
                        runs[-1][3] += 1
                    else:
                        runs.append([key, n, wd % 4, 1])
                for r, ((J, hg), n0, h0_, n) in enumerate(runs):
                    for j in range(4):
                        qb = 4 * J + j
                        pe.matmul(bank[KB * j:KB * (j + 1), WIN * n0:WIN * (n0 + n)].rearrange("p (a b c) -> p a b c", a=n, c=KB),
                                  th.qr[0:PAIR, hg, KB * qb:KB * (qb + 1)],
                                  th.kd[0:PAIR, hg, qb:qb + WIN // KB, h0_:h0_ + n, :].rearrange("p b h k -> p h b k"),
                                  start=(r == 0), stop=False, skip_group_check=True)
                first = [wd for wd in ws if wd < HEADS]
                rest = len(ws) - len(first)
                if first:
                    n = len(first)
                    mm = pe.matmul(bank[:, 0:WIN * n].rearrange("p (a b) -> p a b", a=n), C["identb"][:],
                                   C["mask_first"][:, 0:n, :], start=False, stop=True, skip_group_check=True)
                if rest:
                    n = len(first)
                    o = bank[:, WIN * n:WIN * len(ws)].rearrange("p (a b c) -> p a b c", a=rest, c=KB)
                    mm = pe.matmul(o[:, :, 0:5:4, :], C["identb"][:], C["mask_q"][:, 0:rest, :, :],
                                   start=False, stop=True, skip_group_check=True)
                mm.then_inc(th.s_mfill, 1)

            def max_rows(th, s):
                pe.wait_ge(th.s_mhl, at(s, 1, 1))
                bank = th.bank[2][0:4 * 8, 0:T // 2].bitcast(F16)
                for j in range(NJ):
                    mm = pe.transpose(bank[:, P * j:P * (j + 1)],
                                      th.mhl[:, j].rearrange("p g r h -> p (g r h)"), C["identh"][:])
                mm.then_inc(th.s_mtp, 1)

            def exp_fill(th, s, f):
                bank = th.bank[f % 2]
                if f == 0:
                    pe.wait_ge(th.s_shift, at(s, 64, 64))
                    pe.wait_ge(th.s_vb, at(s, 1, 1))
                if f < 2:
                    pe.wait_ge(th.s_mdone, at(s, NMF, NMF - 1 + f))
                else:
                    pe.wait_ge(th.s_exp, at(s, NEF, f - 1))
                tiles = EXP_FILLS[f]
                for n, (kb, hg, col, q) in enumerate(tiles):
                    pe.matmul(bank[:, col:col + q], th.kd[0:ROWS, hg, PADB + kb].rearrange("p h k -> p (h k)"),
                              th.qr[0:ROWS, hg, KB * kb:KB * kb + q],
                              start=(n == 0), stop=False, skip_group_check=True)
                if f < NEF - 3:
                    o = bank[:, 0:WIN * PB].rearrange("p (a b c) -> p a b c", a=PB, c=KB)
                    mm = pe.matmul(o[:, :, 0:5:4, :], C["identb"][:], C["mask_q"][:],
                                   start=False, stop=True, skip_group_check=True)
                else:
                    for q in sorted({t[3] for t in tiles}):
                        mine = [t for t in tiles if t[3] == q]
                        o = bank[:, mine[0][2]:mine[0][2] + 4 * q].rearrange("p (a b) -> p a b", a=4)
                        mm = pe.matmul(o[:, :, 0:KB], C["identb"][:], C["mask_tail"][:],
                                       start=False, stop=True, skip_group_check=True)
                mm.then_inc(th.s_sfill, 1)

            def pv(th, s, f):
                pe.wait_ge(th.s_exp, at(s, NEF, f + 1))
                tiles = EXP_FILLS[f]
                for n, (kb, hg, col, q) in enumerate(tiles):
                    pe.matmul(th.bank[2][KB * hg:KB * (hg + 1), KB * kb:KB * kb + q],
                              th.vb[:, kb, hg].rearrange("p h d -> p (h d)"), th.p[:, f % 3, col:col + q],
                              start=(kb == 0), stop=(f == NEF - 1), skip_group_check=True)
                for n, (kb, hg, col, q) in enumerate(tiles):
                    mm = pe.matmul(th.bank[3][KB * hg:KB * (hg + 1), KB * kb:KB * kb + q],
                                   C["ones_bd"][:], th.p[:, f % 3, col:col + q],
                                   start=(kb == 0), stop=(f == NEF - 1), skip_group_check=True)
                mm.then_inc(th.s_pv, 1)

            def token_major(bank, lhs, rhs):
                for j in range(NJ):
                    mm = pe.matmul(bank[:, P * j:P * (j + 1)], lhs[:, P * j:P * (j + 1)], rhs, start=True, stop=True)
                return mm

            def a_project(s):
                bk = A.bank
                pe.wait_ge(s_x1, at(s, 1, 1))
                transposes(A, s, 1, 2, bk[0], A.nrm)
                pe.wait_ge(A.s_ft, at(s, 2, 1))
                project(A, bk[1], W["wq"][:]).then_inc(A.s_qk, 1)
                project(A, bk[2], W["wqs"][:]).then_inc(A.s_qk, 1)
                project(A, bk[3], W["wk"][:]).then_inc(A.s_qk, 1)
                project(A, bk[0], W["wks"][:]).then_inc(A.s_qk, 1)
                pe.wait_ge(s_rope, at(s, 4, 1))
                v_blocks(A, s, bk[1], W["wv"])

            def a_out(s):
                pe.wait_ge(A.s_ot, at(s, 1, 1))
                token_major(A.bank[0], A.ot, W["wo"][:]).then_inc(A.s_ops, 1)
                transposes(A, s, 2, 2, A.bank[1], A.nrm)

            def a_ffn(s):
                bk = A.bank
                pe.wait_ge(A.s_ft, at(s, 2, 2))
                at_ = 0
                for m, mt in enumerate(HT):
                    b1, b3 = (bk[2], bk[3]) if m % 2 == 0 else (bk[0], bk[1])
                    if m == 2:
                        pe.wait_ge(s_g, at(s, 3, 1))
                    project(A, b1, W["w1"][:, at_:at_ + mt], mt).then_inc(s_up, 1)
                    project(A, b3, W["w3"][:, at_:at_ + mt], mt).then_inc(s_up, 1)
                    at_ += mt
                pe.wait_ge(s_g, at(s, 3, 3))
                for j in range(NJ):
                    for m, mt in enumerate(HT):
                        mm = pe.matmul(bk[0][:, P * j:P * (j + 1)], gt[0:mt, m, P * j:P * (j + 1)],
                                       W["w2"][0:mt, m, :], start=(m == 0), stop=(m == 2))
                mm.then_inc(s_dn, 1)

            def b_route(s):
                pe.wait_ge(s_yce, at(s, 8, 8))
                transposes(B, s, 1, 3, B.bank[0], B.nrm)
                pe.wait_ge(B.s_ft, at(s, 3, 1))
                pe.wait_ge(s_x3b, at(s, 1, 1))
                for j in range(NJ):
                    mm = pe.matmul(B.bank[1][:, E * j:E * (j + 1)], B.ft[:, P * j:P * (j + 1)], W["router"][:],
                                   start=True, stop=True)
                mm.then_inc(s_lg, 1)

            def moe_up(s, e):
                for m in range(2):
                    if e >= 1:
                        pe.wait_ge(s_hs, at(s, 2 * E, 2 * (e - 1) + m + 1))
                    project(B, B.bank[2 + m], W["m1"][:, e, P * m:P * (m + 1)]).then_inc(s_mup, 1)

            def moe_down(s, e):
                bank = B.bank[e % 2]
                if e >= 2:
                    pe.wait_ge(s_yc, at(s, E, e - 1))
                elif e == 1:
                    pe.wait_ge(s_cw, at(s, 2, 1))
                pe.wait_ge(s_hs, at(s, 2 * E, 2 * e + 2))
                for j in range(NJ):
                    for m in range(2):
                        mm = pe.matmul(bank[:, P * j:P * (j + 1)], hs[:, e % 2, m, P * j:P * (j + 1)],
                                       W["m2"][:, e, m, :], start=(m == 0), stop=(m == 1))
                mm.then_inc(s_y, 1)

            def b_project(s):
                bk = B.bank
                pe.wait_ge(s_hs, at(s, 2 * E, 2 * E))
                transposes(B, s, 2, 3, bk[2], B.nrm)
                pe.wait_ge(B.s_ft, at(s, 3, 2))
                project(B, bk[3], W["bq"][:]).then_inc(B.s_qk, 1)
                project(B, bk[0], W["bk"][:]).then_inc(B.s_qk, 1)
                v_blocks(B, s, bk[1], W["bv"])
                pe.wait_ge(s_gkd, at(s, 1, 1))
                pe.wait_ge(B.s_hi, at(s, 2, 1))
                for j in range(NJ):
                    mm = pe.matmul(bk[2][:, 64 * j:64 * (j + 1)], B.q32[:, P * j:P * (j + 1)],
                                   gkd[:].rearrange("p h g -> p (h g)"), start=True, stop=True)
                pe.matmul(bk[2][0:64, 256:384], gft[:],
                          W["bvn"][:], start=True, stop=True).then_inc(s_gvp, 1)

            def b_global(s):
                bk = B.bank
                pe.wait_ge(s_gp, at(s, 1, 1))
                pe.wait_ge(B.s_hl, at(s, 2, 1))
                pass_on(pe, s_passed["pe"])
                for j in range(NJ):
                    mm = pe.transpose(bk[3][0:64, P * j:P * (j + 1)], gp[:, j].rearrange("p h g -> p (h g)"), C["ident"][:])
                mm.then_inc(s_gpp, 1)
                pe.wait_ge(s_gpt, at(s, 1, 1))
                pe.wait_ge(s_gv, at(s, 1, 1))
                pe.wait_ge(B.s_mt, at(s, 1, 1))
                pe.matmul(bk[2][:], gv[:], gpt[:], start=True, stop=True).then_inc(s_ogp, 1)

            def b_out(s):
                bk = B.bank
                pe.wait_ge(B.s_ot, at(s, 1, 1))
                token_major(bk[0], B.ot, W["bo"][:]).then_inc(B.s_ops, 1)
                transposes(B, s, 3, 3, bk[1], B.nrm)
                pe.wait_ge(B.s_ft, at(s, 3, 3))
                for j in range(NJ):
                    mm = pe.matmul(bk[2][:, E * j:E * (j + 1)], B.ft[:, P * j:P * (j + 1)], W["wg"][:],
                                   start=True, stop=True)
                mm.then_inc(s_lg, 1)

            def b_experts(s):
                bk = B.bank
                for j in range(NJ):
                    for half in range(2):
                        n = 2 * j + half
                        b = bk[(3, 0)[n % 2]]
                        if n >= 2:
                            pe.wait_ge(s_yce, at(s + 1, 8, n - 1))
                        elif n == 1:
                            pe.wait_ge(B.s_h, at(s, 1, 1))
                        pe.matmul(b[:], B.ft[:, P * j:P * (j + 1)], W["we"][:, 512 * half:512 * (half + 1)],
                                  start=True, stop=True).then_inc(s_ye, 1)
                pe.wait_ge(s_cw, at(s, 2, 2))
                for j in range(NJ):
                    mm = pe.transpose(bk[2][0:E, P * j:P * (j + 1)], cw[:, j, :], C["ident"][:])
                mm.then_inc(s_cwp, 1)
                pe.wait_ge(s_cwt, at(s, 1, 1))
                token_major(bk[1], cwt, W["be"][:]).then_inc(s_bp, 1)

            pe.sem_inc(A.s_pv, NEF)
            pe.sem_inc(B.s_pv, NEF)
            pe.wait_ge(s_w, n_w)
            pe.wait_ge(s_c, n_c)
            pe.wait_ge(s_ind, 32)

            def trip(sa, sb_):
                if sa is not None:
                    a_project(sa)
                if sb_ is not None:
                    b_route(sb_)
                    moe_up(sb_, 0)
                f = 0
                for e in range(E):
                    if sb_ is not None:
                        if e + 1 < E:
                            moe_up(sb_, e + 1)
                        moe_down(sb_, e)
                    if sa is not None and e >= 1:
                        last = NMF * e // (E - 1)
                        while f < last:
                            max_fill(A, sa, f)
                            f += 1
                if sa is not None:
                    max_rows(A, sa)
                if sb_ is not None:
                    b_project(sb_)
                if sa is not None:
                    for f in range(NEF):
                        exp_fill(A, sa, f)
                        if f >= 1:
                            pv(A, sa, f - 1)
                    pv(A, sa, NEF - 1)
                    a_out(sa)
                if sb_ is not None:
                    for f in range(NMF):
                        max_fill(B, sb_, f)
                    max_rows(B, sb_)
                    b_global(sb_)
                if sa is not None:
                    a_ffn(sa)
                if sb_ is not None:
                    for f in range(NEF):
                        exp_fill(B, sb_, f)
                        if f == 0:
                            pe.wait_ge(s_ogt, at(sb_, 1, 1))
                        if f >= 1:
                            pv(B, sb_, f - 1)
                    pv(B, sb_, NEF - 1)
                    b_out(sb_)
                    b_experts(sb_)
            trip(0, None)
            with pe.Fori(1, SEQS) as i:
                trip(i, i - 1)
            trip(None, SEQS - 1)

        @block.scalar
        def _(act):
            for n, a in c.items():
                act.dma_start(C[n][:], a).then_inc(s_c, 16)
            act.wait_ge(s_w, n_w)
            act.wait_ge(s_c, n_c)
            act.wait_ge(s_init, 1)

            def copy(o, i):
                return act.activation(o, i, ACT.Copy)

            def v_place(th, s, bank):
                act.wait_ge(th.s_vps, at(s, 1, 1))
                act.wait_ge(th.s_pv, at(s, NEF, NEF))
                for h in range(4):
                    r = slice(KB * h, KB * (h + 1))
                    ins = copy(th.vb[r, :, :, h, :], bank[r, :].rearrange("p (k g d) -> p k g d", k=NB, g=HG))
                ins.then_inc(th.s_vb, 1)

            def max_rows(th, s):
                act.wait_ge(th.s_mtp, at(s, 1, 1))
                copy(th.mt[:], th.bank[2][0:32, 0:T // 2].bitcast(F16)).then_inc(th.s_mt, 1)

            def exps(th, s, f):
                act.wait_ge(th.s_sfill, at(s, NEF, f + 1))
                if f >= 3:
                    act.wait_ge(th.s_pv, at(s + 1, NEF, f - 2))
                n = sum(t[3] for t in EXP_FILLS[f])
                act.activation(th.p[:, f % 3, 0:n], th.bank[f % 2][:, 0:n], ACT.Exp, scale=SCALE).then_inc(th.s_exp, 1)

            def a_features(s, k):
                act.wait_ge(A.s_tps, at(s, 2, k))
                act.activation(A.ft[:], A.bank[k - 1][:], ACT.Identity, scale=W["ln"][:, 2 * k - 2:2 * k - 1],
                               bias=W["ln"][:, 2 * k - 1:2 * k]).then_inc(A.s_ft, 1)

            def b_features(s, k, bank):
                act.wait_ge(B.s_tps, at(s, 3, k))
                if k == 2:
                    copy(gft[:].rearrange("p (h g) -> p h g", g=NG),
                         bank[:, 0:T:STRIDE].unsqueeze(1).broadcast_to([D, HEADS, NG]))
                copy(B.ft[:], bank[:]).then_inc(B.s_ft, 1)

            def a_split(s):
                for n, src in ((0, A.q32), (1, A.k32)):
                    act.wait_ge(s_q32, at(s, 2, n + 1))
                    copy(A.hl[:, 2 * n], src[:]).then_inc(A.s_hi, 1)

            def b_split(s):
                act.wait_ge(B.s_qk, at(s, 2, 2))
                copy(B.k32[:, 0:T:STRIDE], B.bank[0][:, 0:T:STRIDE]).then_inc(s_k32, 1)
                copy(B.q32[:], B.bank[3][:])
                copy(B.hl[:, 0], B.bank[3][:]).then_inc(B.s_hi, 1)
                copy(B.hl[:, 2], B.bank[0][:]).then_inc(B.s_hi, 1)

            def a_tanh(s, m):
                act.wait_ge(s_up, at(s, 6, 2 * m + 1))
                if m == 2:
                    act.wait_ge(s_g, at(s, 3, 1))
                act.activation(tanh_t[0:HT[m], m % 2], A.bank[2 if m % 2 == 0 else 0][0:HT[m], :], ACT.Tanh,
                               scale=0.5).then_inc(s_th, 1)

            def moe_tanh(s, e):
                for m in range(2):
                    act.wait_ge(s_mup, at(s, 2 * E, 2 * e + m + 1))
                    if e >= 1:
                        act.wait_ge(s_hs, at(s, 2 * E, 2 * e + m - 1))
                    act.activation(mth[:, m], B.bank[2 + m][:], ACT.Tanh, scale=0.5).then_inc(s_mth, 1)

            def gate_exp(s, k):
                act.wait_ge(s_ls, at(s, 2, k))
                act.activation(lg[:, 1], lg[:, 0], ACT.Exp).then_inc(s_le, 1)

            def trip(sa, sb_):
                if sa is not None:
                    a_features(sa, 1)
                if sb_ is not None:
                    b_features(sb_, 1, B.bank[0])
                    gate_exp(sb_, 1)
                if sa is not None:
                    a_split(sa)
                    v_place(A, sa, A.bank[1])
                if sb_ is not None:
                    for e in range(E):
                        moe_tanh(sb_, e)
                if sa is not None:
                    max_rows(A, sa)
                if sb_ is not None:
                    b_features(sb_, 2, B.bank[2])
                    b_split(sb_)
                    v_place(B, sb_, B.bank[1])
                    act.wait_ge(s_gsh, at(sb_, 1, 1))
                    act.activation(gp[:], gs[:], ACT.Exp, scale=SCALE).then_inc(s_ge, 1)
                if sa is not None:
                    for f in range(NEF):
                        exps(A, sa, f)
                    a_features(sa, 2)
                if sb_ is not None:
                    max_rows(B, sb_)
                    act.wait_ge(s_gpp, at(sb_, 1, 1))
                    copy(gpt[:], B.bank[3][0:64, :]).then_inc(s_gpt, 1)
                    act.wait_ge(s_ogp, at(sb_, 1, 1))
                    copy(ogt[:], B.bank[2][:]).then_inc(s_ogt, 1)
                if sa is not None:
                    for m in range(3):
                        a_tanh(sa, m)
                if sb_ is not None:
                    for f in range(NEF):
                        exps(B, sb_, f)
                    b_features(sb_, 3, B.bank[1])
                    gate_exp(sb_, 2)
                    act.wait_ge(s_cwp, at(sb_, 1, 1))
                    copy(cwt[:], B.bank[2][0:E, :]).then_inc(s_cwt, 1)
            trip(0, None)
            with act.Fori(1, SEQS) as i:
                trip(i, i - 1)
            trip(None, SEQS - 1)

        @block.vector
        def _(dve):
            dve.sem_inc(s_xfree, 1)
            dve.sem_inc(s_x1, 1)
            dve.sem_inc(s_yce, 8)
            dve.sem_inc(s_x3b, 1)
            dve.wait_ge(s_c, n_c)
            dve.wait_ge(s_w, n_w)
            da, db = Steps(dve, A.s_dve, DVE_A), Steps(dve, B.s_dve, DVE_B)

            def stats(th, d, src):
                for j in range(NJ):
                    d.mark(dve.bn_stats(th.st[:, j], src[:, j]))
                d.wait()
                pass_on(dve, s_passed["dve"])
                for j in range(NJ):
                    ins = dve.bn_aggr(th.mv[:, j], th.st[:, j])
                ins.then_inc(th.s_mv, 1)

            def norm(th, s, k, per, dst, src, r):
                for j in range(NJ):
                    ins = dve.tensor_scalar(dst[:, j], src[:, j], th.mv[:, j, 0:1], th.rs[:, r, j:j + 1],
                                            ALU.subtract, ALU.mult)
                return ins

            def maxima(th, s, f):
                dve.wait_ge(th.s_mfill, at(s, NMF, f + 1))
                n = len(MAX_FILLS[f])
                dve.tensor_reduce(th.m[:, PB * f:PB * f + n],
                                  th.bank[f % 2][:, 0:WIN * n].rearrange("p (a b) -> p a b", a=n),
                                  AX.X, ALU.max).then_inc(th.s_mdone, 1)

            def max_split(th, d, s):
                dve.wait_ge(th.s_mdone, at(s, NMF, NMF))
                m = th.m[:].rearrange("p (j g h) -> p j g h", j=NJ, g=HG)
                d.link(dve.tensor_scalar(th.mhl[:, :, :, 0, :], m, -1.0 / MSCALE, None, ALU.mult))
                dve.scalar_tensor_tensor(th.mhl[:, :, :, 1, :].rearrange("p j g h -> p (j g) h"),
                                         m.rearrange("p j g h -> p (j g) h"), -1.0 / MSCALE,
                                         th.mhl[:, :, :, 0, :].rearrange("p j g h -> p (j g) h"),
                                         ALU.mult, ALU.subtract).then_inc(th.s_mhl, 1)

            def divide(th, d, s):
                dve.wait_ge(th.s_pv, at(s + 1, NEF, NEF))
                d.link(dve.reciprocal(th.rden[:], th.bank[3][:]))
                return dve.tensor_tensor(th.ot[:], th.bank[2][:], th.rden[:], ALU.mult)

            def top2(d, s, k, bank, eps, factor):
                dve.wait_ge(s_lg, at(s, 2, k))
                l = bank[:, 0:NJ * E].rearrange("p (j e) -> p j e", j=NJ)
                sh = [P, NJ, E]
                rd = lambda n: red[:, n].unsqueeze(2).broadcast_to(sh)
                if k == 2:
                    d.link(dve.tensor_tensor(lg[:, 8], l, W["b_g"][:].unsqueeze(1).broadcast_to(sh), ALU.add))
                    l = lg[:, 8]
                d.link(dve.tensor_reduce(red[:, 0], l, AX.X, ALU.max))
                dve.tensor_tensor(lg[:, 0], l, rd(0), ALU.subtract).then_inc(s_ls, 1)
                dve.wait_ge(s_le, at(s, 2, k))
                d.link(dve.tensor_reduce(red[:, 1], lg[:, 1], AX.X, ALU.add))
                d.link(dve.reciprocal(red[:, 2], red[:, 1]))
                d.link(dve.tensor_tensor(lg[:, 2], lg[:, 1], rd(2), ALU.mult))
                order = C["order"][:].unsqueeze(1).broadcast_to(sh)
                d.link(dve.tensor_reduce(red[:, 3], lg[:, 2], AX.X, ALU.max))
                d.link(dve.tensor_tensor(lg[:, 3], lg[:, 2], rd(3), ALU.is_equal))
                d.link(dve.tensor_tensor(lg[:, 4], lg[:, 3], order, ALU.mult))
                d.link(dve.tensor_reduce(red[:, 4], lg[:, 4], AX.X, ALU.max))
                d.link(dve.tensor_tensor(lg[:, 5], order, rd(4), ALU.is_equal))
                d.link(dve.scalar_tensor_tensor(lg[:, 6], lg[:, 5], -4.0, lg[:, 2], ALU.mult, ALU.add))
                d.link(dve.tensor_reduce(red[:, 5], lg[:, 6], AX.X, ALU.max))
                d.link(dve.tensor_tensor(lg[:, 7], lg[:, 6], rd(5), ALU.is_equal))
                d.link(dve.tensor_tensor(lg[:, 3], lg[:, 7], order, ALU.mult))
                d.link(dve.tensor_reduce(red[:, 6], lg[:, 3], AX.X, ALU.max))
                d.link(dve.tensor_tensor(lg[:, 4], order, rd(6), ALU.is_equal))
                d.link(dve.tensor_tensor(lg[:, 6], lg[:, 4], lg[:, 5], ALU.add))
                d.link(dve.tensor_tensor(lg[:, 7], lg[:, 2], lg[:, 6], ALU.mult))
                d.link(dve.tensor_reduce(red[:, 7], lg[:, 7], AX.X, ALU.add))
                if eps:
                    d.link(dve.tensor_scalar(red[:, 7], red[:, 7], eps, None, ALU.max))
                d.link(dve.reciprocal(red[:, 0], red[:, 7]))
                dve.scalar_tensor_tensor(cw[:], lg[:, 7], factor, rd(0), ALU.mult, ALU.mult).then_inc(s_cw, 1)

            def a_norm(s):
                da.begin(s)
                dve.wait_ge(s_xin, at(s, 16, 16))
                stats(A, da, xin)
                dve.wait_ge(A.s_rs, at(s, 2, 1))
                norm(A, s, 1, 2, A.nrm, xin, 1).then_inc(A.s_nrm, 1)
                norm(A, s, 1, 2, a0, xin, 0).then_inc(s_xfree, 1)

            def a_rope(s):
                for n, (bank, tab) in enumerate(((1, "cos"), (2, "sin"), (3, "cos"), (0, "sin"))):
                    dve.wait_ge(A.s_qk, at(s, 4, n + 1))
                    dve.tensor_tensor(rope_t[:, n], A.bank[bank][:], C[tab][:], ALU.mult).then_inc(s_rope, 1)

            def a_resid(s):
                dve.wait_ge(A.s_ops, at(s, 1, 1))
                da.link(dve.tensor_tensor(h0[:].rearrange("p j d -> p (j d)"), A.bank[0][:],
                                          a0[:].rearrange("p j d -> p (j d)"), ALU.add))
                stats(A, da, h0)
                dve.wait_ge(A.s_rs, at(s, 2, 2))
                norm(A, s, 2, 2, A.nrm, h0, 0).then_inc(A.s_nrm, 1)

            def a_gate(s):
                for m, mt in enumerate(HT):
                    dve.wait_ge(s_th, at(s, 3, m + 1))
                    b1, b3 = (A.bank[2], A.bank[3]) if m % 2 == 0 else (A.bank[0], A.bank[1])
                    da.link(dve.scalar_tensor_tensor(sg[0:mt, m % 2], tanh_t[0:mt, m % 2], 1.0, b1[0:mt, :],
                                                     ALU.add, ALU.mult))
                    dve.wait_ge(s_up, at(s, 6, 2 * m + 2))
                    dve.scalar_tensor_tensor(gt[0:mt, m], sg[0:mt, m % 2], 0.5, b3[0:mt, :],
                                             ALU.mult, ALU.mult).then_inc(s_g, 1)
                dve.wait_ge(s_dn, at(s, 1, 1))
                dve.wait_ge(s_hh, at(s, 1, 1))
                dve.tensor_tensor(x1[:].rearrange("p j d -> p (j d)"), A.bank[0][:],
                                  xh[:].rearrange("p j d -> p (j d)"), ALU.add).then_inc(s_x1, 1)
                da.end()

            def b_norm(s, k, src, sem_, v):
                dve.wait_ge(sem_, v)
                stats(B, db, src)
                dve.wait_ge(B.s_rs, at(s, 3, k))
                norm(B, s, k, 3, B.nrm, src, 0).then_inc(B.s_nrm, 1)

            def moe_gate(s, e):
                if e == 0:
                    dve.wait_ge(s_fold, at(s, NJ, NJ))
                for m in range(2):
                    dve.wait_ge(s_mth, at(s, 2 * E, 2 * e + m + 1))
                    dve.scalar_tensor_tensor(hs[:, e % 2, m], mth[:, m], 1.0, B.bank[2 + m][:],
                                             ALU.add, ALU.mult).then_inc(s_hs, 1)

            def moe_scale(s, e):
                if e == 0:
                    dve.wait_ge(s_cw, at(s, 2, 1))
                dve.wait_ge(s_y, at(s, E, e + 1))
                if e >= 2:
                    dve.wait_ge(s_acc, at(s, E, e - 1))
                dve.tensor_tensor(yc[:, e % 2], B.bank[e % 2][:].rearrange("p (j d) -> p j d", j=NJ),
                                  cw[:, :, e:e + 1].broadcast_to([P, NJ, D]), ALU.mult).then_inc(s_yc, 1)

            def b_pairs(s):
                dve.wait_ge(s_k32, at(s, 1, 1))
                dve.tensor_tensor(gkd[:], B.k32[:, 0:T:STRIDE].unsqueeze(1).broadcast_to([D, HEADS, NG]),
                                  C["head_mask"][:].unsqueeze(2).broadcast_to([D, HEADS, NG]),
                                  ALU.mult).then_inc(s_gkd, 1)
                for n in range(2):
                    dve.wait_ge(B.s_hi, at(s, 2, n + 1))
                    dve.tensor_tensor(B.hl[:, 2 * n + 1], B.bank[(3, 0)[n]][:], B.hl[:, 2 * n],
                                      ALU.subtract).then_inc(B.s_hl, 1)

            def b_global(s):
                dve.wait_ge(s_gvp, at(s, 1, 1))
                sh = [P, NJ, HEADS, NG]
                g4 = B.bank[2][:, 0:256].rearrange("p (a g) -> p a g", g=NG)
                v3 = lambda t: t[:].rearrange("p j h g -> p (j h) g")
                rd = lambda n: gred[:, n].rearrange("p j h -> p (j h)")
                bc = lambda n: rd(n).unsqueeze(2).broadcast_to([P, NJ * HEADS, NG])
                db.link(dve.tensor_reduce(rd(0), g4, AX.X, ALU.max))
                dve.tensor_tensor(v3(gs), g4, bc(0), ALU.subtract).then_inc(s_gsh, 1)
                dve.tensor_tensor(gv[:], B.bank[2][0:64, 256:384], C["gv_mask"][:], ALU.mult).then_inc(s_gv, 1)
                dve.wait_ge(s_ge, at(s, 1, 1))
                db.link(dve.tensor_reduce(rd(1), v3(gp), AX.X, ALU.add))
                db.link(dve.reciprocal(rd(2), rd(1)))
                dve.tensor_tensor(v3(gp), v3(gp), bc(2), ALU.mult).then_inc(s_gp, 1)

            def b_resid(s):
                db.link(divide(B, db, s))
                dve.wait_ge(s_ogt, at(s, 1, 1))
                dve.tensor_tensor(B.ot[:], B.ot[:], ogt[:], ALU.add).then_inc(B.s_ot, 1)
                dve.wait_ge(B.s_ops, at(s, 1, 1))
                dve.wait_ge(s_x2b, at(s, 1, 1))
                dve.tensor_tensor(x3[:].rearrange("p j d -> p (j d)"), B.bank[0][:],
                                  x2b[:].rearrange("p j d -> p (j d)"), ALU.add).then_inc(B.s_h, 1)

            def b_scale(s):
                dve.wait_ge(s_cw, at(s, 2, 2))
                for n in range(8):
                    j, half = n // 2, n % 2
                    dve.wait_ge(s_ye, at(s, 8, n + 1))
                    if n >= 4:
                        dve.wait_ge(s_fold, at(s + 1, NJ, j - 1))
                    dve.tensor_tensor(yce[:, j % 2, half].rearrange("p (e d) -> p e d", e=4),
                                      B.bank[(3, 0)[n % 2]][:].rearrange("p (e d) -> p e d", e=4),
                                      cw[:, j, 4 * half:4 * half + 4].unsqueeze(2).broadcast_to([P, 4, D]),
                                      ALU.mult).then_inc(s_yce, 1)
                dve.wait_ge(s_bp, at(s, 1, 1))
                dve.tensor_tensor(x3b[:].rearrange("p j d -> p (j d)"), B.bank[1][:],
                                  x3[:].rearrange("p j d -> p (j d)"), ALU.add).then_inc(s_x3b, 1)

            def trip(sa, sb_):
                if sa is not None:
                    a_norm(sa)
                if sb_ is not None:
                    db.begin(sb_)
                    b_norm(sb_, 1, x1, s_x1, at(sb_ + 1, 1, 1))
                if sa is not None:
                    a_rope(sa)
                if sb_ is not None:
                    top2(db, sb_, 1, B.bank[1], 1e-9, 0.5)
                    moe_gate(sb_, 0)
                f = 0
                for e in range(E):
                    if sb_ is not None:
                        if e + 1 < E:
                            moe_gate(sb_, e + 1)
                        moe_scale(sb_, e)
                    if sa is not None and e >= 1:
                        last = NMF * e // (E - 1)
                        while f < last:
                            maxima(A, sa, f)
                            f += 1
                if sa is not None:
                    max_split(A, da, sa)
                if sb_ is not None:
                    b_norm(sb_, 2, acc, s_acc, at(sb_, E, E))
                    b_pairs(sb_)
                    b_global(sb_)
                if sa is not None:
                    divide(A, da, sa).then_inc(A.s_ot, 1)
                    a_resid(sa)
                if sb_ is not None:
                    for f in range(NMF):
                        maxima(B, sb_, f)
                    max_split(B, db, sb_)
                if sa is not None:
                    a_gate(sa)
                if sb_ is not None:
                    b_resid(sb_)
                    b_norm(sb_, 3, x3, B.s_h, at(sb_, 1, 1))
                    top2(db, sb_, 2, B.bank[2], None, 1.0)
                    b_scale(sb_)
                    db.end()
            trip(0, None)
            with dve.Fori(1, SEQS) as i:
                trip(i, i - 1)
            trip(None, SEQS - 1)

        @block.gpsimd
        def _(pool):
            pool.sem_inc(s_xfree, 1)
            pool.sem_inc(s_out, 16)
            pool.sem_inc(s_fold, NJ)
            pool.wait_ge(s_c, n_c)
            pa, pb = Steps(pool, A.s_pool, POOL_A), Steps(pool, B.s_pool, POOL_B)
            for th in (A, B):
                pool.memset(th.kd[:].rearrange("p g b h k -> p (g b h k)").bitcast(F32), 0.0)
                pool.memset(th.vb[:].rearrange("p k g h d -> p (k g h d)"), 0.0)
                ins = pool.memset(th.qr[:].rearrange("p g n -> p (g n)").bitcast(F32), 0.0)
            ins.then_inc(s_init, 1)

            def copy(o, i):
                return pool.tensor_scalar(o, i, 1.0, 1.0, ALU.mult, ALU.mult)

            def rstd(th, p, s, k, per, both):
                pool.wait_ge(th.s_mv, at(s, per, k))
                pass_on(pool, s_passed["pool"])
                n = 2 if both else 1
                var = th.mv[:, :, 1]
                if both:
                    p.mark(pool.tensor_scalar(th.ve[:, 1], var, 1.0 + EPS, EPS * EPS, ALU.mult, ALU.add))
                p.link(pool.tensor_scalar(th.ve[:, 0], var, EPS, 1.0, ALU.add, ALU.mult))
                pool.tensor_tensor(th.rs[:, 0:n], th.ve[:, 0:n], C["half"][:, 0:n], ALU.pow).then_inc(th.s_rs, 1)

            def k_blocks(th, s):
                pool.wait_ge(th.s_rep, at(s, 96, 96))
                pass_on(pool, s_passed["pool"])
                for g in range(HG):
                    for h in range(4):
                        ins = pool.tensor_scalar(th.kd[0:PAIR, g, PADB:, h, :],
                                                 th.kr[0:PAIR, g, :].rearrange("p (b k) -> p b k", k=KB),
                                                 C["own_head"][0:PAIR, h:h + 1], 1.0, ALU.mult, ALU.mult)
                ins.then_inc(th.s_kd, 1)

            def a_sum(s):
                for n, dst in ((0, A.q32), (1, A.k32)):
                    pool.wait_ge(s_rope, at(s, 4, 2 * n + 2))
                    pool.tensor_tensor(dst[:], rope_t[:, 2 * n], rope_t[:, 2 * n + 1], ALU.add).then_inc(s_q32, 1)
                for n, src in ((0, A.q32), (1, A.k32)):
                    pool.wait_ge(A.s_hi, at(s, 2, n + 1))
                    pool.tensor_tensor(A.hl[:, 2 * n + 1], src[:], A.hl[:, 2 * n], ALU.subtract).then_inc(A.s_hl, 1)

            def moe_sum(s, e):
                pool.wait_ge(s_yc, at(s, E, e + 1))
                if e >= 1:
                    pool.wait_ge(s_acc, at(s, E, e))
                pool.tensor_tensor(acc[:], yc[:, e % 2], (x1 if e == 0 else acc)[:], ALU.add).then_inc(s_acc, 1)

            def fold_experts(s):
                for j in range(NJ):
                    pool.wait_ge(s_yce, at(s + 1, 8, 2 * j + 2))
                    f = fold[:, 0]
                    pb.link(pool.tensor_tensor(f, yce[:, j % 2, 0], yce[:, j % 2, 1], ALU.add))
                    pb.link(pool.tensor_tensor(fold[:, 1, 0:2 * D], f[:, 0:2 * D], f[:, 2 * D:4 * D], ALU.add))
                    pool.tensor_tensor(fsum[:, j], fold[:, 1, 0:D], fold[:, 1, D:2 * D], ALU.add).then_inc(s_fold, 1)

            def trip(sa, sb_):
                if sa is not None:
                    pa.begin(sa)
                    rstd(A, pa, sa, 1, 2, True)
                    copy(xres[:].rearrange("p j d -> p (j d)"), xin[:].rearrange("p j d -> p (j d)")).then_inc(s_xfree, 1)
                if sb_ is not None:
                    pb.begin(sb_)
                    rstd(B, pb, sb_, 1, 3, False)
                if sa is not None:
                    a_sum(sa)
                    k_blocks(A, sa)
                if sb_ is not None:
                    for e in range(E):
                        moe_sum(sb_, e)
                    rstd(B, pb, sb_, 2, 3, False)
                    pool.tensor_tensor(x2b[:], acc[:], W["b_out"][:].unsqueeze(1).broadcast_to([P, NJ, D]),
                                       ALU.add).then_inc(s_x2b, 1)
                    k_blocks(B, sb_)
                if sa is not None:
                    rstd(A, pa, sa, 2, 2, False)
                    pool.tensor_tensor(xh[:], xres[:], h0[:], ALU.add).then_inc(s_hh, 1)
                    pa.end()
                if sb_ is not None:
                    rstd(B, pb, sb_, 3, 3, False)
                    fold_experts(sb_)
                    pool.wait_ge(s_fold, at(sb_ + 1, NJ, NJ))
                    pool.wait_ge(s_x3b, at(sb_ + 1, 1, 1))
                    pool.wait_ge(s_out, at(sb_, 16, 16))
                    pool.tensor_tensor(xout[:], fsum[:], x3b[:], ALU.add).then_inc(s_xo, 1)
                    pb.end()
            trip(0, None)
            with pool.Fori(1, SEQS) as i:
                trip(i, i - 1)
            trip(None, SEQS - 1)


def _constants():

    f32, f16, bf16 = np.float32, np.float16, np.dtype("bfloat16")
    p = np.arange(P)
    q, j = p % KB, p // KB
    w = np.arange(WIN)
    own = np.where((w[None] >= q[:, None]) & (w[None] <= q[:, None] + WINDOW), 0.0, BIG)
    first = np.where(KB * (j[:, None] - 4) + w[None] >= 0, own, BIG)
    edges = own.reshape(P, 5, KB)[:, [0, 4]]
    freqs = (1.0 / np.power(f32(10000.0), np.arange(0, HD, 2, dtype=f32) / f32(HD))).astype(f32)
    ang = np.outer(freqs, np.arange(T, dtype=f32)).astype(f32)
    d, d_head = p % HD, p // HD % 4
    sign = np.where(d % 2 == 0, -1.0, 1.0)[:, None]
    g = np.arange(HEADS * NG) // NG
    ind = np.zeros((8, HG * (PADB + NB), 4, KB), f16)
    for r in range(8):
        ind[r, :, r % 4] = MSCALE
    ind = ind.reshape(8, -1)
    rep = lambda a, n: np.repeat(a[:, None], n, 1)
    c = {
        "ident": np.eye(P, dtype=f32),
        "identb": np.eye(P).astype(bf16),
        "identh": np.eye(P, dtype=f16),
        "mask_first": rep(first, PB).astype(bf16),
        "mask_q": rep(edges, PB).astype(bf16),
        "mask_tail": rep(edges[:, 0], 4).astype(bf16),
        "ones_bd": (j[:, None] == (p[None, :KB] // HD)).astype(f32),
        "cos": np.cos(ang[d // 2].astype(np.float64)).astype(f32),
        "sin": (np.sin(ang[d // 2].astype(np.float64)) * sign).astype(f32),
        "head_mask": (p[:, None] // HD == np.arange(HEADS)[None]).astype(f32),
        "gv_mask": (g[:, None] == p[None] // HD).astype(f32),
        "half": np.full((P, 2, NJ), -0.5, f32),
        "own_head": (d_head[:, None] == np.arange(4)[None]).astype(f32),
        "order": np.broadcast_to(E - np.arange(E, dtype=f32), (P, E)),
    }
    return {k: np.ascontiguousarray(v) for k, v in c.items()}, ind


def kernel(**inputs):
    import concourse.bacc as bacc
    from concourse.bass_utils import run_bass_kernel_spmd

    i = {k: np.asarray(v) for k, v in inputs.items()}
    swap = np.arange(D) ^ 1
    heads = lambda m: m.reshape(D, HG, 4, HD).transpose(0, 2, 1, 3).reshape(D, 4, KB)
    w2 = np.zeros((3 * P, D), i["L0_attn_w2"].dtype)
    w2[:HID] = i["L0_attn_w2"]
    qkv = i["L1_attn_w_qkv"].T
    w = {
        "wq": i["L0_attn_wq"], "wqs": i["L0_attn_wq"][:, swap],
        "wk": i["L0_attn_wk"], "wks": i["L0_attn_wk"][:, swap],
        "wv": heads(i["L0_attn_wv"]), "wo": i["L0_attn_wo"],
        "ln": np.stack([i["L0_attn_ln1_g"], i["L0_attn_ln1_b"], i["L0_attn_ln2_g"], i["L0_attn_ln2_b"]], 1),
        "w1": i["L0_attn_w1"], "w3": i["L0_attn_w3"], "w2": w2.reshape(3, P, D).transpose(1, 0, 2),
        "router": i["L0_ffn_router_w"],
        "m1": i["L0_ffn_w1"].transpose(1, 0, 2),
        "m2": i["L0_ffn_w2"].reshape(E, 2, P, D).transpose(2, 0, 1, 3),
        "bq": qkv[:, :D], "bk": qkv[:, D:2 * D], "bvn": qkv[:, 2 * D:], "bv": heads(qkv[:, 2 * D:]),
        "bo": i["L1_attn_w_out"].T, "b_out": np.broadcast_to(i["L1_attn_b_out"], (P, D)),
        "wg": i["L1_ffn_Wg"], "b_g": np.broadcast_to(i["L1_ffn_bg"], (P, E)),
        "we": i["L1_ffn_We"].transpose(1, 0, 2).reshape(D, E * D), "be": i["L1_ffn_be"],
    }
    w = {k: np.ascontiguousarray(v) for k, v in w.items()}
    c, ind = _constants()
    x = np.ascontiguousarray(i["L0_attn_x"]).reshape(SEQS * T, D)
    nc = bacc.Bacc("TRN2", target_bir_lowering=False, num_devices=1)
    arrays = {}

    def dram(name, a):
        arrays[name] = a
        return nc.dram_tensor(name, a.shape, mybir.dt.from_np(a.dtype), kind="ExternalInput").ap()

    w_in = {k: dram(f"w_in_{k}", v) for k, v in w.items()}
    c_in = {k: dram(f"c_in_{k}", v) for k, v in c.items()}
    x_in, ind_in = dram("x_dram", x), dram("ind_dram", ind)
    out = nc.dram_tensor("out_dram", x.shape, F32, kind="ExternalOutput").ap()
    model_kernel(nc, x_in, out, w_in, c_in, ind_in)
    r = run_bass_kernel_spmd(nc, [arrays], core_ids=[0])
    return r.results[0]["out_dram"].reshape(SEQS, T, D)
```

```python
from contextlib import ExitStack

import numpy as np

import concourse.bass as bass
from concourse import mybir

F32 = mybir.dt.float32
F16 = mybir.dt.float16
BF16 = mybir.dt.bfloat16
ALU = mybir.AluOpType
ACT = mybir.ActivationFunctionType
AX = mybir.AxisListType

P = 128
D = 128
SEQS, T = 8, 512
NJ = T // P
HEADS, HD = 16, 8
HG = 4
KB = 32
NB = T // KB
WINDOW = 128
PADB = WINDOW // KB
WIN = WINDOW + KB
HID = 352
HT = (128, 128, 96)
E = 8
FE = 256
STRIDE = 128
NG = T // STRIDE
EPS = 1e-5
SCALE = HD ** -0.5
MSCALE = 1024.0
PAIR = 3 * KB
ROWS = PAIR + 8
BIG = -1.0e30
PB = 3

MAX_FILLS = [list(range(w, min(w + PB, NJ * HEADS))) for w in range(0, NJ * HEADS, PB)]


def exp_fills():
    full = [(kb, hg) for kb in range(NB - 4) for hg in range(HG)]
    fills = [[(kb, hg, n * WIN, WIN) for n, (kb, hg) in enumerate(full[i:i + PB])]
             for i in range(0, len(full), PB)]
    for kbs in ((NB - 4,), (NB - 3,), (NB - 2, NB - 1)):
        at, tiles = 0, []
        for kb in kbs:
            n = T - KB * kb
            for hg in range(HG):
                tiles.append((kb, hg, at, n))
                at += n
        fills.append(tiles)
    return fills


EXP_FILLS = exp_fills()
NMF, NEF = len(MAX_FILLS), len(EXP_FILLS)


def at(s, per, k):
    return s * per + k


def pass_on(eng, passed):
    eng.sem_inc(passed, 1)


TAIL = 13
EXP_TAIL = 11
EXP_LEAD = 3
EXP_E = 4
MAX_LEAD = 3
MAX_E = 16


def exp_in_tail(n):
    return EXP_TAIL * (n + 1) // TAIL


def exp_until(e):
    first = EXP_TAIL + EXP_LEAD
    return min(NEF + 1, first + -(-(NEF + 1 - first) * (e + 1) // EXP_E))


def max_until(f):
    return min(NMF, MAX_LEAD + (NMF - MAX_LEAD) * (f + 1) // MAX_E)


class Steps:

    def __init__(self, eng, sem, per):
        self.eng, self.sem, self.per, self.n, self.s = eng, sem, per, 0, 0

    def begin(self, s):
        self.s, self.n = s, 0

    def mark(self, ins):
        ins.then_inc(self.sem, 1)
        self.n += 1
        return self.n

    def wait(self, n=None):
        self.eng.wait_ge(self.sem, at(self.s, self.per, self.n if n is None else n))

    def link(self, ins):
        self.mark(ins)
        self.wait()

    def end(self):
        assert self.n == self.per, (self.sem, self.n)


FRONT_W = ("ln", "wq", "wqs", "wk", "wks", "wv")
REST_W = ("wo", "w1", "w3", "w2", "router", "m1", "m2", "bq", "bk", "bv", "bo", "b_out", "wg", "b_g", "we", "be")

DVE_F, DVE_A, DVE_B = 5, 12, 60
POOL_F, POOL_A, POOL_B = 2, 1, 11
ACT_B = 1


def model_kernel(nc, x, out, w, c, indicator):
    x_v = x.rearrange("(s j p) d -> s p j d", p=P, j=NJ)
    out_v = out.rearrange("(s j p) d -> s p j d", p=P, j=NJ)
    ctx = ExitStack()
    with ctx:
        def sb(name, shape, dt=F32):
            return ctx.enter_context(nc.sbuf_tensor(name, shape, dt))

        def sem(name):
            return ctx.enter_context(nc.semaphore(name))

        W = {n: sb(f"w_{n}", list(a.shape), a.dtype) for n, a in w.items()}
        C = {n: sb(f"c_{n}", list(a.shape), a.dtype) for n, a in c.items()}
        s_w = sem("weights_in")
        s_c = sem("constants_in")
        s_init = sem("buffers_cleared")
        s_vclear = sem("v_blocks_cleared")
        s_w2 = sem("later_weights_in")
        n_w, n_w2, n_c = 16 * len(FRONT_W), 16 * len(REST_W), 16 * len(c)

        class Thread:

            def __init__(self, t):
                self.t = t
                self.bank = [ctx.enter_context(nc.psum_tensor(f"{t}_bank{i}", [P, 512], F32)) for i in range(4)]
                self.st = sb(f"{t}_st", [P, NJ, 6])
                self.mv = sb(f"{t}_mv", [P, NJ, 2])
                self.ve = sb(f"{t}_ve", [P, 2, NJ])
                self.rs = sb(f"{t}_rs", [P, 2, NJ])
                self.nrm = sb(f"{t}_nrm", [P, NJ, D])
                self.ft = sb(f"{t}_ft", [D, T])
                self.q32 = sb(f"{t}_q32", [D, T])
                self.k32 = sb(f"{t}_k32", [D, T if t == "a" else NG])
                self.ot = self.q32
                self.hl = sb(f"{t}_hl", [D, 4, T], F16)
                self.scr = nc.dram_tensor(f"{t}_scr", (4, D, T), F16, kind="Internal").ap()
                self.qr = sb(f"{t}_qr", [P, HG, T], F16)
                self.kr = self.hl
                self.kd = sb(f"{t}_kd", [P, HG, PADB + NB, 4, KB], F16)
                self.vb = sb(f"{t}_vb", [P, NB, HG, 2, 4, HD])
                self.m = sb(f"{t}_m", [P, NJ * HEADS])
                self.mhl = sb(f"{t}_mhl", [P, NJ, HG, 2, 4], F16)
                self.mt = sb(f"{t}_mt", [HG * 8, T], F16)
                self.p = sb(f"{t}_p", [P, 4, 512])
                self.nd, self.ob = self.p[:, 0:2], self.p[:, 2].rearrange("p (j g h d) -> p j g h d", j=NJ, g=HG, h=4)
                self.rd = sb(f"{t}_rd", [P, 2, NJ, 2, 4])
                self.s_mv = sem(f"{t}_stats_ready")
                self.s_rs = sem(f"{t}_rstd_ready")
                self.s_nrm = sem(f"{t}_normed")
                self.s_tps = sem(f"{t}_transposed")
                self.s_ft = sem(f"{t}_features_ready")
                self.s_qk = sem(f"{t}_qk_projected")
                self.s_hl = sem(f"{t}_pairs_split")
                self.s_hi = sem(f"{t}_high_parts")
                self.s_vps = sem(f"{t}_v_projected")
                self.s_vb = sem(f"{t}_v_placed")
                self.s_scr = sem(f"{t}_pairs_out")
                self.s_rep = sem(f"{t}_pairs_spread")
                self.s_kd = sem(f"{t}_k_in_blocks")
                self.s_mfill = sem(f"{t}_max_scores")
                self.s_mdone = sem(f"{t}_max_taken")
                self.s_mhl = sem(f"{t}_max_split")
                self.s_mtp = sem(f"{t}_max_transposed")
                self.s_mt = sem(f"{t}_max_rows")
                self.s_shift = sem(f"{t}_max_placed")
                self.s_sfill = sem(f"{t}_scores")
                self.s_exp = sem(f"{t}_exp_done")
                self.s_pv = sem(f"{t}_pv_done")
                self.s_nd = sem(f"{t}_sums_copied")
                self.s_ndt = sem(f"{t}_sums_transposed")
                self.s_ob = sem(f"{t}_divided")
                self.s_obt = sem(f"{t}_quotient_transposed")
                self.s_ot = sem(f"{t}_attended")
                self.s_ops = sem(f"{t}_attn_projected")
                self.s_h = sem(f"{t}_residual_added")
                self.s_dve = sem(f"{t}_dve_steps")
                self.s_pool = sem(f"{t}_pool_steps")

        A, B = Thread("a"), Thread("b")
        s_passed = {n: sem(f"{n}_passed") for n in ("pe", "dve", "pool")}

        xin = sb("xin", [P, NJ, D])
        xres = sb("xres", [P, NJ, D])
        a0 = sb("a0", [P, NJ, D])
        rope_t = A.p
        h0 = sb("h0", [P, NJ, D])
        xh = sb("xh", [P, NJ, D])
        tanh_t, sg = rope_t[:, 0:2], rope_t[:, 2:4]
        gt = sb("gt", [P, 3, T])
        x1 = sb("x1", [P, NJ, D])
        s_xin = sem("x_in")
        s_poolf = sem("front_pool_steps")
        s_dvef = sem("front_dve_steps")
        s_xfree = sem("x_copied")
        s_rope = sem("rope_products")
        s_q32 = sem("rope_summed")
        s_hh = sem("h_plus_x")
        s_up = sem("ffn_up")
        s_th = sem("ffn_tanh")
        s_g = sem("ffn_gated")
        s_dn = sem("ffn_down")
        s_x1 = sem("x1_ready")

        acc = sb("acc", [P, NJ, D])
        lg = sb("lg", [P, 10, NJ, E])
        red = sb("red", [P, 8, NJ])
        cw = sb("cw", [P, NJ, E])
        mth = sb("mth", [P, 2, T])
        hs = B.p[:].rearrange("p (a b) n -> p a b n", a=2)
        yc = sb("yc", [P, 2, NJ, D])
        gkd = sb("gkd", [D, HEADS, NG])
        gft = sb("gft", [D, HEADS * NG])
        gs = sb("gs", [P, NJ, HEADS, NG])
        gp = sb("gp", [P, NJ, HEADS, NG])
        gred = sb("gred", [P, 3, NJ, HEADS])
        gpt = sb("gpt", [HEADS * NG, T])
        gv = sb("gv", [HEADS * NG, D])
        ogt = sb("ogt", [D, T])
        x2b = sb("x2b", [P, NJ, D])
        x3 = sb("x3", [P, NJ, D])
        cwt = gpt[0:E, :]
        yce = hs
        fold = yc[:].rearrange("p a j d -> p a (j d)")
        x3b = x2b
        fsum = acc
        xout = sb("xout", [P, NJ, D])
        s_lg = sem("logits")
        s_le = sem("gate_exp")
        s_ls = sem("gate_shifted")
        s_cw = sem("gates_ready")
        s_mup = sem("moe_up")
        s_mth = sem("moe_tanh")
        s_hs = sem("moe_hidden")
        s_y = sem("moe_down")
        s_yc = sem("moe_gated")
        s_acc = sem("moe_summed")
        s_k32 = sem("k_copied")
        s_gkd = sem("global_keys")
        s_gsh = sem("global_shifted")
        s_ge = sem("global_exp")
        s_gp = sem("global_probs")
        s_gpp = sem("global_probs_transposed")
        s_gpt = sem("global_probs_rows")
        s_gvp = sem("global_v_projected")
        s_gv = sem("global_v_placed")
        s_ogp = sem("global_out")
        s_ogt = sem("global_out_copied")
        s_x2b = sem("x2_plus_bias")
        s_cwp = sem("gates_transposed")
        s_cwt = sem("gates_rows")
        s_ye = sem("expert_out")
        s_yce = sem("expert_gated")
        s_fold = sem("expert_folded")
        s_bp = sem("expert_bias")
        s_x3b = sem("x3_plus_biases")
        s_ind = sem("indicator_rows_in")
        s_xo = sem("x_out_ready")
        s_out = sem("x_stored")

        block = ctx.enter_context(nc.Block())

        @block.sync
        def _(sp):
            def load(s):
                sp.wait_ge(s_xfree, at(s, 2, 2))
                sp.dma_start(xin[:], x_v[s]).then_inc(s_xin, 16)

            def spread(th, s):
                sp.wait_ge(th.s_hl, at(s, 2, 2))
                sp.dma_start(th.scr.rearrange("c p n -> p c n"), th.hl[:]).then_inc(th.s_scr, 16)
                sp.wait_ge(th.s_scr, at(s, 16, 16))
                sp.wait_ge(th.s_pv, at(s, NEF, NEF))
                rows = th.scr.rearrange("c (g r) n -> c r g n", g=HG)
                for part, of in ((0, 0), (1, 1), (2, 0)):
                    sp.dma_start(th.qr[KB * part:KB * (part + 1), :, :], rows[of]).then_inc(th.s_rep, 16)
                for part, of in ((0, 2), (1, 2), (2, 3)):
                    sp.dma_start(th.kr[KB * part:KB * (part + 1), :, :], rows[of]).then_inc(th.s_rep, 16)

            def store(s):
                sp.wait_ge(s_xo, at(s, 1, 1))
                sp.dma_start(out_v[s], xout[:]).then_inc(s_out, 16)

            load(0)
            for n in FRONT_W:
                sp.dma_start(W[n][:], w[n]).then_inc(s_w, 16)
            sp.wait_ge(s_init, 2)
            for th in (A, B):
                sp.dma_start(th.kd[PAIR:ROWS].rearrange("p g b h k -> p (g b h k)"), indicator).then_inc(s_ind, 16)
            for n in REST_W:
                sp.dma_start(W[n][:], w[n]).then_inc(s_w2, 16)

            def trip(sr, sb_, sf):
                if sf is not None and sr is not None:
                    load(sf)
                if sb_ is not None:
                    spread(B, sb_)
                if sf is not None:
                    spread(A, sf)
                if sb_ is not None:
                    store(sb_)
            trip(None, None, 0)
            trip(0, None, 1)
            with sp.Fori(1, SEQS - 1) as i:
                trip(i, i - 1, i + 1)
            trip(SEQS - 1, SEQS - 2, None)
            trip(None, SEQS - 1, None)
            sp.wait_ge(s_out, 16 * SEQS + 16)

        @block.tensor
        def _(pe):
            def transposes(th, s, k, per, bank, src):
                pe.wait_ge(th.s_nrm, at(s, per, k))
                for j in range(NJ):
                    mm = pe.transpose(bank[:, P * j:P * (j + 1)], src[:, j, :], C["ident"][:])
                mm.then_inc(th.s_tps, 1)

            def project(th, bank, wt, m=P):
                return pe.matmul(bank[0:m, :], wt, th.ft[:], start=True, stop=True)

            def v_rows(th, bank, wv):
                token_major(bank, th.ft, wv[:]).then_inc(th.s_vps, 1)

            def max_fill(th, s, f):
                bank = th.bank[f % 2]
                if f == 0:
                    pe.wait_ge(th.s_rep, at(s, 96, 96))
                    pe.wait_ge(th.s_kd, at(s, 1, 1))
                if f == 1:
                    pe.wait_ge(th.s_vb, at(s, 1, 1))
                if f >= 2:
                    pe.wait_ge(th.s_mdone, at(s, NMF, f - 1))
                ws = MAX_FILLS[f]
                runs = []
                for n, wd in enumerate(ws):
                    key = (wd // HEADS, wd % HEADS // 4)
                    if runs and runs[-1][0] == key:
                        runs[-1][3] += 1
                    else:
                        runs.append([key, n, wd % 4, 1])
                for r, ((J, hg), n0, h0_, n) in enumerate(runs):
                    for j in range(4):
                        qb = 4 * J + j
                        pe.matmul(bank[KB * j:KB * (j + 1), WIN * n0:WIN * (n0 + n)].rearrange("p (a b c) -> p a b c", a=n, c=KB),
                                  th.qr[0:PAIR, hg, KB * qb:KB * (qb + 1)],
                                  th.kd[0:PAIR, hg, qb:qb + WIN // KB, h0_:h0_ + n, :].rearrange("p b h k -> p h b k"),
                                  start=(r == 0), stop=False, skip_group_check=True)
                first = [wd for wd in ws if wd < HEADS]
                rest = len(ws) - len(first)
                if first:
                    n = len(first)
                    mm = pe.matmul(bank[:, 0:WIN * n].rearrange("p (a b) -> p a b", a=n), C["identb"][:],
                                   C["mask_first"][:, 0:n, :], start=False, stop=True, skip_group_check=True)
                if rest:
                    n = len(first)
                    o = bank[:, WIN * n:WIN * len(ws)].rearrange("p (a b c) -> p a b c", a=rest, c=KB)
                    mm = pe.matmul(o[:, :, 0:5:4, :], C["identb"][:], C["mask_q"][:, 0:rest, :, :],
                                   start=False, stop=True, skip_group_check=True)
                mm.then_inc(th.s_mfill, 1)

            def max_rows(th, s):
                pe.wait_ge(th.s_mhl, at(s, 1, 1))
                bank = th.bank[2][0:4 * 8, 0:T // 2].bitcast(F16)
                for j in range(NJ):
                    mm = pe.transpose(bank[:, P * j:P * (j + 1)],
                                      th.mhl[:, j].rearrange("p g r h -> p (g r h)"), C["identh"][:])
                mm.then_inc(th.s_mtp, 1)

            def exp_fill(th, s, f):
                bank = th.bank[f % 2]
                if f == 0:
                    pe.wait_ge(th.s_shift, at(s, 64, 64))
                    pe.wait_ge(th.s_vb, at(s, 1, 1))
                if f < 2:
                    pe.wait_ge(th.s_mdone, at(s, NMF, NMF - 1 + f))
                else:
                    pe.wait_ge(th.s_exp, at(s, NEF, f - 1))
                tiles = EXP_FILLS[f]
                for n, (kb, hg, col, q) in enumerate(tiles):
                    pe.matmul(bank[:, col:col + q], th.kd[0:ROWS, hg, PADB + kb].rearrange("p h k -> p (h k)"),
                              th.qr[0:ROWS, hg, KB * kb:KB * kb + q],
                              start=(n == 0), stop=False, skip_group_check=True)
                if f < NEF - 3:
                    o = bank[:, 0:WIN * PB].rearrange("p (a b c) -> p a b c", a=PB, c=KB)
                    mm = pe.matmul(o[:, :, 0:5:4, :], C["identb"][:], C["mask_q"][:],
                                   start=False, stop=True, skip_group_check=True)
                else:
                    for q in sorted({t[3] for t in tiles}):
                        mine = [t for t in tiles if t[3] == q]
                        o = bank[:, mine[0][2]:mine[0][2] + 4 * q].rearrange("p (a b) -> p a b", a=4)
                        mm = pe.matmul(o[:, :, 0:KB], C["identb"][:], C["mask_tail"][:],
                                       start=False, stop=True, skip_group_check=True)
                mm.then_inc(th.s_sfill, 1)

            def pv(th, s, f):
                pe.wait_ge(th.s_exp, at(s, NEF, f + 1))
                for kb, hg, col, q in EXP_FILLS[f]:
                    half = 64 * (hg % 2)
                    mm = pe.matmul(th.bank[2 + hg // 2][half:half + 64, KB * kb:KB * kb + q],
                                   th.vb[:, kb, hg].rearrange("p a h d -> p (a h d)"), th.p[:, f % 3, col:col + q],
                                   start=(kb == 0), stop=(f == NEF - 1), skip_group_check=True)
                mm.then_inc(th.s_pv, 1)

            def quotient(th, s):
                pe.wait_ge(th.s_nd, at(s, 1, 1))
                for half in range(2):
                    for j in range(NJ):
                        mm = pe.transpose(th.bank[half][:, P * j:P * (j + 1)], th.nd[:, half, P * j:P * (j + 1)],
                                          C["ident"][:])
                mm.then_inc(th.s_ndt, 1)

            def quotient_back(th, s):
                pe.wait_ge(th.s_ob, at(s, 1, 1))
                for j in range(NJ):
                    mm = pe.transpose(th.bank[2][:, P * j:P * (j + 1)],
                                      th.ob[:, j].rearrange("p g h d -> p (g h d)"), C["ident"][:])
                mm.then_inc(th.s_obt, 1)

            def token_major(bank, lhs, rhs):
                for j in range(NJ):
                    mm = pe.matmul(bank[:, P * j:P * (j + 1)], lhs[:, P * j:P * (j + 1)], rhs, start=True, stop=True)
                return mm

            def a_front_turn(s, last):
                if last is not None:
                    pe.wait_ge(s_g, at(last, 3, 2))
                transposes(A, s, 1, 2, A.bank[1], A.nrm)

            def a_project(s, last):
                bk = A.bank
                pe.wait_ge(A.s_ft, at(s, 2, 1))
                if last is not None:
                    pe.wait_ge(s_g, at(last, 3, 3))
                project(A, bk[2], W["wq"][:]).then_inc(A.s_qk, 1)
                project(A, bk[3], W["wqs"][:]).then_inc(A.s_qk, 1)
                project(A, bk[1], W["wk"][:]).then_inc(A.s_qk, 1)
                pe.wait_ge(s_x1, at(s, 1, 1))
                project(A, bk[0], W["wks"][:]).then_inc(A.s_qk, 1)

            def a_v(s):
                pe.wait_ge(s_rope, at(s, 4, 1))
                v_rows(A, A.bank[2], W["wv"])

            def a_out(s):
                pe.wait_ge(A.s_ot, at(s, 1, 1))
                token_major(A.bank[0], A.ot, W["wo"][:]).then_inc(A.s_ops, 1)

            def a_turn(s):
                transposes(A, s, 2, 2, A.bank[1], A.nrm)

            def a_up(s):
                bk = A.bank
                pe.wait_ge(A.s_ft, at(s, 2, 2))
                at_ = 0
                for m, mt in enumerate(HT):
                    b1, b3 = (bk[2], bk[3]) if m % 2 == 0 else (bk[0], bk[1])
                    if m == 2:
                        pe.wait_ge(s_g, at(s, 3, 1))
                    project(A, b1, W["w1"][:, at_:at_ + mt], mt).then_inc(s_up, 1)
                    project(A, b3, W["w3"][:, at_:at_ + mt], mt).then_inc(s_up, 1)
                    at_ += mt

            def a_down(s):
                bk = A.bank
                pe.wait_ge(s_g, at(s, 3, 3))
                for j in range(NJ):
                    for m, mt in enumerate(HT):
                        mm = pe.matmul(bk[0][:, P * j:P * (j + 1)], gt[0:mt, m, P * j:P * (j + 1)],
                                       W["w2"][0:mt, m, :], start=(m == 0), stop=(m == 2))
                mm.then_inc(s_dn, 1)

            def b_route(s):
                pe.wait_ge(s_yce, at(s, 8, 8))
                transposes(B, s, 1, 3, B.bank[0], B.nrm)
                pe.wait_ge(B.s_ft, at(s, 3, 1))
                pe.wait_ge(s_x3b, at(s, 1, 1))
                for j in range(NJ):
                    mm = pe.matmul(B.bank[1][:, E * j:E * (j + 1)], B.ft[:, P * j:P * (j + 1)], W["router"][:],
                                   start=True, stop=True)
                mm.then_inc(s_lg, 1)

            def moe_up(s, e):
                for m in range(2):
                    if e >= 1:
                        pe.wait_ge(s_hs, at(s, 2 * E, 2 * (e - 1) + m + 1))
                    project(B, B.bank[2 + m], W["m1"][:, e, P * m:P * (m + 1)]).then_inc(s_mup, 1)

            def moe_down(s, e):
                bank = B.bank[e % 2]
                if e >= 2:
                    pe.wait_ge(s_yc, at(s, E, e - 1))
                elif e == 1:
                    pe.wait_ge(s_cw, at(s, 2, 1))
                pe.wait_ge(s_hs, at(s, 2 * E, 2 * e + 2))
                for j in range(NJ):
                    for m in range(2):
                        mm = pe.matmul(bank[:, P * j:P * (j + 1)], hs[:, e % 2, m, P * j:P * (j + 1)],
                                       W["m2"][:, e, m, :], start=(m == 0), stop=(m == 1))
                mm.then_inc(s_y, 1)

            def b_mid_turn(s):
                bk = B.bank
                pe.wait_ge(s_hs, at(s, 2 * E, 2 * E))
                transposes(B, s, 2, 3, bk[2], B.nrm)

            def b_qkv(s):
                bk = B.bank
                pe.wait_ge(B.s_ft, at(s, 3, 2))
                project(B, bk[3], W["bq"][:]).then_inc(B.s_qk, 1)
                project(B, bk[0], W["bk"][:]).then_inc(B.s_qk, 1)
                v_rows(B, bk[1], W["bv"])

            def b_global_scores(s):
                bk = B.bank
                pe.wait_ge(s_gkd, at(s, 1, 1))
                pe.wait_ge(B.s_hi, at(s, 2, 1))
                for j in range(NJ):
                    mm = pe.matmul(bk[2][:, 64 * j:64 * (j + 1)], B.q32[:, P * j:P * (j + 1)],
                                   gkd[:].rearrange("p h g -> p (h g)"), start=True, stop=True)
                pe.matmul(bk[2][0:64, 256:384], gft[:],
                          W["bv"][:], start=True, stop=True).then_inc(s_gvp, 1)

            def b_global(s):
                bk = B.bank
                pe.wait_ge(s_gp, at(s, 1, 1))
                pe.wait_ge(B.s_hl, at(s, 2, 1))
                pass_on(pe, s_passed["pe"])
                for j in range(NJ):
                    mm = pe.transpose(bk[3][0:64, P * j:P * (j + 1)], gp[:, j].rearrange("p h g -> p (h g)"), C["ident"][:])
                mm.then_inc(s_gpp, 1)

            def b_global_out(s):
                bk = B.bank
                pe.wait_ge(s_gpt, at(s, 1, 1))
                pe.wait_ge(s_gv, at(s, 1, 1))
                pe.matmul(bk[3][:], gv[:], gpt[:], start=True, stop=True).then_inc(s_ogp, 1)

            def b_out(s):
                pe.wait_ge(B.s_ot, at(s, 1, 1))
                token_major(B.bank[0], B.ot, W["bo"][:]).then_inc(B.s_ops, 1)

            def b_turn(s):
                bk = B.bank
                transposes(B, s, 3, 3, bk[1], B.nrm)
                pe.wait_ge(B.s_ft, at(s, 3, 3))
                for j in range(NJ):
                    mm = pe.matmul(bk[2][:, E * j:E * (j + 1)], B.ft[:, P * j:P * (j + 1)], W["wg"][:],
                                   start=True, stop=True)
                mm.then_inc(s_lg, 1)

            def b_expert(s, n):
                j, half = n // 2, n % 2
                if n >= 2:
                    pe.wait_ge(s_yce, at(s + 1, 8, n - 1))
                elif n == 1:
                    pe.wait_ge(B.s_h, at(s, 1, 1))
                pe.matmul(B.bank[(3, 0)[n % 2]][:], B.ft[:, P * j:P * (j + 1)], W["we"][:, 512 * half:512 * (half + 1)],
                          start=True, stop=True).then_inc(s_ye, 1)

            def b_gates_turn(s):
                bk = B.bank
                pe.wait_ge(s_cw, at(s, 2, 2))
                for j in range(NJ):
                    mm = pe.transpose(bk[2][0:E, P * j:P * (j + 1)], cw[:, j, :], C["ident"][:])
                mm.then_inc(s_cwp, 1)

            def b_biases(s):
                bk = B.bank
                pe.wait_ge(s_cwt, at(s, 1, 1))
                token_major(bk[1], cwt, W["be"][:]).then_inc(s_bp, 1)

            pe.sem_inc(A.s_pv, NEF)
            pe.sem_inc(B.s_pv, NEF)
            pe.wait_ge(s_w, n_w)
            pe.wait_ge(s_c, n_c)
            pe.wait_ge(s_ind, 32)

            def exp_step(th, s, f):
                if f < NEF:
                    exp_fill(th, s, f)
                if f >= 1:
                    pv(th, s, f - 1)

            def trip(sr, sb_, sf):
                f = EXP_TAIL
                if sr is not None:
                    while f < EXP_TAIL + EXP_LEAD:
                        exp_step(A, sr, f)
                        f += 1
                if sb_ is not None:
                    b_route(sb_)
                    moe_up(sb_, 0)
                for e in range(E):
                    if sb_ is not None:
                        if e + 1 < E:
                            moe_up(sb_, e + 1)
                        moe_down(sb_, e)
                    if sr is not None:
                        while f < exp_until(e):
                            exp_step(A, sr, f)
                            f += 1
                        if e == 4:
                            quotient(A, sr)
                        elif e == 5:
                            quotient_back(A, sr)
                        elif e == 6:
                            a_out(sr)
                        elif e == 7:
                            a_turn(sr)
                if sr is not None:
                    a_up(sr)
                if sb_ is not None:
                    b_mid_turn(sb_)
                if sf is not None:
                    a_front_turn(sf, sr)
                if sb_ is not None:
                    b_qkv(sb_)
                if sr is not None:
                    a_down(sr)
                if sf is not None:
                    a_project(sf, sr)
                if sb_ is not None:
                    b_global_scores(sb_)
                if sf is not None:
                    a_v(sf)
                if sb_ is not None:
                    for f in range(NMF):
                        max_fill(B, sb_, f)
                        if f == 4:
                            b_global(sb_)
                        elif f == 8:
                            b_global_out(sb_)
                    max_rows(B, sb_)
                m = 0
                while sf is not None and m < MAX_LEAD:
                    max_fill(A, sf, m)
                    m += 1
                for f in range(NEF + 1):
                    if sf is not None and f == NEF:
                        max_rows(A, sf)
                    if sb_ is not None:
                        exp_step(B, sb_, f)
                    while sf is not None and m < max_until(f):
                        max_fill(A, sf, m)
                        m += 1
                f = 0
                for n in range(TAIL):
                    if sb_ is not None:
                        if n == 0:
                            quotient(B, sb_)
                        elif n == 1:
                            quotient_back(B, sb_)
                        elif n == 2:
                            b_out(sb_)
                        elif n == 4:
                            b_turn(sb_)
                        if n >= 5:
                            b_expert(sb_, n - 5)
                        if n == TAIL - 2:
                            b_gates_turn(sb_)
                        elif n == TAIL - 1:
                            b_biases(sb_)
                    while sf is not None and f < exp_in_tail(n):
                        exp_step(A, sf, f)
                        f += 1
            trip(None, None, 0)
            pe.wait_ge(s_w2, n_w2)
            trip(0, None, 1)
            with pe.Fori(1, SEQS - 1) as i:
                trip(i, i - 1, i + 1)
            trip(SEQS - 1, SEQS - 2, None)
            trip(None, SEQS - 1, None)

        @block.scalar
        def _(act):
            for n, a in c.items():
                act.dma_start(C[n][:], a).then_inc(s_c, 16)
            act.wait_ge(s_w, n_w)
            act.wait_ge(s_init, 2)

            def copy(o, i):
                return act.activation(o, i, ACT.Copy)

            def v_place(th, s, bank):
                act.wait_ge(th.s_vps, at(s, 1, 1))
                act.wait_ge(th.s_pv, at(s, NEF, NEF))
                for b in range(4):
                    src = bank[KB * b:KB * (b + 1), :].rearrange("p (j g h d) -> p j g h d", j=NJ, g=HG, h=4)
                    for h in range(4):
                        ins = copy(th.vb[KB * h:KB * (h + 1), b:NB:4, :, 0, h, :], src[:, :, :, h, :])
                ins.then_inc(th.s_vb, 1)

            def max_rows(th, s):
                act.wait_ge(th.s_mtp, at(s, 1, 1))
                copy(th.mt[:], th.bank[2][0:32, 0:T // 2].bitcast(F16)).then_inc(th.s_mt, 1)
                act.wait_ge(th.s_mt, at(s, 1, 1))
                for g in range(HG):
                    act.dma_start(th.qr[PAIR:ROWS, g, :], th.mt[8 * g:8 * g + 8, :]).then_inc(th.s_shift, 16)

            def exps(th, s, f):
                act.wait_ge(th.s_sfill, at(s, NEF, f + 1))
                if f >= 3:
                    act.wait_ge(th.s_pv, at(s + 1, NEF, f - 2))
                n = sum(t[3] for t in EXP_FILLS[f])
                act.activation(th.p[:, f % 3, 0:n], th.bank[f % 2][:, 0:n], ACT.Exp, scale=SCALE).then_inc(th.s_exp, 1)

            def sums(th, s):
                act.wait_ge(th.s_pv, at(s + 1, NEF, NEF))
                copy(th.nd[:, 0], th.bank[2][:])
                copy(th.nd[:, 1], th.bank[3][:]).then_inc(th.s_nd, 1)

            def a_attended(s):
                act.wait_ge(A.s_obt, at(s, 1, 1))
                copy(A.ot[:], A.bank[2][:]).then_inc(A.s_ot, 1)

            def a_features(s, k, bank):
                act.wait_ge(A.s_tps, at(s, 2, k))
                act.activation(A.ft[:], bank[:], ACT.Identity, scale=W["ln"][:, 2 * k - 2:2 * k - 1],
                               bias=W["ln"][:, 2 * k - 1:2 * k]).then_inc(A.s_ft, 1)

            def b_features(s, k, bank):
                act.wait_ge(B.s_tps, at(s, 3, k))
                if k == 2:
                    copy(gft[:].rearrange("p (h g) -> p h g", g=NG),
                         bank[:, 0:T:STRIDE].unsqueeze(1).broadcast_to([D, HEADS, NG]))
                copy(B.ft[:], bank[:]).then_inc(B.s_ft, 1)

            def a_split(s):
                for n, src in ((0, A.q32), (1, A.k32)):
                    act.wait_ge(s_q32, at(s, 2, n + 1))
                    copy(A.hl[:, 2 * n], src[:]).then_inc(A.s_hi, 1)

            def b_split(s):
                act.wait_ge(B.s_qk, at(s, 2, 2))
                copy(B.k32[:], B.bank[0][:, 0:T:STRIDE]).then_inc(s_k32, 1)
                copy(B.q32[:], B.bank[3][:])
                copy(B.hl[:, 0], B.bank[3][:]).then_inc(B.s_hi, 1)
                copy(B.hl[:, 2], B.bank[0][:]).then_inc(B.s_hi, 1)

            def a_tanh(s, m):
                act.wait_ge(s_up, at(s, 6, 2 * m + 1))
                if m == 2:
                    act.wait_ge(s_g, at(s, 3, 1))
                act.activation(tanh_t[0:HT[m], m % 2], A.bank[2 if m % 2 == 0 else 0][0:HT[m], :], ACT.Tanh,
                               scale=0.5).then_inc(s_th, 1)

            def moe_tanh(s, e):
                for m in range(2):
                    act.wait_ge(s_mup, at(s, 2 * E, 2 * e + m + 1))
                    if e >= 1:
                        act.wait_ge(s_hs, at(s, 2 * E, 2 * e + m - 1))
                    act.activation(mth[:, m], B.bank[2 + m][:], ACT.Tanh, scale=0.5).then_inc(s_mth, 1)

            def gate_exp(s, k):
                act.wait_ge(s_ls, at(s, 2, k))
                act.activation(lg[:, 1], lg[:, 0], ACT.Exp).then_inc(s_le, 1)

            def trip(sr, sb_, sf):
                f = EXP_TAIL
                if sr is not None:
                    while f < EXP_TAIL + EXP_LEAD:
                        exps(A, sr, f)
                        f += 1
                if sb_ is not None:
                    b_features(sb_, 1, B.bank[0])
                    moe_tanh(sb_, 0)
                    gate_exp(sb_, 1)
                for e in range(E):
                    if sb_ is not None and e + 1 < E:
                        moe_tanh(sb_, e + 1)
                    if sr is not None:
                        while f < min(NEF, exp_until(e)):
                            exps(A, sr, f)
                            f += 1
                        if e == 3:
                            sums(A, sr)
                        elif e == 5:
                            a_attended(sr)
                        elif e == 7:
                            a_features(sr, 2, A.bank[1])
                if sr is not None:
                    for m in range(3):
                        a_tanh(sr, m)
                if sb_ is not None:
                    b_features(sb_, 2, B.bank[2])
                if sf is not None:
                    a_features(sf, 1, A.bank[1])
                if sb_ is not None:
                    b_split(sb_)
                    v_place(B, sb_, B.bank[1])
                    act.wait_ge(s_gsh, at(sb_, 1, 1))
                    act.activation(gp[:], gs[:], ACT.Exp, scale=SCALE).then_inc(s_ge, 1)
                if sf is not None:
                    a_split(sf)
                    v_place(A, sf, A.bank[2])
                if sb_ is not None:
                    act.wait_ge(s_gpp, at(sb_, 1, 1))
                    copy(gpt[:], B.bank[3][0:64, :]).then_inc(s_gpt, 1)
                    act.wait_ge(s_ogp, at(sb_, 1, 1))
                    copy(ogt[:], B.bank[3][:]).then_inc(s_ogt, 1)
                    max_rows(B, sb_)
                    for f in range(NEF):
                        exps(B, sb_, f)
                if sf is not None:
                    max_rows(A, sf)
                f = 0
                for n in range(TAIL):
                    if sb_ is not None:
                        if n == 0:
                            sums(B, sb_)
                        elif n == 4:
                            b_features(sb_, 3, B.bank[1])
                        elif n == 5:
                            gate_exp(sb_, 2)
                        elif n == TAIL - 1:
                            act.wait_ge(s_cwp, at(sb_, 1, 1))
                            copy(cwt, B.bank[2][0:E, :]).then_inc(s_cwt, 1)
                    while sf is not None and f < exp_in_tail(n):
                        exps(A, sf, f)
                        f += 1
            trip(None, None, 0)
            act.wait_ge(s_c, n_c)
            trip(0, None, 1)
            with act.Fori(1, SEQS - 1) as i:
                trip(i, i - 1, i + 1)
            trip(SEQS - 1, SEQS - 2, None)
            trip(None, SEQS - 1, None)

        @block.vector
        def _(dve):
            dve.sem_inc(s_xfree, 1)
            dve.sem_inc(s_x1, 1)
            dve.sem_inc(s_yce, 8)
            dve.sem_inc(s_x3b, 1)
            for th in (A, B):
                ins = dve.memset(th.kd[0:PAIR, :, 0:PADB].rearrange("p g b h k -> p g (b h k)").bitcast(F32), 0.0)
            ins.then_inc(s_init, 1)
            dve.wait_ge(s_c, n_c)
            da, db = Steps(dve, A.s_dve, DVE_A), Steps(dve, B.s_dve, DVE_B)
            df = Steps(dve, s_dvef, DVE_F)

            def stats(th, d, src):
                for j in range(NJ):
                    d.mark(dve.bn_stats(th.st[:, j], src[:, j]))
                d.wait()
                pass_on(dve, s_passed["dve"])
                for j in range(NJ):
                    ins = dve.bn_aggr(th.mv[:, j], th.st[:, j])
                ins.then_inc(th.s_mv, 1)

            def norm(th, s, k, per, dst, src, r):
                for j in range(NJ):
                    ins = dve.tensor_scalar(dst[:, j], src[:, j], th.mv[:, j, 0:1], th.rs[:, r, j:j + 1],
                                            ALU.subtract, ALU.mult)
                return ins

            def maxima(th, s, f):
                dve.wait_ge(th.s_mfill, at(s, NMF, f + 1))
                n = len(MAX_FILLS[f])
                dve.tensor_reduce(th.m[:, PB * f:PB * f + n],
                                  th.bank[f % 2][:, 0:WIN * n].rearrange("p (a b) -> p a b", a=n),
                                  AX.X, ALU.max).then_inc(th.s_mdone, 1)

            def max_split(th, d, s):
                dve.wait_ge(th.s_mdone, at(s, NMF, NMF))
                m = th.m[:].rearrange("p (j g h) -> p j g h", j=NJ, g=HG)
                d.link(dve.tensor_scalar(th.mhl[:, :, :, 0, :], m, -1.0 / MSCALE, None, ALU.mult))
                dve.scalar_tensor_tensor(th.mhl[:, :, :, 1, :].rearrange("p j g h -> p (j g) h"),
                                         m.rearrange("p j g h -> p (j g) h"), -1.0 / MSCALE,
                                         th.mhl[:, :, :, 0, :].rearrange("p j g h -> p (j g) h"),
                                         ALU.mult, ALU.subtract).then_inc(th.s_mhl, 1)

            def divide(th, d, s):
                dve.wait_ge(th.s_ndt, at(s, 1, 1))
                for half in range(2):
                    den = th.bank[half][:].rearrange("p (j g a h d) -> p j g a h d", j=NJ, g=2, a=2, h=4)
                    for g in range(2):
                        d.mark(dve.reciprocal(th.rd[:, half, :, g, :], den[:, :, g, 1, :, 0]))
                d.wait()
                for half in range(2):
                    num = th.bank[half][:].rearrange("p (j g a h d) -> p j g a h d", j=NJ, g=2, a=2, h=4)
                    for g in range(2):
                        ins = dve.tensor_tensor(th.ob[:, :, 2 * half + g], num[:, :, g, 0],
                                                th.rd[:, half, :, g, :].unsqueeze(3).broadcast_to([P, NJ, 4, HD]), ALU.mult)
                ins.then_inc(th.s_ob, 1)

            def k_blocks(th, s):
                dve.wait_ge(th.s_rep, at(s, 96, 96))
                pass_on(dve, s_passed["dve"])
                for g in range(HG):
                    for h in range(4):
                        ins = dve.tensor_scalar(th.kd[0:PAIR, g, PADB:, h, :],
                                                th.kr[0:PAIR, g, :].rearrange("p (b k) -> p b k", k=KB),
                                                C["own_head"][0:PAIR, h:h + 1], None, ALU.mult)
                ins.then_inc(th.s_kd, 1)

            def top2(d, s, k, bank, eps, factor):
                dve.wait_ge(s_lg, at(s, 2, k))
                l = bank[:, 0:NJ * E].rearrange("p (j e) -> p j e", j=NJ)
                sh = [P, NJ, E]
                rd = lambda n: red[:, n].unsqueeze(2).broadcast_to(sh)
                if k == 2:
                    d.link(dve.tensor_tensor(lg[:, 8], l, W["b_g"][:].unsqueeze(1).broadcast_to(sh), ALU.add))
                    l = lg[:, 8]
                d.link(dve.tensor_reduce(red[:, 0], l, AX.X, ALU.max))
                dve.tensor_tensor(lg[:, 0], l, rd(0), ALU.subtract).then_inc(s_ls, 1)
                dve.wait_ge(s_le, at(s, 2, k))
                d.link(dve.tensor_reduce(red[:, 1], lg[:, 1], AX.X, ALU.add))
                d.link(dve.reciprocal(red[:, 2], red[:, 1]))
                d.link(dve.tensor_tensor(lg[:, 2], lg[:, 1], rd(2), ALU.mult))
                order = C["order"][:].unsqueeze(1).broadcast_to(sh)
                d.link(dve.tensor_reduce(red[:, 3], lg[:, 2], AX.X, ALU.max))
                d.link(dve.tensor_tensor(lg[:, 3], lg[:, 2], rd(3), ALU.is_equal))
                d.link(dve.tensor_tensor(lg[:, 4], lg[:, 3], order, ALU.mult))
                d.link(dve.tensor_reduce(red[:, 4], lg[:, 4], AX.X, ALU.max))
                d.link(dve.tensor_tensor(lg[:, 5], order, rd(4), ALU.is_equal))
                d.link(dve.scalar_tensor_tensor(lg[:, 6], lg[:, 5], -4.0, lg[:, 2], ALU.mult, ALU.add))
                d.link(dve.tensor_reduce(red[:, 5], lg[:, 6], AX.X, ALU.max))
                d.link(dve.tensor_tensor(lg[:, 7], lg[:, 6], rd(5), ALU.is_equal))
                d.link(dve.tensor_tensor(lg[:, 3], lg[:, 7], order, ALU.mult))
                d.link(dve.tensor_reduce(red[:, 6], lg[:, 3], AX.X, ALU.max))
                d.link(dve.tensor_tensor(lg[:, 4], order, rd(6), ALU.is_equal))
                d.link(dve.tensor_tensor(lg[:, 6], lg[:, 4], lg[:, 5], ALU.add))
                d.link(dve.tensor_tensor(lg[:, 7], lg[:, 2], lg[:, 6], ALU.mult))
                d.link(dve.tensor_reduce(red[:, 7], lg[:, 7], AX.X, ALU.add))
                if eps:
                    d.link(dve.tensor_scalar(red[:, 7], red[:, 7], eps, None, ALU.max))
                d.link(dve.reciprocal(red[:, 0], red[:, 7]))
                dve.scalar_tensor_tensor(cw[:], lg[:, 7], factor, rd(0), ALU.mult, ALU.mult).then_inc(s_cw, 1)

            def a_stats(s):
                dve.wait_ge(s_xin, at(s, 16, 16))
                stats(A, df, xin)

            def a_norm(s, last):
                dve.wait_ge(A.s_rs, at(s, 2, 1))
                if last is not None:
                    dve.wait_ge(A.s_tps, at(last, 2, 2))
                norm(A, s, 1, 2, A.nrm, xin, 1).then_inc(A.s_nrm, 1)

            def a_base(s):
                norm(A, s, 1, 2, a0, xin, 0).then_inc(s_xfree, 1)

            def a_rope(s):
                for n, (bank, tab) in enumerate(((2, "cos"), (3, "sin"), (1, "cos"), (0, "sin"))):
                    dve.wait_ge(A.s_qk, at(s, 4, n + 1))
                    dve.tensor_tensor(rope_t[:, n], A.bank[bank][:], C[tab][:], ALU.mult).then_inc(s_rope, 1)

            def a_resid(s):
                dve.wait_ge(A.s_ops, at(s, 1, 1))
                da.link(dve.tensor_tensor(h0[:].rearrange("p j d -> p (j d)"), A.bank[0][:],
                                          a0[:].rearrange("p j d -> p (j d)"), ALU.add))
                stats(A, da, h0)

            def a_norm2(s):
                dve.wait_ge(A.s_rs, at(s, 2, 2))
                norm(A, s, 2, 2, A.nrm, h0, 0).then_inc(A.s_nrm, 1)

            def a_gate(s, ms):
                for m in ms:
                    mt = HT[m]
                    dve.wait_ge(s_th, at(s, 3, m + 1))
                    b1, b3 = (A.bank[2], A.bank[3]) if m % 2 == 0 else (A.bank[0], A.bank[1])
                    da.link(dve.scalar_tensor_tensor(sg[0:mt, m % 2], tanh_t[0:mt, m % 2], 1.0, b1[0:mt, :],
                                                     ALU.add, ALU.mult))
                    dve.wait_ge(s_up, at(s, 6, 2 * m + 2))
                    dve.scalar_tensor_tensor(gt[0:mt, m], sg[0:mt, m % 2], 0.5, b3[0:mt, :],
                                             ALU.mult, ALU.mult).then_inc(s_g, 1)

            def a_end(s):
                dve.wait_ge(s_dn, at(s, 1, 1))
                dve.wait_ge(s_hh, at(s, 1, 1))
                dve.tensor_tensor(x1[:].rearrange("p j d -> p (j d)"), A.bank[0][:],
                                  xh[:].rearrange("p j d -> p (j d)"), ALU.add).then_inc(s_x1, 1)
                da.end()

            def b_stats(s, src, ready, v):
                dve.wait_ge(ready, v)
                stats(B, db, src)

            def b_norm(s, k, src):
                dve.wait_ge(B.s_rs, at(s, 3, k))
                norm(B, s, k, 3, B.nrm, src, 0).then_inc(B.s_nrm, 1)

            def moe_gate(s, e):
                if e == 0:
                    dve.wait_ge(s_fold, at(s, NJ, NJ))
                for m in range(2):
                    dve.wait_ge(s_mth, at(s, 2 * E, 2 * e + m + 1))
                    dve.scalar_tensor_tensor(hs[:, e % 2, m], mth[:, m], 1.0, B.bank[2 + m][:],
                                             ALU.add, ALU.mult).then_inc(s_hs, 1)

            def moe_scale(s, e):
                if e == 0:
                    dve.wait_ge(s_cw, at(s, 2, 1))
                dve.wait_ge(s_y, at(s, E, e + 1))
                if e >= 2:
                    dve.wait_ge(s_acc, at(s, E, e - 1))
                dve.tensor_tensor(yc[:, e % 2], B.bank[e % 2][:].rearrange("p (j d) -> p j d", j=NJ),
                                  cw[:, :, e:e + 1].broadcast_to([P, NJ, D]), ALU.mult).then_inc(s_yc, 1)

            def b_pairs(s):
                dve.wait_ge(s_k32, at(s, 1, 1))
                dve.tensor_tensor(gkd[:], B.k32[:].unsqueeze(1).broadcast_to([D, HEADS, NG]),
                                  C["head_mask"][:].unsqueeze(2).broadcast_to([D, HEADS, NG]),
                                  ALU.mult).then_inc(s_gkd, 1)
                for n in range(2):
                    dve.wait_ge(B.s_hi, at(s, 2, n + 1))
                    dve.tensor_tensor(B.hl[:, 2 * n + 1], B.bank[(3, 0)[n]][:], B.hl[:, 2 * n],
                                      ALU.subtract).then_inc(B.s_hl, 1)

            def b_global(s):
                dve.wait_ge(s_gvp, at(s, 1, 1))
                g4 = B.bank[2][:, 0:256].rearrange("p (a g) -> p a g", g=NG)
                v3 = lambda t: t[:].rearrange("p j h g -> p (j h) g")
                rd = lambda n: gred[:, n].rearrange("p j h -> p (j h)")
                bc = lambda n: rd(n).unsqueeze(2).broadcast_to([P, NJ * HEADS, NG])
                db.link(dve.tensor_reduce(rd(0), g4, AX.X, ALU.max))
                dve.tensor_tensor(v3(gs), g4, bc(0), ALU.subtract).then_inc(s_gsh, 1)
                dve.tensor_tensor(gv[:], B.bank[2][0:64, 256:384], C["gv_mask"][:], ALU.mult).then_inc(s_gv, 1)

            def b_global_probs(s):
                v3 = lambda t: t[:].rearrange("p j h g -> p (j h) g")
                rd = lambda n: gred[:, n].rearrange("p j h -> p (j h)")
                bc = lambda n: rd(n).unsqueeze(2).broadcast_to([P, NJ * HEADS, NG])
                dve.wait_ge(s_ge, at(s, 1, 1))
                db.link(dve.tensor_reduce(rd(1), v3(gp), AX.X, ALU.add))
                db.link(dve.reciprocal(rd(2), rd(1)))
                dve.tensor_tensor(v3(gp), v3(gp), bc(2), ALU.mult).then_inc(s_gp, 1)

            def b_attended(s):
                dve.wait_ge(B.s_obt, at(s, 1, 1))
                dve.wait_ge(s_ogt, at(s, 1, 1))
                dve.tensor_tensor(B.ot[:], B.bank[2][:], ogt[:], ALU.add).then_inc(B.s_ot, 1)

            def b_resid(s):
                dve.wait_ge(B.s_ops, at(s, 1, 1))
                dve.wait_ge(s_x2b, at(s, 1, 1))
                dve.tensor_tensor(x3[:].rearrange("p j d -> p (j d)"), B.bank[0][:],
                                  x2b[:].rearrange("p j d -> p (j d)"), ALU.add).then_inc(B.s_h, 1)

            def b_scale(s, n):
                j, half = n // 2, n % 2
                if n == 0:
                    dve.wait_ge(s_cw, at(s, 2, 2))
                dve.wait_ge(s_ye, at(s, 8, n + 1))
                if n >= 4:
                    dve.wait_ge(s_fold, at(s + 1, NJ, j - 1))
                dve.tensor_tensor(yce[:, j % 2, half].rearrange("p (e d) -> p e d", e=4),
                                  B.bank[(3, 0)[n % 2]][:].rearrange("p (e d) -> p e d", e=4),
                                  cw[:, j, 4 * half:4 * half + 4].unsqueeze(2).broadcast_to([P, 4, D]),
                                  ALU.mult).then_inc(s_yce, 1)

            def b_biases(s):
                dve.wait_ge(s_bp, at(s, 1, 1))
                dve.tensor_tensor(x3b[:].rearrange("p j d -> p (j d)"), B.bank[1][:],
                                  x3[:].rearrange("p j d -> p (j d)"), ALU.add).then_inc(s_x3b, 1)

            def trip(sr, sb_, sf):
                if sb_ is not None:
                    db.begin(sb_)
                    b_stats(sb_, x1, s_x1, at(sb_ + 1, 1, 1))
                    b_norm(sb_, 1, x1)
                    moe_gate(sb_, 0)
                    top2(db, sb_, 1, B.bank[1], 1e-9, 0.5)
                for e in range(E):
                    if sb_ is not None:
                        if e + 1 < E:
                            moe_gate(sb_, e + 1)
                        moe_scale(sb_, e)
                    if sr is not None:
                        if e == 4:
                            da.begin(sr)
                            divide(A, da, sr)
                        elif e == 6:
                            a_resid(sr)
                        elif e == 7:
                            a_norm2(sr)
                if sb_ is not None:
                    b_stats(sb_, acc, s_acc, at(sb_, E, E))
                if sf is not None:
                    df.begin(sf)
                    a_stats(sf)
                if sb_ is not None:
                    b_norm(sb_, 2, acc)
                if sr is not None:
                    a_gate(sr, (0,))
                if sf is not None:
                    a_norm(sf, sr)
                if sr is not None:
                    a_gate(sr, (1, 2))
                if sf is not None:
                    a_base(sf)
                if sb_ is not None:
                    b_pairs(sb_)
                if sr is not None:
                    a_end(sr)
                if sf is not None:
                    a_rope(sf)
                if sb_ is not None:
                    b_global(sb_)
                    k_blocks(B, sb_)
                    b_global_probs(sb_)
                    for f in range(NMF):
                        maxima(B, sb_, f)
                    max_split(B, db, sb_)
                if sf is not None:
                    for f in range(NMF):
                        maxima(A, sf, f)
                    max_split(A, df, sf)
                    df.end()
                for n in range(TAIL):
                    if sb_ is not None:
                        if n == 0:
                            divide(B, db, sb_)
                        elif n == 1:
                            b_attended(sb_)
                        elif n == 2:
                            b_resid(sb_)
                            b_stats(sb_, x3, B.s_h, at(sb_, 1, 1))
                        elif n == 4:
                            b_norm(sb_, 3, x3)
                            top2(db, sb_, 2, B.bank[2], None, 1.0)
                        elif n >= 5:
                            b_scale(sb_, n - 5)
                if sb_ is not None:
                    b_biases(sb_)
                    db.end()
            trip(None, None, 0)
            trip(0, None, 1)
            with dve.Fori(1, SEQS - 1) as i:
                trip(i, i - 1, i + 1)
            trip(SEQS - 1, SEQS - 2, None)
            trip(None, SEQS - 1, None)

        @block.gpsimd
        def _(pool):
            pool.sem_inc(s_xfree, 1)
            pool.sem_inc(s_out, 16)
            pool.sem_inc(s_fold, NJ)
            pool.wait_ge(s_c, n_c)
            pa, pb = Steps(pool, A.s_pool, POOL_A), Steps(pool, B.s_pool, POOL_B)
            pf = Steps(pool, s_poolf, POOL_F)
            def copy(o, i):
                return pool.tensor_scalar(o, i, 1.0, 1.0, ALU.mult, ALU.mult)

            for th in (A, B):
                pool.memset(th.vb[:].rearrange("p k g a h d -> p (k g a h d)"), 0.0).then_inc(s_vclear, 1)
            pool.wait_ge(s_vclear, 2)
            for th in (A, B):
                ins = copy(th.vb[:].rearrange("p k g a h d -> p (k g) a (h d)")[:, :, 1, :],
                           C["ones_bd"][:].unsqueeze(1).broadcast_to([P, NB * HG, KB]))
            ins.then_inc(s_init, 1)

            def rstd(th, p, s, k, per, both):
                pool.wait_ge(th.s_mv, at(s, per, k))
                pass_on(pool, s_passed["pool"])
                n = 2 if both else 1
                var = th.mv[:, :, 1]
                if both:
                    p.mark(pool.tensor_scalar(th.ve[:, 1], var, 1.0 + EPS, EPS * EPS, ALU.mult, ALU.add))
                p.link(pool.tensor_scalar(th.ve[:, 0], var, EPS, 1.0, ALU.add, ALU.mult))
                pool.tensor_tensor(th.rs[:, 0:n], th.ve[:, 0:n], C["half"][:, 0:n], ALU.pow).then_inc(th.s_rs, 1)

            def a_sum(s):
                for n, dst in ((0, A.q32), (1, A.k32)):
                    pool.wait_ge(s_rope, at(s, 4, 2 * n + 2))
                    pool.tensor_tensor(dst[:], rope_t[:, 2 * n], rope_t[:, 2 * n + 1], ALU.add).then_inc(s_q32, 1)
                for n, src in ((0, A.q32), (1, A.k32)):
                    pool.wait_ge(A.s_hi, at(s, 2, n + 1))
                    pool.tensor_tensor(A.hl[:, 2 * n + 1], src[:], A.hl[:, 2 * n], ALU.subtract).then_inc(A.s_hl, 1)

            def moe_sum(s, e):
                pool.wait_ge(s_yc, at(s, E, e + 1))
                if e >= 1:
                    pool.wait_ge(s_acc, at(s, E, e))
                pool.tensor_tensor(acc[:], yc[:, e % 2], (x1 if e == 0 else acc)[:], ALU.add).then_inc(s_acc, 1)

            def fold_experts(s):
                for j in range(NJ):
                    pool.wait_ge(s_yce, at(s + 1, 8, 2 * j + 2))
                    f = fold[:, 0]
                    pb.link(pool.tensor_tensor(f, yce[:, j % 2, 0], yce[:, j % 2, 1], ALU.add))
                    pb.link(pool.tensor_tensor(fold[:, 1, 0:2 * D], f[:, 0:2 * D], f[:, 2 * D:4 * D], ALU.add))
                    pool.tensor_tensor(fsum[:, j], fold[:, 1, 0:D], fold[:, 1, D:2 * D], ALU.add).then_inc(s_fold, 1)

            def k_blocks(th, s):
                pool.wait_ge(th.s_rep, at(s, 96, 96))
                pass_on(pool, s_passed["pool"])
                for g in range(HG):
                    for h in range(4):
                        ins = pool.tensor_scalar(th.kd[0:PAIR, g, PADB:, h, :],
                                                 th.kr[0:PAIR, g, :].rearrange("p (b k) -> p b k", k=KB),
                                                 C["own_head"][0:PAIR, h:h + 1], 1.0, ALU.mult, ALU.mult)
                ins.then_inc(th.s_kd, 1)

            def trip(sr, sb_, sf):
                if sb_ is not None:
                    pb.begin(sb_)
                    rstd(B, pb, sb_, 1, 3, False)
                for e in range(E):
                    if sb_ is not None:
                        moe_sum(sb_, e)
                    if sr is not None and e == 6:
                        pa.begin(sr)
                        rstd(A, pa, sr, 2, 2, False)
                        pool.tensor_tensor(xh[:], xres[:], h0[:], ALU.add).then_inc(s_hh, 1)
                        pa.end()
                if sb_ is not None:
                    rstd(B, pb, sb_, 2, 3, False)
                if sf is not None:
                    pf.begin(sf)
                    rstd(A, pf, sf, 1, 2, True)
                if sb_ is not None:
                    pool.tensor_tensor(x2b[:], acc[:], W["b_out"][:].unsqueeze(1).broadcast_to([P, NJ, D]),
                                       ALU.add).then_inc(s_x2b, 1)
                if sf is not None:
                    copy(xres[:].rearrange("p j d -> p (j d)"), xin[:].rearrange("p j d -> p (j d)")).then_inc(s_xfree, 1)
                    a_sum(sf)
                    k_blocks(A, sf)
                    pf.end()
                if sb_ is not None:
                    rstd(B, pb, sb_, 3, 3, False)
                    fold_experts(sb_)
                    pool.wait_ge(s_fold, at(sb_ + 1, NJ, NJ))
                    pool.wait_ge(s_x3b, at(sb_ + 1, 1, 1))
                    pool.wait_ge(s_out, at(sb_, 16, 16))
                    pool.tensor_tensor(xout[:], fsum[:], x3b[:], ALU.add).then_inc(s_xo, 1)
                    pb.end()
            trip(None, None, 0)
            pool.wait_ge(s_w2, n_w2)
            trip(0, None, 1)
            with pool.Fori(1, SEQS - 1) as i:
                trip(i, i - 1, i + 1)
            trip(SEQS - 1, SEQS - 2, None)
            trip(None, SEQS - 1, None)


def _constants():

    f32, f16, bf16 = np.float32, np.float16, np.dtype("bfloat16")
    p = np.arange(P)
    q, j = p % KB, p // KB
    w = np.arange(WIN)
    own = np.where((w[None] >= q[:, None]) & (w[None] <= q[:, None] + WINDOW), 0.0, BIG)
    first = np.where(KB * (j[:, None] - 4) + w[None] >= 0, own, BIG)
    edges = own.reshape(P, 5, KB)[:, [0, 4]]
    freqs = (1.0 / np.power(f32(10000.0), np.arange(0, HD, 2, dtype=f32) / f32(HD))).astype(f32)
    ang = np.outer(freqs, np.arange(T, dtype=f32)).astype(f32)
    d, d_head = p % HD, p // HD % 4
    sign = np.where(d % 2 == 0, -1.0, 1.0)[:, None]
    g = np.arange(HEADS * NG) // NG
    ind = np.zeros((8, HG * (PADB + NB), 4, KB), f16)
    for r in range(8):
        ind[r, :, r % 4] = MSCALE
    ind = ind.reshape(8, -1)
    rep = lambda a, n: np.repeat(a[:, None], n, 1)
    c = {
        "ident": np.eye(P, dtype=f32),
        "identb": np.eye(P).astype(bf16),
        "identh": np.eye(P, dtype=f16),
        "mask_first": rep(first, PB).astype(bf16),
        "mask_q": rep(edges, PB).astype(bf16),
        "mask_tail": rep(edges[:, 0], 4).astype(bf16),
        "ones_bd": (j[:, None] == (p[None, :KB] // HD)).astype(f32),
        "cos": np.cos(ang[d // 2].astype(np.float64)).astype(f32),
        "sin": (np.sin(ang[d // 2].astype(np.float64)) * sign).astype(f32),
        "head_mask": (p[:, None] // HD == np.arange(HEADS)[None]).astype(f32),
        "gv_mask": (g[:, None] == p[None] // HD).astype(f32),
        "half": np.full((P, 2, NJ), -0.5, f32),
        "own_head": (d_head[:, None] == np.arange(4)[None]).astype(f32),
        "order": np.broadcast_to(E - np.arange(E, dtype=f32), (P, E)),
    }
    return {k: np.ascontiguousarray(v) for k, v in c.items()}, ind


def kernel(**inputs):
    import concourse.bacc as bacc
    from concourse.bass_utils import run_bass_kernel_spmd

    i = {k: np.asarray(v) for k, v in inputs.items()}
    swap = np.arange(D) ^ 1
    w2 = np.zeros((3 * P, D), i["L0_attn_w2"].dtype)
    w2[:HID] = i["L0_attn_w2"]
    qkv = i["L1_attn_w_qkv"].T
    w = {
        "wq": i["L0_attn_wq"], "wqs": i["L0_attn_wq"][:, swap],
        "wk": i["L0_attn_wk"], "wks": i["L0_attn_wk"][:, swap],
        "wv": i["L0_attn_wv"], "wo": i["L0_attn_wo"],
        "ln": np.stack([i["L0_attn_ln1_g"], i["L0_attn_ln1_b"], i["L0_attn_ln2_g"], i["L0_attn_ln2_b"]], 1),
        "w1": i["L0_attn_w1"], "w3": i["L0_attn_w3"], "w2": w2.reshape(3, P, D).transpose(1, 0, 2),
        "router": i["L0_ffn_router_w"],
        "m1": i["L0_ffn_w1"].transpose(1, 0, 2),
        "m2": i["L0_ffn_w2"].reshape(E, 2, P, D).transpose(2, 0, 1, 3),
        "bq": qkv[:, :D], "bk": qkv[:, D:2 * D], "bv": qkv[:, 2 * D:],
        "bo": i["L1_attn_w_out"].T, "b_out": np.broadcast_to(i["L1_attn_b_out"], (P, D)),
        "wg": i["L1_ffn_Wg"], "b_g": np.broadcast_to(i["L1_ffn_bg"], (P, E)),
        "we": i["L1_ffn_We"].transpose(1, 0, 2).reshape(D, E * D), "be": i["L1_ffn_be"],
    }
    w = {k: np.ascontiguousarray(v) for k, v in w.items()}
    c, ind = _constants()
    x = np.ascontiguousarray(i["L0_attn_x"]).reshape(SEQS * T, D)
    nc = bacc.Bacc("TRN2", target_bir_lowering=False, num_devices=1)
    arrays = {}

    def dram(name, a):
        arrays[name] = a
        return nc.dram_tensor(name, a.shape, mybir.dt.from_np(a.dtype), kind="ExternalInput").ap()

    w_in = {k: dram(f"w_in_{k}", v) for k, v in w.items()}
    c_in = {k: dram(f"c_in_{k}", v) for k, v in c.items()}
    x_in, ind_in = dram("x_dram", x), dram("ind_dram", ind)
    out = nc.dram_tensor("out_dram", x.shape, F32, kind="ExternalOutput").ap()
    model_kernel(nc, x_in, out, w_in, c_in, ind_in)
    r = run_bass_kernel_spmd(nc, [arrays], core_ids=[0])
    return r.results[0]["out_dram"].reshape(SEQS, T, D)
```

```python
from contextlib import ExitStack

import numpy as np

import concourse.bass as bass
from concourse import mybir

F32 = mybir.dt.float32
F16 = mybir.dt.float16
BF16 = mybir.dt.bfloat16
ALU = mybir.AluOpType
ACT = mybir.ActivationFunctionType
AX = mybir.AxisListType

P = 128
D = 128
SEQS, T = 8, 512
NJ = T // P
HEADS, HD = 16, 8
HG = 4
KB = 32
NB = T // KB
WINDOW = 128
PADB = WINDOW // KB
WIN = WINDOW + KB
HID = 352
HT = (128, 128, 96)
E = 8
FE = 256
STRIDE = 128
NG = T // STRIDE
EPS = 1e-5
SCALE = HD ** -0.5
MSCALE = 1024.0
PAIR = 3 * KB
ROWS = PAIR + 8
BIG = -1.0e30
PB = 3

MAX_FILLS = [list(range(w, min(w + PB, NJ * HEADS))) for w in range(0, NJ * HEADS, PB)]


def exp_fills():
    full = [(kb, hg) for kb in range(NB - 4) for hg in range(HG)]
    fills = [[(kb, hg, n * WIN, WIN) for n, (kb, hg) in enumerate(full[i:i + PB])]
             for i in range(0, len(full), PB)]
    for kbs in ((NB - 4,), (NB - 3,), (NB - 2, NB - 1)):
        at, tiles = 0, []
        for kb in kbs:
            n = T - KB * kb
            for hg in range(HG):
                tiles.append((kb, hg, at, n))
                at += n
        fills.append(tiles)
    return fills


EXP_FILLS = exp_fills()
NMF, NEF = len(MAX_FILLS), len(EXP_FILLS)


def at(s, per, k):
    return s * per + k


def pass_on(eng, passed):
    eng.sem_inc(passed, 1)


TAIL = 17
EXP_LEAD = 2
EXP_E = 1
MAX_LEAD = 7
MAX_E = 12
MAX_ROWS = 13


def expert_in_tail(n):
    return {8: 0, 9: 1}.get(n, n - 9 if n >= 11 else None)


def exp_until(e):
    first = TAIL + EXP_LEAD
    return min(NEF + 1, first + -(-(NEF + 1 - first) * (e + 1) // EXP_E))


def max_until(f):
    return min(NMF, MAX_LEAD + -(-(NMF - MAX_LEAD) * (f + 1) // MAX_E))


class Steps:

    def __init__(self, eng, sem, per):
        self.eng, self.sem, self.per, self.n, self.s = eng, sem, per, 0, 0

    def begin(self, s):
        self.s, self.n = s, 0

    def mark(self, ins):
        ins.then_inc(self.sem, 1)
        self.n += 1
        return self.n

    def wait(self, n=None):
        self.eng.wait_ge(self.sem, at(self.s, self.per, self.n if n is None else n))

    def link(self, ins):
        self.mark(ins)
        self.wait()

    def end(self):
        assert self.n == self.per, (self.sem, self.n)


FRONT = ("wq", "wqs", "wk", "wks", "wv")
REST_W = ("wo", "w1", "w3", "w2", "router", "m1", "m2", "bq", "bk", "bv", "bo", "b_out", "wg", "b_g", "we", "be")

FIRST_C = ("half", "ident")
SPLIT_W = ("m1", "we")
WSCALE = 64.0
PRODUCTS = ((0, 0), (0, 1), (1, 0))

DVE_F, DVE_N, DVE_A, DVE_B = 5, NJ, 12, 56
POOL_F, POOL_N, POOL_A, POOL_B = 2, 1, 1, 10
ACT_B = 1


def model_kernel(nc, x, out, w, c, indicator):
    x_v = x.rearrange("(s j p) d -> s p j d", p=P, j=NJ)
    out_v = out.rearrange("(s j p) d -> s p j d", p=P, j=NJ)
    ctx = ExitStack()
    with ctx:
        def sb(name, shape, dt=F32):
            return ctx.enter_context(nc.sbuf_tensor(name, shape, dt))

        def sem(name):
            return ctx.enter_context(nc.semaphore(name))

        W = {n: sb(f"w_{n}", list(a.shape), a.dtype) for n, a in w.items() if n not in SPLIT_W}
        C = {n: sb(f"c_{n}", list(a.shape), a.dtype) for n, a in c.items()}
        for n_, name in enumerate(FRONT):
            W[name] = W["front"][:, D * n_:D * (n_ + 1)]
        W["ln"] = W["front"][:, D * len(FRONT):]
        s_w = sem("weights_in")
        s_c = sem("constants_in")
        s_c1 = sem("first_constants_in")
        s_init = sem("buffers_cleared")
        s_vclear = sem("v_blocks_cleared")
        s_w2 = sem("later_weights_in")
        n_w, n_w2, n_c1, n_c = 16, 16 * len(REST_W), 16 * len(FIRST_C), 16 * (len(c) - len(FIRST_C))

        class Thread:

            def __init__(self, t):
                self.t = t
                self.bank = [ctx.enter_context(nc.psum_tensor(f"{t}_bank{i}", [P, 512], F32)) for i in range(4)]
                self.st = sb(f"{t}_st", [P, NJ, 6])
                self.mv = sb(f"{t}_mv", [P, NJ, 2])
                self.ve = sb(f"{t}_ve", [P, 2, NJ])
                self.rs = sb(f"{t}_rs", [P, 2, NJ])
                self.nrm = sb(f"{t}_nrm", [P, NJ, D])
                self.ft = sb(f"{t}_ft", [D, T])
                self.q32 = sb(f"{t}_q32", [D, T])
                self.k32 = sb(f"{t}_k32", [D, T if t == "a" else NG])
                self.ot = self.q32
                self.hl = sb(f"{t}_hl", [D, 4, T], F16)
                self.scr = nc.dram_tensor(f"{t}_scr", (4, D, T), F16, kind="Internal").ap()
                self.qr = sb(f"{t}_qr", [P, HG, T], F16)
                self.kr = self.hl
                self.kd = sb(f"{t}_kd", [P, HG, PADB + NB, 4, KB], F16)
                self.vb = sb(f"{t}_vb", [P, NB, HG, 2, 4, HD])
                self.m = sb(f"{t}_m", [P, NJ * HEADS])
                self.mhl = sb(f"{t}_mhl", [P, NJ, HG, 2, 4], F16)
                self.mt = sb(f"{t}_mt", [HG * 8, T], F16)
                self.p = sb(f"{t}_p", [P, 4, 512])
                self.nd, self.ob = self.p[:, 0:2], self.p[:, 2].rearrange("p (j g h d) -> p j g h d", j=NJ, g=HG, h=4)
                self.rd = sb(f"{t}_rd", [P, 2, NJ, 2, 4])
                self.s_mv = sem(f"{t}_stats_ready")
                self.s_rs = sem(f"{t}_rstd_ready")
                self.s_nrm = sem(f"{t}_normed")
                self.s_tps = sem(f"{t}_transposed")
                self.s_ft = sem(f"{t}_features_ready")
                self.s_qk = sem(f"{t}_qk_projected")
                self.s_hl = sem(f"{t}_pairs_split")
                self.s_hi = sem(f"{t}_high_parts")
                self.s_vps = sem(f"{t}_v_projected")
                self.s_vb = sem(f"{t}_v_placed")
                self.s_scr = sem(f"{t}_pairs_out")
                self.s_rep = sem(f"{t}_q_spread")
                self.s_krep = sem(f"{t}_k_spread")
                self.s_kd0 = sem(f"{t}_k_groups_0_1")
                self.s_kd1 = sem(f"{t}_k_groups_2_3")
                self.s_mfill = sem(f"{t}_max_scores")
                self.s_mdone = sem(f"{t}_max_taken")
                self.s_mhl = sem(f"{t}_max_split")
                self.s_mtp = sem(f"{t}_max_transposed")
                self.s_mt = sem(f"{t}_max_rows")
                self.s_shift = sem(f"{t}_max_placed")
                self.s_sfill = sem(f"{t}_scores")
                self.s_exp = sem(f"{t}_exp_done")
                self.s_pv = sem(f"{t}_pv_done")
                self.s_nd = sem(f"{t}_sums_copied")
                self.s_ndt = sem(f"{t}_sums_transposed")
                self.s_ob = sem(f"{t}_divided")
                self.s_obt = sem(f"{t}_quotient_transposed")
                self.s_ot = sem(f"{t}_attended")
                self.s_ops = sem(f"{t}_attn_projected")
                self.s_h = sem(f"{t}_residual_added")
                self.s_dve = sem(f"{t}_dve_steps")
                self.s_pool = sem(f"{t}_pool_steps")

        A, B = Thread("a"), Thread("b")
        s_passed = {n: sem(f"{n}_passed") for n in ("pe", "dve", "pool")}

        xin = sb("xin", [P, NJ, D])
        xres = sb("xres", [P, NJ, D])
        a0 = sb("a0", [P, NJ, D])
        rope_t = A.p
        h0 = sb("h0", [P, NJ, D])
        xh = sb("xh", [P, NJ, D])
        tanh_t, sg = rope_t[:, 0:2], rope_t[:, 2:4]
        gt = sb("gt", [P, 3, T])
        x1 = sb("x1", [P, NJ, D])
        s_xin = sem("x_in")
        s_poolf = sem("front_pool_steps")
        s_dvef = sem("front_dve_steps")
        s_dven = sem("x1_norm_dve_steps")
        s_pooln = sem("x1_norm_pool_steps")
        s_xfree = sem("x_copied")
        s_rope = sem("rope_products")
        s_q32 = sem("rope_summed")
        s_hh = sem("h_plus_x")
        s_up = sem("ffn_up")
        s_th = sem("ffn_tanh")
        s_g = sem("ffn_gated")
        s_dn = sem("ffn_down")
        s_x1 = sem("x1_ready")

        acc = sb("acc", [P, NJ, D])
        lg = sb("lg", [P, 10, NJ, E])
        red = sb("red", [P, 8, NJ])
        cw = sb("cw", [P, NJ, E])
        mth = sb("mth", [P, 2, T])
        hs = B.p[:].rearrange("p (a b) n -> p a b n", a=2)
        fold = sb("fold", [P, 2, NJ * D])
        whole = {"m1": B.p[:].rearrange("p a n -> p (a n)"), "we": fold[:].rearrange("p a n -> p (a n)")}
        pair = {n: sb(f"pair_{n}", [P, 2, whole[n].shape[1]], F16) for n in SPLIT_W}
        s_whi = sem("weights_high_parts")
        s_wlo = sem("weights_remainders")
        fpair = sb("fpair", [D, 2, T], F16)
        s_fhi = sem("features_high_part")
        s_flo = sem("features_remainder")
        gkd = sb("gkd", [D, HEADS, NG])
        gft = sb("gft", [D, HEADS * NG])
        gs = sb("gs", [P, NJ, HEADS, NG])
        gp = sb("gp", [P, NJ, HEADS, NG])
        gred = sb("gred", [P, 3, NJ, HEADS])
        gpt = sb("gpt", [HEADS * NG, T])
        gv = sb("gv", [HEADS * NG, D])
        ogt = sb("ogt", [D, T])
        x2b = sb("x2b", [P, NJ, D])
        x3 = sb("x3", [P, NJ, D])
        cwt = gpt[0:E, :]
        yce = hs
        x3b = x2b
        fsum = acc
        xout = sb("xout", [P, NJ, D])
        s_lg = sem("logits")
        s_le = sem("gate_exp")
        s_ls = sem("gate_shifted")
        s_cw = sem("gates_ready")
        s_mup = sem("moe_up")
        s_mth = sem("moe_tanh")
        s_hs = sem("moe_hidden")
        s_y = sem("moe_down")
        s_acc = sem("moe_summed")
        s_k32 = sem("k_copied")
        s_gkd = sem("global_keys")
        s_gsh = sem("global_shifted")
        s_ge = sem("global_exp")
        s_gp = sem("global_probs")
        s_gpp = sem("global_probs_transposed")
        s_gpt = sem("global_probs_rows")
        s_gvp = sem("global_v_projected")
        s_gv = sem("global_v_placed")
        s_ogp = sem("global_out")
        s_ogt = sem("global_out_copied")
        s_x2b = sem("x2_plus_bias")
        s_cwp = sem("gates_transposed")
        s_cwt = sem("gates_rows")
        s_ye = sem("expert_out")
        s_yce = sem("expert_gated")
        s_fold = sem("expert_folded")
        s_bp = sem("expert_bias")
        s_x3b = sem("x3_plus_biases")
        s_ind = sem("indicator_rows_in")
        s_xo = sem("x_out_ready")
        s_out = sem("x_stored")

        block = ctx.enter_context(nc.Block())

        @block.sync
        def _(sp):
            def load(s):
                sp.wait_ge(s_xfree, at(s, 2, 2))
                sp.dma_start(xin[:], x_v[s]).then_inc(s_xin, 16)

            def spread(th, s):
                sp.wait_ge(th.s_hl, at(s, 2, 2))
                sp.dma_start(th.scr.rearrange("c p n -> p c n"), th.hl[:]).then_inc(th.s_scr, 16)
                sp.wait_ge(th.s_scr, at(s, 16, 16))
                sp.wait_ge(th.s_pv, at(s, NEF, NEF))
                rows = th.scr.rearrange("c (g r) n -> c r g n", g=HG)
                for part, of in ((0, 2), (1, 2), (2, 3)):
                    sp.dma_start(th.kr[KB * part:KB * (part + 1), :, :], rows[of]).then_inc(th.s_krep, 16)
                for part, of in ((0, 0), (1, 1), (2, 0)):
                    sp.dma_start(th.qr[KB * part:KB * (part + 1), :, :], rows[of]).then_inc(th.s_rep, 16)

            def place_rows(th, s):
                sp.wait_ge(th.s_mt, at(s, 1, 1))
                for g in range(HG):
                    sp.dma_start(th.qr[PAIR:ROWS, g, :], th.mt[8 * g:8 * g + 8, :]).then_inc(th.s_shift, 16)

            def store(s):
                sp.wait_ge(s_xo, at(s + 1, 1, 1))
                sp.dma_start(out_v[s], xout[:]).then_inc(s_out, 16)

            load(0)
            sp.dma_start(W["front"][:], w["front"]).then_inc(s_w, 16)
            for th in (A, B):
                sp.dma_start(th.kd[PAIR:ROWS].rearrange("p g b h k -> p (g b h k)"), indicator).then_inc(s_ind, 16)
            for n in REST_W:
                sp.dma_start(whole[n] if n in SPLIT_W else W[n][:], w[n]).then_inc(s_w2, 16)

            def trip(sr, sb_, sf):
                if sf is not None and sr is not None:
                    load(sf)
                if sb_ is not None:
                    spread(B, sb_)
                if sf is not None:
                    spread(A, sf)
                if sb_ is not None:
                    place_rows(B, sb_)
                if sf is not None:
                    place_rows(A, sf)
                if sb_ is not None:
                    store(sb_)
            trip(None, None, 0)
            trip(0, None, 1)
            with sp.Fori(1, SEQS - 1) as i:
                trip(i, i - 1, i + 1)
            trip(SEQS - 1, SEQS - 2, None)
            trip(None, SEQS - 1, None)
            sp.wait_ge(s_out, 16 * SEQS + 16)

        @block.tensor
        def _(pe):
            def transposes(th, s, k, per, bank, src):
                for j in range(NJ):
                    pe.wait_ge(th.s_nrm, at(s, NJ * per, NJ * (k - 1) + j + 1))
                    mm = pe.transpose(bank[:, P * j:P * (j + 1)], src[:, j, :], C["ident"][:])
                mm.then_inc(th.s_tps, 1)

            def project(th, bank, wt, m=P):
                return pe.matmul(bank[0:m, :], wt, th.ft[:], start=True, stop=True)

            def v_rows(th, bank, wv):
                token_major(bank, th.ft, wv[:]).then_inc(th.s_vps, 1)

            def max_fill(th, s, f):
                bank = th.bank[f % 2]
                if f == 0:
                    pe.wait_ge(th.s_rep, at(s, 48, 48))
                for g in range(HG):
                    if 4 * g in MAX_FILLS[f]:
                        pe.wait_ge(th.s_kd0 if g < 2 else th.s_kd1, at(s, 2, g % 2 + 1))
                if f == 1:
                    pe.wait_ge(th.s_vb, at(s, 1, 1))
                if f >= 2:
                    pe.wait_ge(th.s_mdone, at(s, NMF, f - 1))
                ws = MAX_FILLS[f]
                runs = []
                for n, wd in enumerate(ws):
                    key = (wd // HEADS, wd % HEADS // 4)
                    if runs and runs[-1][0] == key:
                        runs[-1][3] += 1
                    else:
                        runs.append([key, n, wd % 4, 1])
                for r, ((J, hg), n0, h0_, n) in enumerate(runs):
                    for j in range(4):
                        qb = 4 * J + j
                        pe.matmul(bank[KB * j:KB * (j + 1), WIN * n0:WIN * (n0 + n)].rearrange("p (a b c) -> p a b c", a=n, c=KB),
                                  th.qr[0:PAIR, hg, KB * qb:KB * (qb + 1)],
                                  th.kd[0:PAIR, hg, qb:qb + WIN // KB, h0_:h0_ + n, :].rearrange("p b h k -> p h b k"),
                                  start=(r == 0), stop=False, skip_group_check=True)
                first = [wd for wd in ws if wd < HEADS]
                rest = len(ws) - len(first)
                if first:
                    n = len(first)
                    mm = pe.matmul(bank[:, 0:WIN * n].rearrange("p (a b) -> p a b", a=n), C["identb"][:],
                                   C["mask_first"][:, 0:n, :], start=False, stop=True, skip_group_check=True)
                if rest:
                    n = len(first)
                    o = bank[:, WIN * n:WIN * len(ws)].rearrange("p (a b c) -> p a b c", a=rest, c=KB)
                    mm = pe.matmul(o[:, :, 0:5:4, :], C["identb"][:], C["mask_q"][:, 0:rest, :, :],
                                   start=False, stop=True, skip_group_check=True)
                mm.then_inc(th.s_mfill, 1)

            def max_rows(th, s):
                pe.wait_ge(th.s_mhl, at(s, 1, 1))
                bank = th.bank[2][0:4 * 8, 0:T // 2].bitcast(F16)
                for j in range(NJ):
                    mm = pe.transpose(bank[:, P * j:P * (j + 1)],
                                      th.mhl[:, j].rearrange("p g r h -> p (g r h)"), C["identh"][:])
                mm.then_inc(th.s_mtp, 1)

            def exp_fill(th, s, f):
                bank = th.bank[f % 2]
                if f == 0:
                    pe.wait_ge(th.s_shift, at(s, 64, 64))
                    pe.wait_ge(th.s_vb, at(s, 1, 1))
                if f < 2:
                    pe.wait_ge(th.s_mdone, at(s, NMF, NMF - 1 + f))
                else:
                    pe.wait_ge(th.s_exp, at(s, NEF, f - 1))
                tiles = EXP_FILLS[f]
                for n, (kb, hg, col, q) in enumerate(tiles):
                    pe.matmul(bank[:, col:col + q], th.kd[0:ROWS, hg, PADB + kb].rearrange("p h k -> p (h k)"),
                              th.qr[0:ROWS, hg, KB * kb:KB * kb + q],
                              start=(n == 0), stop=False, skip_group_check=True)
                if f < NEF - 3:
                    o = bank[:, 0:WIN * PB].rearrange("p (a b c) -> p a b c", a=PB, c=KB)
                    mm = pe.matmul(o[:, :, 0:5:4, :], C["identb"][:], C["mask_q"][:],
                                   start=False, stop=True, skip_group_check=True)
                else:
                    for q in sorted({t[3] for t in tiles}):
                        mine = [t for t in tiles if t[3] == q]
                        o = bank[:, mine[0][2]:mine[0][2] + 4 * q].rearrange("p (a b) -> p a b", a=4)
                        mm = pe.matmul(o[:, :, 0:KB], C["identb"][:], C["mask_tail"][:],
                                       start=False, stop=True, skip_group_check=True)
                mm.then_inc(th.s_sfill, 1)

            def pv(th, s, f):
                pe.wait_ge(th.s_exp, at(s, NEF, f + 1))
                for kb, hg, col, q in EXP_FILLS[f]:
                    half = 64 * (hg % 2)
                    mm = pe.matmul(th.bank[2 + hg // 2][half:half + 64, KB * kb:KB * kb + q],
                                   th.vb[:, kb, hg].rearrange("p a h d -> p (a h d)"), th.p[:, f % 3, col:col + q],
                                   start=(kb == 0), stop=(f == NEF - 1), skip_group_check=True)
                mm.then_inc(th.s_pv, 1)

            def quotient(th, s):
                pe.wait_ge(th.s_nd, at(s, 1, 1))
                for half in range(2):
                    for j in range(NJ):
                        mm = pe.transpose(th.bank[half][:, P * j:P * (j + 1)], th.nd[:, half, P * j:P * (j + 1)],
                                          C["ident"][:])
                mm.then_inc(th.s_ndt, 1)

            def quotient_back(th, s):
                pe.wait_ge(th.s_ob, at(s, 1, 1))
                for j in range(NJ):
                    mm = pe.transpose(th.bank[2][:, P * j:P * (j + 1)],
                                      th.ob[:, j].rearrange("p g h d -> p (g h d)"), C["ident"][:])
                mm.then_inc(th.s_obt, 1)

            def token_major(bank, lhs, rhs):
                for j in range(NJ):
                    mm = pe.matmul(bank[:, P * j:P * (j + 1)], lhs[:, P * j:P * (j + 1)], rhs, start=True, stop=True)
                return mm

            def a_front_turn(s, last):
                if last is not None:
                    pe.wait_ge(s_g, at(last, 3, 2))
                transposes(A, s, 1, 2, A.bank[1], A.nrm)

            def a_project(s):
                bk = A.bank
                pe.wait_ge(A.s_ft, at(s, 2, 1))
                project(A, bk[2], W["wq"][:]).then_inc(A.s_qk, 1)
                project(A, bk[3], W["wqs"][:]).then_inc(A.s_qk, 1)
                project(A, bk[1], W["wk"][:]).then_inc(A.s_qk, 1)
                pe.wait_ge(s_x1, at(s, 1, 1))
                project(A, bk[0], W["wks"][:]).then_inc(A.s_qk, 1)

            def a_v(s):
                pe.wait_ge(s_rope, at(s, 4, 1))
                v_rows(A, A.bank[2], W["wv"])

            def a_out(s):
                pe.wait_ge(A.s_ot, at(s, 1, 1))
                token_major(A.bank[0], A.ot, W["wo"][:]).then_inc(A.s_ops, 1)

            def a_turn(s):
                transposes(A, s, 2, 2, A.bank[1], A.nrm)

            def a_up(s, ms):
                bk = A.bank
                pe.wait_ge(A.s_ft, at(s, 2, 2))
                for m in ms:
                    mt, at_ = HT[m], sum(HT[:m])
                    b1, b3 = (bk[2], bk[3]) if m % 2 == 0 else (bk[0], bk[1])
                    if m == 2:
                        pe.wait_ge(s_g, at(s, 3, 1))
                    project(A, b1, W["w1"][:, at_:at_ + mt], mt).then_inc(s_up, 1)
                    project(A, b3, W["w3"][:, at_:at_ + mt], mt).then_inc(s_up, 1)

            def a_down(s):
                bk = A.bank
                pe.wait_ge(s_g, at(s, 3, 3))
                for j in range(NJ):
                    for m, mt in enumerate(HT):
                        mm = pe.matmul(bk[0][:, P * j:P * (j + 1)], gt[0:mt, m, P * j:P * (j + 1)],
                                       W["w2"][0:mt, m, :], start=(m == 0), stop=(m == 2))
                mm.then_inc(s_dn, 1)

            def b_route(s):
                pe.wait_ge(s_yce, at(s, 8, 8))
                transposes(B, s, 1, 3, B.bank[0], B.nrm)

            def b_logits(s):
                pe.wait_ge(B.s_ft, at(s, 3, 1))
                pe.wait_ge(s_x3b, at(s, 1, 1))
                for j in range(NJ):
                    mm = pe.matmul(B.bank[1][:, E * j:E * (j + 1)], B.ft[:, P * j:P * (j + 1)], W["router"][:],
                                   start=True, stop=True)
                mm.then_inc(s_lg, 1)

            def moe_up(s, e):
                for m in range(2):
                    if e >= 1:
                        pe.wait_ge(s_hs, at(s, 2 * E, 2 * (e - 1) + m + 1))
                    if e == 0 and m == 0:
                        pe.wait_ge(s_flo, at(s, 2, 1))
                    at_ = FE * e + P * m
                    for n, (a, b) in enumerate(PRODUCTS):
                        mm = pe.matmul(B.bank[2 + m][:], pair["m1"][:, a, at_:at_ + P], fpair[:, b],
                                       start=(n == 0), stop=(n == 2))
                    mm.then_inc(s_mup, 1)

            def moe_down(s, e):
                bank = B.bank[e % 2]
                if e >= 2:
                    pe.wait_ge(s_acc, at(s, E, e - 1))
                elif e == 1:
                    pe.wait_ge(s_ls, at(s, 2, 1))
                pe.wait_ge(s_hs, at(s, 2 * E, 2 * e + 2))
                for j in range(NJ):
                    for m in range(2):
                        mm = pe.matmul(bank[:, P * j:P * (j + 1)], hs[:, e % 2, m, P * j:P * (j + 1)],
                                       W["m2"][:, e, m, :], start=(m == 0), stop=(m == 1))
                mm.then_inc(s_y, 1)

            def b_mid_turn(s):
                bk = B.bank
                pe.wait_ge(s_hs, at(s, 2 * E, 2 * E))
                transposes(B, s, 2, 3, bk[2], B.nrm)

            def b_qkv(s):
                bk = B.bank
                pe.wait_ge(B.s_ft, at(s, 3, 2))
                project(B, bk[3], W["bq"][:]).then_inc(B.s_qk, 1)
                project(B, bk[0], W["bk"][:]).then_inc(B.s_qk, 1)
                v_rows(B, bk[1], W["bv"])

            def b_global_scores(s):
                bk = B.bank
                pe.wait_ge(s_gkd, at(s, 1, 1))
                pe.wait_ge(B.s_hi, at(s, 2, 1))
                for j in range(NJ):
                    mm = pe.matmul(bk[2][:, 64 * j:64 * (j + 1)], B.q32[:, P * j:P * (j + 1)],
                                   gkd[:].rearrange("p h g -> p (h g)"), start=True, stop=True)
                pe.matmul(bk[2][0:64, 256:384], gft[:],
                          W["bv"][:], start=True, stop=True).then_inc(s_gvp, 1)

            def b_global(s):
                bk = B.bank
                pe.wait_ge(s_gp, at(s, 1, 1))
                pe.wait_ge(B.s_hl, at(s, 2, 1))
                pass_on(pe, s_passed["pe"])
                for j in range(NJ):
                    mm = pe.transpose(bk[3][0:64, P * j:P * (j + 1)], gp[:, j].rearrange("p h g -> p (h g)"), C["ident"][:])
                mm.then_inc(s_gpp, 1)

            def b_global_out(s):
                bk = B.bank
                pe.wait_ge(s_gpt, at(s, 1, 1))
                pe.wait_ge(s_gv, at(s, 1, 1))
                pe.matmul(bk[3][:], gv[:], gpt[:], start=True, stop=True).then_inc(s_ogp, 1)

            def b_out(s):
                pe.wait_ge(B.s_ot, at(s, 1, 1))
                token_major(B.bank[0], B.ot, W["bo"][:]).then_inc(B.s_ops, 1)

            def b_turn(s):
                bk = B.bank
                transposes(B, s, 3, 3, bk[1], B.nrm)

            def b_last_logits(s):
                bk = B.bank
                pe.wait_ge(B.s_ft, at(s, 3, 3))
                for j in range(NJ):
                    mm = pe.matmul(bk[2][:, E * j:E * (j + 1)], B.ft[:, P * j:P * (j + 1)], W["wg"][:],
                                   start=True, stop=True)
                mm.then_inc(s_lg, 1)

            def b_expert(s, n):
                j, half = n // 2, n % 2
                if n >= 2:
                    pe.wait_ge(s_yce, at(s + 1, 8, n - 1))
                elif n == 1:
                    pe.wait_ge(B.s_h, at(s, 1, 1))
                if n == 0:
                    pe.wait_ge(s_flo, at(s, 2, 2))
                for i, (a, b) in enumerate(PRODUCTS):
                    mm = pe.matmul(B.bank[(3, 0)[n % 2]][:], fpair[:, a, P * j:P * (j + 1)],
                                   pair["we"][:, b, 512 * half:512 * (half + 1)], start=(i == 0), stop=(i == 2))
                mm.then_inc(s_ye, 1)

            def b_gates_turn(s):
                bk = B.bank
                pe.wait_ge(s_cw, at(s, 2, 2))
                for j in range(NJ):
                    mm = pe.transpose(bk[2][0:E, P * j:P * (j + 1)], cw[:, j, :], C["ident"][:])
                mm.then_inc(s_cwp, 1)

            def b_biases(s):
                bk = B.bank
                pe.wait_ge(s_cwt, at(s, 1, 1))
                token_major(bk[1], cwt, W["be"][:]).then_inc(s_bp, 1)

            pe.sem_inc(A.s_pv, NEF)
            pe.sem_inc(B.s_pv, NEF)
            pe.wait_ge(s_w, n_w)
            pe.wait_ge(s_c1, n_c1)

            def exp_step(th, s, f):
                if f < NEF:
                    exp_fill(th, s, f)
                if f >= 1:
                    pv(th, s, f - 1)

            def trip(sr, sb_, sf):
                if sb_ is not None:
                    b_route(sb_)
                if sr is not None:
                    for f in range(TAIL, TAIL + EXP_LEAD - 1):
                        exp_step(A, sr, f)
                if sb_ is not None:
                    b_logits(sb_)
                    moe_up(sb_, 0)
                f = TAIL + EXP_LEAD - 1
                if sr is not None:
                    exp_step(A, sr, f)
                    f += 1
                for e in range(E):
                    if sb_ is not None and e + 1 < E:
                        moe_up(sb_, e + 1)
                    if sr is not None:
                        if e == 2:
                            quotient(A, sr)
                        elif e == 3:
                            quotient_back(A, sr)
                        elif e == 4:
                            a_out(sr)
                        elif e == 6:
                            a_turn(sr)
                        elif e == 7:
                            a_up(sr, (0,))
                    if sb_ is not None:
                        moe_down(sb_, e)
                    while sr is not None and f < exp_until(e):
                        exp_step(A, sr, f)
                        f += 1
                if sr is not None:
                    a_up(sr, (1, 2))
                if sb_ is not None:
                    b_mid_turn(sb_)
                if sb_ is not None:
                    b_qkv(sb_)
                if sf is not None:
                    a_front_turn(sf, sr)
                if sr is not None:
                    a_down(sr)
                if sf is not None:
                    a_project(sf)
                if sb_ is not None:
                    b_global_scores(sb_)
                if sf is not None:
                    if sb_ is None:
                        a_v(sf)
                    if sr is None:
                        pe.wait_ge(s_c, n_c)
                        pe.wait_ge(s_ind, 32)
                        pe.wait_ge(s_init, 3)
                if sb_ is not None:
                    for f in range(NMF):
                        max_fill(B, sb_, f)
                        if f == 3 and sf is not None:
                            a_v(sf)
                        if f == 4:
                            b_global(sb_)
                        elif f == 8:
                            b_global_out(sb_)
                m = 0
                while sf is not None and m < MAX_LEAD:
                    if m == 2 and sb_ is not None:
                        max_rows(B, sb_)
                    max_fill(A, sf, m)
                    m += 1
                if sf is None and sb_ is not None:
                    max_rows(B, sb_)
                for f in range(NEF + 1):
                    if sb_ is not None:
                        exp_step(B, sb_, f)
                    while sf is not None and m < max_until(f):
                        max_fill(A, sf, m)
                        m += 1
                    if sf is not None and f == MAX_ROWS:
                        max_rows(A, sf)
                for n in range(TAIL):
                    if sf is not None:
                        exp_step(A, sf, n)
                    if sb_ is not None:
                        if n == 0:
                            quotient(B, sb_)
                        elif n == 2:
                            quotient_back(B, sb_)
                        elif n == 3:
                            b_out(sb_)
                        elif n == 7:
                            b_turn(sb_)
                        elif n == 8:
                            b_last_logits(sb_)
                        if expert_in_tail(n) is not None:
                            b_expert(sb_, expert_in_tail(n))
                        if n == TAIL - 2:
                            b_gates_turn(sb_)
                        elif n == TAIL - 1:
                            b_biases(sb_)
            trip(None, None, 0)
            pe.wait_ge(s_w2, n_w2)
            trip(0, None, 1)
            pe.wait_ge(s_wlo, sum(whole[n].shape[1] // T for n in SPLIT_W))
            with pe.Fori(1, SEQS - 1) as i:
                trip(i, i - 1, i + 1)
            trip(SEQS - 1, SEQS - 2, None)
            trip(None, SEQS - 1, None)

        @block.scalar
        def _(act):
            for n in FIRST_C:
                act.dma_start(C[n][:], c[n]).then_inc(s_c1, 16)
            for n, a in c.items():
                if n not in FIRST_C:
                    act.dma_start(C[n][:], a).then_inc(s_c, 16)
            act.wait_ge(s_w, n_w)

            def copy(o, i):
                return act.activation(o, i, ACT.Copy)

            def v_place(th, s, bank):
                act.wait_ge(th.s_vps, at(s, 1, 1))
                act.wait_ge(th.s_pv, at(s, NEF, NEF))
                for b in range(4):
                    src = bank[KB * b:KB * (b + 1), :].rearrange("p (j g h d) -> p j g h d", j=NJ, g=HG, h=4)
                    for h in range(4):
                        ins = copy(th.vb[KB * h:KB * (h + 1), b:NB:4, :, 0, h, :], src[:, :, :, h, :])
                ins.then_inc(th.s_vb, 1)

            def k_blocks(th, s, groups, done):
                act.wait_ge(th.s_krep, at(s, 48, 48))
                for g in groups:
                    for h in range(4):
                        ins = act.activation(th.kd[0:PAIR, g, PADB:, h, :],
                                             th.kr[0:PAIR, g, :].rearrange("p (b k) -> p b k", k=KB),
                                             ACT.Copy, scale=C["own_head"][0:PAIR, h:h + 1])
                    ins.then_inc(done, 1)

            def max_rows(th, s):
                act.wait_ge(th.s_mtp, at(s, 1, 1))
                copy(th.mt[:], th.bank[2][0:32, 0:T // 2].bitcast(F16)).then_inc(th.s_mt, 1)

            def exps(th, s, f):
                act.wait_ge(th.s_sfill, at(s, NEF, f + 1))
                if f >= 3:
                    act.wait_ge(th.s_pv, at(s + 1, NEF, f - 2))
                n = sum(t[3] for t in EXP_FILLS[f])
                act.activation(th.p[:, f % 3, 0:n], th.bank[f % 2][:, 0:n], ACT.Exp, scale=SCALE).then_inc(th.s_exp, 1)

            def sums(th, s):
                act.wait_ge(th.s_pv, at(s + 1, NEF, NEF))
                copy(th.nd[:, 0], th.bank[2][:])
                copy(th.nd[:, 1], th.bank[3][:]).then_inc(th.s_nd, 1)

            def a_attended(s):
                act.wait_ge(A.s_obt, at(s, 1, 1))
                copy(A.ot[:], A.bank[2][:]).then_inc(A.s_ot, 1)

            def a_features(s, k, bank):
                act.wait_ge(A.s_tps, at(s, 2, k))
                act.activation(A.ft[:], bank[:], ACT.Identity, scale=W["ln"][:, 2 * k - 2:2 * k - 1],
                               bias=W["ln"][:, 2 * k - 1:2 * k]).then_inc(A.s_ft, 1)

            def b_features(s, k, bank):
                act.wait_ge(B.s_tps, at(s, 3, k))
                if k == 2:
                    copy(gft[:].rearrange("p (h g) -> p h g", g=NG),
                         bank[:, 0:T:STRIDE].unsqueeze(1).broadcast_to([D, HEADS, NG]))
                copy(B.ft[:], bank[:]).then_inc(B.s_ft, 1)
                if k != 2:
                    copy(fpair[:, 0], bank[:]).then_inc(s_fhi, 1)

            def a_split(s):
                for n, src in ((0, A.q32), (1, A.k32)):
                    act.wait_ge(s_q32, at(s, 2, n + 1))
                    copy(A.hl[:, 2 * n], src[:]).then_inc(A.s_hi, 1)

            def b_split(s):
                act.wait_ge(B.s_qk, at(s, 2, 2))
                copy(B.k32[:], B.bank[0][:, 0:T:STRIDE]).then_inc(s_k32, 1)
                copy(B.q32[:], B.bank[3][:])
                copy(B.hl[:, 0], B.bank[3][:]).then_inc(B.s_hi, 1)
                copy(B.hl[:, 2], B.bank[0][:]).then_inc(B.s_hi, 1)

            def a_tanh(s, m):
                act.wait_ge(s_up, at(s, 6, 2 * m + 1))
                if m == 2:
                    act.wait_ge(s_g, at(s, 3, 1))
                act.activation(tanh_t[0:HT[m], m % 2], A.bank[2 if m % 2 == 0 else 0][0:HT[m], :], ACT.Tanh,
                               scale=0.5).then_inc(s_th, 1)

            def moe_tanh(s, e):
                for m in range(2):
                    act.wait_ge(s_mup, at(s, 2 * E, 2 * e + m + 1))
                    if e >= 1:
                        act.wait_ge(s_hs, at(s, 2 * E, 2 * e + m - 1))
                    act.activation(mth[:, m], B.bank[2 + m][:], ACT.Tanh, scale=0.5 / WSCALE).then_inc(s_mth, 1)

            def gate_exp(s, k):
                act.wait_ge(s_ls, at(s, 2, k))
                act.activation(lg[:, 1], lg[:, 0], ACT.Exp).then_inc(s_le, 1)

            def trip(sr, sb_, sf):
                if sb_ is not None:
                    b_features(sb_, 1, B.bank[0])
                if sr is not None:
                    for f in range(TAIL, TAIL + EXP_LEAD - 1):
                        exps(A, sr, f)
                if sb_ is not None:
                    moe_tanh(sb_, 0)
                    gate_exp(sb_, 1)
                f = TAIL + EXP_LEAD - 1
                if sr is not None:
                    exps(A, sr, f)
                    f += 1
                for e in range(E):
                    if sb_ is not None and e + 1 < E:
                        moe_tanh(sb_, e + 1)
                    if sr is not None:
                        if e == 3:
                            a_attended(sr)
                        elif e == 6:
                            a_features(sr, 2, A.bank[1])
                        elif e == 7:
                            a_tanh(sr, 0)
                        while f < min(NEF, exp_until(e)):
                            exps(A, sr, f)
                            f += 1
                        if e == EXP_E - 1:
                            sums(A, sr)
                if sr is not None:
                    a_tanh(sr, 1)
                    a_tanh(sr, 2)
                if sb_ is not None:
                    b_features(sb_, 2, B.bank[2])
                if sb_ is not None:
                    b_split(sb_)
                if sf is not None:
                    a_features(sf, 1, A.bank[1])
                if sb_ is not None:
                    v_place(B, sb_, B.bank[1])
                    act.wait_ge(s_gsh, at(sb_, 1, 1))
                    act.activation(gp[:], gs[:], ACT.Exp, scale=SCALE).then_inc(s_ge, 1)
                if sf is not None:
                    a_split(sf)
                    if sr is None:
                        act.wait_ge(s_init, 3)
                if sb_ is not None:
                    k_blocks(B, sb_, (2, 3), B.s_kd1)
                if sf is not None:
                    v_place(A, sf, A.bank[2])
                if sb_ is not None:
                    act.wait_ge(s_gpp, at(sb_, 1, 1))
                    copy(gpt[:], B.bank[3][0:64, :]).then_inc(s_gpt, 1)
                    act.wait_ge(s_ogp, at(sb_, 1, 1))
                    copy(ogt[:], B.bank[3][:]).then_inc(s_ogt, 1)
                if sf is not None:
                    if sr is None:
                        act.wait_ge(s_c, n_c)
                    k_blocks(A, sf, (0, 1), A.s_kd0)
                if sb_ is not None:
                    max_rows(B, sb_)
                for f in range(NEF):
                    if sb_ is not None:
                        exps(B, sb_, f)
                    if sf is not None and f == MAX_ROWS:
                        max_rows(A, sf)
                for n in range(TAIL):
                    if sb_ is not None:
                        if n == 0:
                            sums(B, sb_)
                        elif n == 8:
                            b_features(sb_, 3, B.bank[1])
                        elif n == 9:
                            gate_exp(sb_, 2)
                        elif n == TAIL - 1:
                            act.wait_ge(s_cwp, at(sb_, 1, 1))
                            copy(cwt, B.bank[2][0:E, :]).then_inc(s_cwt, 1)
                    if sf is not None:
                        exps(A, sf, n)
            trip(None, None, 0)
            act.wait_ge(s_w2, n_w2)
            for n in SPLIT_W:
                for at_ in range(0, whole[n].shape[1], T):
                    act.activation(pair[n][:, 0, at_:at_ + T], whole[n][:, at_:at_ + T], ACT.Copy,
                                   scale=WSCALE).then_inc(s_whi, 1)
            trip(0, None, 1)
            with act.Fori(1, SEQS - 1) as i:
                trip(i, i - 1, i + 1)
            trip(SEQS - 1, SEQS - 2, None)
            trip(None, SEQS - 1, None)

        @block.vector
        def _(dve):
            dve.sem_inc(s_xfree, 1)
            dve.sem_inc(s_x1, 1)
            dve.sem_inc(s_yce, 8)
            dve.sem_inc(s_x3b, 1)
            for th in (A, B):
                ins = dve.memset(th.kd[0:PAIR, :, 0:PADB].rearrange("p g b h k -> p g (b h k)").bitcast(F32), 0.0)
            ins.then_inc(s_init, 1)
            dve.memset(A.vb[:].rearrange("p k g a h d -> p (k g a h d)"), 0.0).then_inc(s_vclear, 1)
            da, db = Steps(dve, A.s_dve, DVE_A), Steps(dve, B.s_dve, DVE_B)
            df, dn = Steps(dve, s_dvef, DVE_F), Steps(dve, s_dven, DVE_N)

            def stats(th, d, src):
                for j in range(NJ):
                    d.mark(dve.bn_stats(th.st[:, j], src[:, j]))
                d.wait()
                pass_on(dve, s_passed["dve"])
                for j in range(NJ):
                    ins = dve.bn_aggr(th.mv[:, j], th.st[:, j])
                ins.then_inc(th.s_mv, 1)

            def norm(th, dst, src, r, done=None):
                for j in range(NJ):
                    ins = dve.tensor_scalar(dst[:, j], src[:, j], th.mv[:, j, 0:1], th.rs[:, r, j:j + 1],
                                            ALU.subtract, ALU.mult)
                    if done is not None:
                        ins.then_inc(done, 1)
                return ins

            def maxima(th, s, f):
                dve.wait_ge(th.s_mfill, at(s, NMF, f + 1))
                n = len(MAX_FILLS[f])
                dve.tensor_reduce(th.m[:, PB * f:PB * f + n],
                                  th.bank[f % 2][:, 0:WIN * n].rearrange("p (a b) -> p a b", a=n),
                                  AX.X, ALU.max).then_inc(th.s_mdone, 1)

            def max_split(th, d, s):
                dve.wait_ge(th.s_mdone, at(s, NMF, NMF))
                m = th.m[:].rearrange("p (j g h) -> p j g h", j=NJ, g=HG)
                d.link(dve.tensor_scalar(th.mhl[:, :, :, 0, :], m, -1.0 / MSCALE, None, ALU.mult))
                dve.scalar_tensor_tensor(th.mhl[:, :, :, 1, :].rearrange("p j g h -> p (j g) h"),
                                         m.rearrange("p j g h -> p (j g) h"), -1.0 / MSCALE,
                                         th.mhl[:, :, :, 0, :].rearrange("p j g h -> p (j g) h"),
                                         ALU.mult, ALU.subtract).then_inc(th.s_mhl, 1)

            def divide(th, d, s):
                dve.wait_ge(th.s_ndt, at(s, 1, 1))
                for half in range(2):
                    den = th.bank[half][:].rearrange("p (j g a h d) -> p j g a h d", j=NJ, g=2, a=2, h=4)
                    for g in range(2):
                        d.mark(dve.reciprocal(th.rd[:, half, :, g, :], den[:, :, g, 1, :, 0]))
                d.wait()
                for half in range(2):
                    num = th.bank[half][:].rearrange("p (j g a h d) -> p j g a h d", j=NJ, g=2, a=2, h=4)
                    for g in range(2):
                        ins = dve.tensor_tensor(th.ob[:, :, 2 * half + g], num[:, :, g, 0],
                                                th.rd[:, half, :, g, :].unsqueeze(3).broadcast_to([P, NJ, 4, HD]), ALU.mult)
                ins.then_inc(th.s_ob, 1)

            def k_blocks(th, s, groups, done):
                dve.wait_ge(th.s_krep, at(s, 48, 48))
                pass_on(dve, s_passed["dve"])
                for g in groups:
                    for h in range(4):
                        ins = dve.tensor_scalar(th.kd[0:PAIR, g, PADB:, h, :],
                                                th.kr[0:PAIR, g, :].rearrange("p (b k) -> p b k", k=KB),
                                                C["own_head"][0:PAIR, h:h + 1], None, ALU.mult)
                    ins.then_inc(done, 1)

            def feature_rest(s, k, bank):
                dve.wait_ge(s_fhi, at(s, 2, k))
                dve.tensor_tensor(fpair[:, 1], bank[:], fpair[:, 0], ALU.subtract).then_inc(s_flo, 1)

            def shifted(d, s, k, bank):
                dve.wait_ge(s_lg, at(s, 2, k))
                l = bank[:, 0:NJ * E].rearrange("p (j e) -> p j e", j=NJ)
                sh = [P, NJ, E]
                if k == 2:
                    d.link(dve.tensor_tensor(lg[:, 8], l, W["b_g"][:].unsqueeze(1).broadcast_to(sh), ALU.add))
                    l = lg[:, 8]
                d.link(dve.tensor_reduce(red[:, 0], l, AX.X, ALU.max))
                dve.tensor_tensor(lg[:, 0], l, red[:, 0].unsqueeze(2).broadcast_to(sh), ALU.subtract).then_inc(s_ls, 1)

            def top2(d, s, k, eps, factor, between=None):
                sh = [P, NJ, E]
                rd = lambda n: red[:, n].unsqueeze(2).broadcast_to(sh)
                dve.wait_ge(s_le, at(s, 2, k))
                d.link(dve.tensor_reduce(red[:, 1], lg[:, 1], AX.X, ALU.add))
                d.link(dve.reciprocal(red[:, 2], red[:, 1]))
                d.link(dve.tensor_tensor(lg[:, 2], lg[:, 1], rd(2), ALU.mult))
                order = C["order"][:].unsqueeze(1).broadcast_to(sh)
                d.link(dve.tensor_reduce(red[:, 3], lg[:, 2], AX.X, ALU.max))
                d.link(dve.tensor_tensor(lg[:, 3], lg[:, 2], rd(3), ALU.is_equal))
                d.link(dve.tensor_tensor(lg[:, 4], lg[:, 3], order, ALU.mult))
                d.link(dve.tensor_reduce(red[:, 4], lg[:, 4], AX.X, ALU.max))
                d.link(dve.tensor_tensor(lg[:, 5], order, rd(4), ALU.is_equal))
                if between is not None:
                    between()
                d.link(dve.scalar_tensor_tensor(lg[:, 6], lg[:, 5], -4.0, lg[:, 2], ALU.mult, ALU.add))
                d.link(dve.tensor_reduce(red[:, 5], lg[:, 6], AX.X, ALU.max))
                d.mark(dve.tensor_tensor(red[:, 7], red[:, 3], red[:, 5], ALU.add))
                d.link(dve.tensor_tensor(lg[:, 7], lg[:, 6], rd(5), ALU.is_equal))
                if eps:
                    d.mark(dve.tensor_scalar(red[:, 7], red[:, 7], eps, None, ALU.max))
                d.link(dve.tensor_tensor(lg[:, 3], lg[:, 7], order, ALU.mult))
                d.mark(dve.reciprocal(red[:, 0], red[:, 7]))
                d.link(dve.tensor_reduce(red[:, 6], lg[:, 3], AX.X, ALU.max))
                d.mark(dve.scalar_tensor_tensor(lg[:, 9], lg[:, 2], factor, rd(0), ALU.mult, ALU.mult))
                d.link(dve.tensor_tensor(lg[:, 4], order, rd(6), ALU.is_equal))
                d.link(dve.tensor_tensor(lg[:, 6], lg[:, 4], lg[:, 5], ALU.add))
                dve.tensor_tensor(cw[:], lg[:, 9], lg[:, 6], ALU.mult).then_inc(s_cw, 1)

            def a_stats(s):
                dve.wait_ge(s_xin, at(s, 16, 16))
                stats(A, df, xin)

            def a_norm(s, last):
                dve.wait_ge(A.s_rs, at(s, 2, 1))
                if last is not None:
                    dve.wait_ge(A.s_tps, at(last, 2, 2))
                norm(A, A.nrm, xin, 1, A.s_nrm)

            def a_base(s):
                norm(A, a0, xin, 0).then_inc(s_xfree, 1)

            def a_rope(s):
                for n, (bank, tab) in enumerate(((2, "cos"), (3, "sin"), (1, "cos"), (0, "sin"))):
                    dve.wait_ge(A.s_qk, at(s, 4, n + 1))
                    dve.tensor_tensor(rope_t[:, n], A.bank[bank][:], C[tab][:], ALU.mult).then_inc(s_rope, 1)

            def a_resid(s):
                dve.wait_ge(A.s_ops, at(s, 1, 1))
                da.link(dve.tensor_tensor(h0[:].rearrange("p j d -> p (j d)"), A.bank[0][:],
                                          a0[:].rearrange("p j d -> p (j d)"), ALU.add))
                stats(A, da, h0)

            def a_norm2(s):
                dve.wait_ge(A.s_rs, at(s, 2, 2))
                norm(A, A.nrm, h0, 0, A.s_nrm)

            def a_gate(s, ms):
                for m in ms:
                    mt = HT[m]
                    dve.wait_ge(s_th, at(s, 3, m + 1))
                    b1, b3 = (A.bank[2], A.bank[3]) if m % 2 == 0 else (A.bank[0], A.bank[1])
                    da.link(dve.scalar_tensor_tensor(sg[0:mt, m % 2], tanh_t[0:mt, m % 2], 1.0, b1[0:mt, :],
                                                     ALU.add, ALU.mult))
                    dve.wait_ge(s_up, at(s, 6, 2 * m + 2))
                    dve.scalar_tensor_tensor(gt[0:mt, m], sg[0:mt, m % 2], 0.5, b3[0:mt, :],
                                             ALU.mult, ALU.mult).then_inc(s_g, 1)

            def a_end(s):
                dve.wait_ge(s_dn, at(s, 1, 1))
                dve.wait_ge(s_hh, at(s, 1, 1))
                dve.tensor_tensor(x1[:].rearrange("p j d -> p (j d)"), A.bank[0][:],
                                  xh[:].rearrange("p j d -> p (j d)"), ALU.add).then_inc(s_x1, 1)
                da.end()

            def b_stats(s, d, src, ready, v):
                dve.wait_ge(ready, v)
                stats(B, d, src)

            def b_norm(s, k, src):
                dve.wait_ge(B.s_rs, at(s, 3, k))
                norm(B, B.nrm, src, 0, B.s_nrm)

            def moe_gate(s, e):
                if e == 0:
                    dve.wait_ge(s_fold, at(s, NJ, NJ))
                for m in range(2):
                    dve.wait_ge(s_mth, at(s, 2 * E, 2 * e + m + 1))
                    dve.scalar_tensor_tensor(hs[:, e % 2, m], mth[:, m], 1.0, B.bank[2 + m][:],
                                             ALU.add, ALU.mult).then_inc(s_hs, 1)

            def moe_scale(s, e):
                if e == 0:
                    dve.wait_ge(s_cw, at(s, 2, 1))
                dve.wait_ge(s_y, at(s, E, e + 1))
                if e == 0:
                    dve.wait_ge(s_xo, at(s, 1, 1))
                else:
                    dve.wait_ge(s_acc, at(s, E, e))
                for j in range(NJ):
                    ins = dve.scalar_tensor_tensor(acc[:, j], B.bank[e % 2][:, P * j:P * (j + 1)], cw[:, j, e:e + 1],
                                                   (acc if e else x1)[:, j], ALU.mult, ALU.add)
                ins.then_inc(s_acc, 1)

            def b_pairs(s):
                dve.wait_ge(s_k32, at(s, 1, 1))
                dve.tensor_tensor(gkd[:], B.k32[:].unsqueeze(1).broadcast_to([D, HEADS, NG]),
                                  C["head_mask"][:].unsqueeze(2).broadcast_to([D, HEADS, NG]),
                                  ALU.mult).then_inc(s_gkd, 1)
                for n in range(2):
                    dve.wait_ge(B.s_hi, at(s, 2, n + 1))
                    dve.tensor_tensor(B.hl[:, 2 * n + 1], B.bank[(3, 0)[n]][:], B.hl[:, 2 * n],
                                      ALU.subtract).then_inc(B.s_hl, 1)

            def b_global(s):
                dve.wait_ge(s_gvp, at(s, 1, 1))
                g4 = B.bank[2][:, 0:256].rearrange("p (a g) -> p a g", g=NG)
                v3 = lambda t: t[:].rearrange("p j h g -> p (j h) g")
                rd = lambda n: gred[:, n].rearrange("p j h -> p (j h)")
                bc = lambda n: rd(n).unsqueeze(2).broadcast_to([P, NJ * HEADS, NG])
                db.link(dve.tensor_reduce(rd(0), g4, AX.X, ALU.max))
                dve.tensor_tensor(v3(gs), g4, bc(0), ALU.subtract).then_inc(s_gsh, 1)
                dve.tensor_tensor(gv[:], B.bank[2][0:64, 256:384], C["gv_mask"][:], ALU.mult).then_inc(s_gv, 1)

            def b_global_probs(s):
                v3 = lambda t: t[:].rearrange("p j h g -> p (j h) g")
                rd = lambda n: gred[:, n].rearrange("p j h -> p (j h)")
                bc = lambda n: rd(n).unsqueeze(2).broadcast_to([P, NJ * HEADS, NG])
                dve.wait_ge(s_ge, at(s, 1, 1))
                db.link(dve.tensor_reduce(rd(1), v3(gp), AX.X, ALU.add))
                db.link(dve.reciprocal(rd(2), rd(1)))
                dve.tensor_tensor(v3(gp), v3(gp), bc(2), ALU.mult).then_inc(s_gp, 1)

            def b_attended(s):
                dve.wait_ge(B.s_obt, at(s, 1, 1))
                dve.wait_ge(s_ogt, at(s, 1, 1))
                dve.tensor_tensor(B.ot[:], B.bank[2][:], ogt[:], ALU.add).then_inc(B.s_ot, 1)

            def b_resid(s):
                dve.wait_ge(B.s_ops, at(s, 1, 1))
                dve.wait_ge(s_x2b, at(s, 1, 1))
                dve.tensor_tensor(x3[:].rearrange("p j d -> p (j d)"), B.bank[0][:],
                                  x2b[:].rearrange("p j d -> p (j d)"), ALU.add).then_inc(B.s_h, 1)

            def b_scale(s, n):
                j, half = n // 2, n % 2
                if n == 0:
                    dve.wait_ge(s_cw, at(s, 2, 2))
                dve.wait_ge(s_ye, at(s, 8, n + 1))
                if n >= 4:
                    dve.wait_ge(s_fold, at(s + 1, NJ, j - 1))
                dve.scalar_tensor_tensor(yce[:, j % 2, half].rearrange("p (e d) -> p e d", e=4),
                                         B.bank[(3, 0)[n % 2]][:].rearrange("p (e d) -> p e d", e=4), 1 / WSCALE,
                                         cw[:, j, 4 * half:4 * half + 4].unsqueeze(2).broadcast_to([P, 4, D]),
                                         ALU.mult, ALU.mult).then_inc(s_yce, 1)

            def b_biases(s):
                dve.wait_ge(s_bp, at(s, 1, 1))
                dve.tensor_tensor(x3b[:].rearrange("p j d -> p (j d)"), B.bank[1][:],
                                  x3[:].rearrange("p j d -> p (j d)"), ALU.add).then_inc(s_x3b, 1)

            def trip(sr, sb_, sf):
                if sb_ is not None:
                    db.begin(sb_)
                    feature_rest(sb_, 1, B.bank[0])
                    shifted(db, sb_, 1, B.bank[1])
                    moe_gate(sb_, 0)
                    moe_gate(sb_, 1)
                    top2(db, sb_, 1, 1e-9, 0.5 / WSCALE, between=lambda: moe_gate(sb_, 2))
                for e in range(E):
                    if sb_ is not None and 3 <= e + 1 < E:
                        moe_gate(sb_, e + 1)
                    if sr is not None:
                        if e == 2:
                            da.begin(sr)
                            divide(A, da, sr)
                        elif e == 4:
                            a_resid(sr)
                        elif e == 5:
                            a_norm2(sr)
                        elif e == 7:
                            a_gate(sr, (0,))
                    if sf is not None:
                        if e == 6:
                            df.begin(sf)
                            a_stats(sf)
                        elif e == 7:
                            a_norm(sf, sr)
                    if sb_ is not None:
                        moe_scale(sb_, e)
                if sb_ is not None:
                    b_stats(sb_, db, acc, s_acc, at(sb_, E, E))
                if sb_ is not None:
                    b_norm(sb_, 2, acc)
                if sr is not None:
                    a_gate(sr, (1,))
                if sr is not None:
                    a_gate(sr, (2,))
                if sb_ is not None:
                    b_pairs(sb_)
                if sf is not None:
                    a_base(sf)
                if sr is not None:
                    a_end(sr)
                if sf is not None:
                    if sr is None:
                        dve.wait_ge(s_c, n_c)
                    a_rope(sf)
                if sb_ is not None:
                    b_global(sb_)
                    k_blocks(B, sb_, (0, 1), B.s_kd0)
                    b_global_probs(sb_)
                    for f in range(NMF):
                        maxima(B, sb_, f)
                    max_split(B, db, sb_)
                if sf is not None:
                    for f in range(NMF):
                        maxima(A, sf, f)
                    max_split(A, df, sf)
                    df.end()
                for n in range(TAIL):
                    if sb_ is not None:
                        if n == 0:
                            divide(B, db, sb_)
                        elif n == 2:
                            b_attended(sb_)
                        elif n == 3:
                            b_resid(sb_)
                            b_stats(sb_, db, x3, B.s_h, at(sb_, 1, 1))
                        elif n == 4:
                            b_norm(sb_, 3, x3)
                        elif n == 8:
                            feature_rest(sb_, 2, B.bank[1])
                            shifted(db, sb_, 2, B.bank[2])
                            top2(db, sb_, 2, None, 1.0)
                        if expert_in_tail(n) is not None:
                            b_scale(sb_, expert_in_tail(n))
                    if sr is not None:
                        if n == 5:
                            dn.begin(sr)
                            b_stats(sr, dn, x1, s_x1, at(sr + 1, 1, 1))
                            dn.end()
                        elif n == 10:
                            b_norm(sr, 1, x1)
                if sb_ is not None:
                    b_biases(sb_)
                    db.end()
            trip(None, None, 0)
            done = 0
            for n in SPLIT_W:
                for at_ in range(0, whole[n].shape[1], T):
                    done += 1
                    dve.wait_ge(s_whi, done)
                    dve.scalar_tensor_tensor(pair[n][:, 1, at_:at_ + T], whole[n][:, at_:at_ + T], WSCALE,
                                             pair[n][:, 0, at_:at_ + T], ALU.mult, ALU.subtract).then_inc(s_wlo, 1)
            trip(0, None, 1)
            with dve.Fori(1, SEQS - 1) as i:
                trip(i, i - 1, i + 1)
            trip(SEQS - 1, SEQS - 2, None)
            trip(None, SEQS - 1, None)

        @block.gpsimd
        def _(pool):
            pool.sem_inc(s_xfree, 1)
            pool.sem_inc(s_xo, 1)
            pool.sem_inc(s_out, 16)
            pool.sem_inc(s_fold, NJ)
            pa, pb = Steps(pool, A.s_pool, POOL_A), Steps(pool, B.s_pool, POOL_B)
            pf, pn = Steps(pool, s_poolf, POOL_F), Steps(pool, s_pooln, POOL_N)
            def copy(o, i):
                return pool.tensor_scalar(o, i, 1.0, 1.0, ALU.mult, ALU.mult)

            def ones(th):
                copy(th.vb[:].rearrange("p k g a h d -> p (k g) a (h d)")[:, :, 1, :],
                     C["ones_bd"][:].unsqueeze(1).broadcast_to([P, NB * HG, KB])).then_inc(s_init, 1)

            pool.wait_ge(s_c1, n_c1)

            def rstd(th, p, s, k, per, both):
                pool.wait_ge(th.s_mv, at(s, per, k))
                pass_on(pool, s_passed["pool"])
                n = 2 if both else 1
                var = th.mv[:, :, 1]
                if both:
                    p.mark(pool.tensor_scalar(th.ve[:, 1], var, 1.0 + EPS, EPS * EPS, ALU.mult, ALU.add))
                p.link(pool.tensor_scalar(th.ve[:, 0], var, EPS, 1.0, ALU.add, ALU.mult))
                pool.tensor_tensor(th.rs[:, 0:n], th.ve[:, 0:n], C["half"][:, 0:n], ALU.pow).then_inc(th.s_rs, 1)

            def a_sum(s):
                for n, dst in ((0, A.q32), (1, A.k32)):
                    pool.wait_ge(s_rope, at(s, 4, 2 * n + 2))
                    pool.tensor_tensor(dst[:], rope_t[:, 2 * n], rope_t[:, 2 * n + 1], ALU.add).then_inc(s_q32, 1)
                for n, src in ((0, A.q32), (1, A.k32)):
                    pool.wait_ge(A.s_hi, at(s, 2, n + 1))
                    pool.tensor_tensor(A.hl[:, 2 * n + 1], src[:], A.hl[:, 2 * n], ALU.subtract).then_inc(A.s_hl, 1)

            def fold_experts(s):
                for j in range(NJ):
                    pool.wait_ge(s_yce, at(s + 1, 8, 2 * j + 2))
                    f = fold[:, 0]
                    pb.link(pool.tensor_tensor(f, yce[:, j % 2, 0], yce[:, j % 2, 1], ALU.add))
                    pb.link(pool.tensor_tensor(fold[:, 1, 0:2 * D], f[:, 0:2 * D], f[:, 2 * D:4 * D], ALU.add))
                    pool.tensor_tensor(fsum[:, j], fold[:, 1, 0:D], fold[:, 1, D:2 * D], ALU.add).then_inc(s_fold, 1)

            def k_blocks(th, s, groups, done):
                pool.wait_ge(th.s_krep, at(s, 48, 48))
                pass_on(pool, s_passed["pool"])
                for g in groups:
                    for h in range(4):
                        ins = pool.tensor_scalar(th.kd[0:PAIR, g, PADB:, h, :],
                                                 th.kr[0:PAIR, g, :].rearrange("p (b k) -> p b k", k=KB),
                                                 C["own_head"][0:PAIR, h:h + 1], 1.0, ALU.mult, ALU.mult)
                    ins.then_inc(done, 1)

            def trip(sr, sb_, sf):
                if sb_ is not None:
                    pb.begin(sb_)
                if sr is not None:
                    pa.begin(sr)
                    rstd(A, pa, sr, 2, 2, False)
                    pool.tensor_tensor(xh[:], xres[:], h0[:], ALU.add).then_inc(s_hh, 1)
                    pa.end()
                if sf is not None:
                    pf.begin(sf)
                    rstd(A, pf, sf, 1, 2, True)
                if sb_ is not None:
                    rstd(B, pb, sb_, 2, 3, False)
                if sb_ is not None:
                    pool.wait_ge(s_acc, at(sb_, E, E))
                    pool.tensor_tensor(x2b[:], acc[:], W["b_out"][:].unsqueeze(1).broadcast_to([P, NJ, D]),
                                       ALU.add).then_inc(s_x2b, 1)
                if sf is not None:
                    copy(xres[:].rearrange("p j d -> p (j d)"), xin[:].rearrange("p j d -> p (j d)")).then_inc(s_xfree, 1)
                    if sr is None:
                        pool.memset(B.vb[:].rearrange("p k g a h d -> p (k g a h d)"), 0.0).then_inc(s_vclear, 1)
                        pool.wait_ge(s_c, n_c)
                        pool.wait_ge(s_vclear, 2)
                    a_sum(sf)
                    if sr is None:
                        ones(A)
                        ones(B)
                    k_blocks(A, sf, (2, 3), A.s_kd1)
                    pf.end()
                if sb_ is not None:
                    rstd(B, pb, sb_, 3, 3, False)
                if sr is not None:
                    pn.begin(sr)
                    rstd(B, pn, sr, 1, 3, False)
                    pn.end()
                if sb_ is not None:
                    fold_experts(sb_)
                    pool.wait_ge(s_fold, at(sb_ + 1, NJ, NJ))
                    pool.wait_ge(s_x3b, at(sb_ + 1, 1, 1))
                    pool.wait_ge(s_out, at(sb_, 16, 16))
                    pool.tensor_tensor(xout[:], fsum[:], x3b[:], ALU.add).then_inc(s_xo, 1)
                    pb.end()
            trip(None, None, 0)
            pool.wait_ge(s_w2, n_w2)
            trip(0, None, 1)
            pool.wait_ge(s_wlo, sum(whole[n].shape[1] // T for n in SPLIT_W))
            with pool.Fori(1, SEQS - 1) as i:
                trip(i, i - 1, i + 1)
            trip(SEQS - 1, SEQS - 2, None)
            trip(None, SEQS - 1, None)


def _constants():

    f32, f16, bf16 = np.float32, np.float16, np.dtype("bfloat16")
    p = np.arange(P)
    q, j = p % KB, p // KB
    w = np.arange(WIN)
    own = np.where((w[None] >= q[:, None]) & (w[None] <= q[:, None] + WINDOW), 0.0, BIG)
    first = np.where(KB * (j[:, None] - 4) + w[None] >= 0, own, BIG)
    edges = own.reshape(P, 5, KB)[:, [0, 4]]
    freqs = (1.0 / np.power(f32(10000.0), np.arange(0, HD, 2, dtype=f32) / f32(HD))).astype(f32)
    ang = np.outer(freqs, np.arange(T, dtype=f32)).astype(f32)
    d, d_head = p % HD, p // HD % 4
    sign = np.where(d % 2 == 0, -1.0, 1.0)[:, None]
    g = np.arange(HEADS * NG) // NG
    ind = np.zeros((8, HG * (PADB + NB), 4, KB), f16)
    for r in range(8):
        ind[r, :, r % 4] = MSCALE
    ind = ind.reshape(8, -1)
    rep = lambda a, n: np.repeat(a[:, None], n, 1)
    c = {
        "ident": np.eye(P, dtype=f32),
        "identb": np.eye(P).astype(bf16),
        "identh": np.eye(P, dtype=f16),
        "mask_first": rep(first, PB).astype(bf16),
        "mask_q": rep(edges, PB).astype(bf16),
        "mask_tail": rep(edges[:, 0], 4).astype(bf16),
        "ones_bd": (j[:, None] == (p[None, :KB] // HD)).astype(f32),
        "cos": np.cos(ang[d // 2].astype(np.float64)).astype(f32),
        "sin": (np.sin(ang[d // 2].astype(np.float64)) * sign).astype(f32),
        "head_mask": (p[:, None] // HD == np.arange(HEADS)[None]).astype(f32),
        "gv_mask": (g[:, None] == p[None] // HD).astype(f32),
        "half": np.full((P, 2, NJ), -0.5, f32),
        "own_head": (d_head[:, None] == np.arange(4)[None]).astype(f32),
        "order": np.broadcast_to(E - np.arange(E, dtype=f32), (P, E)),
    }
    return {k: np.ascontiguousarray(v) for k, v in c.items()}, ind


def kernel(**inputs):
    import concourse.bacc as bacc
    from concourse.bass_utils import run_bass_kernel_spmd

    i = {k: np.asarray(v) for k, v in inputs.items()}
    swap = np.arange(D) ^ 1
    w2 = np.zeros((3 * P, D), i["L0_attn_w2"].dtype)
    w2[:HID] = i["L0_attn_w2"]
    qkv = i["L1_attn_w_qkv"].T
    w = {
        "front": np.concatenate([i["L0_attn_wq"], i["L0_attn_wq"][:, swap],
                                 i["L0_attn_wk"], i["L0_attn_wk"][:, swap], i["L0_attn_wv"],
                                 np.stack([i["L0_attn_ln1_g"], i["L0_attn_ln1_b"],
                                           i["L0_attn_ln2_g"], i["L0_attn_ln2_b"]], 1)], 1),
        "wo": i["L0_attn_wo"],
        "w1": i["L0_attn_w1"], "w3": i["L0_attn_w3"], "w2": w2.reshape(3, P, D).transpose(1, 0, 2),
        "router": i["L0_ffn_router_w"],
        "m1": i["L0_ffn_w1"].transpose(1, 0, 2).reshape(D, E * FE),
        "m2": i["L0_ffn_w2"].reshape(E, 2, P, D).transpose(2, 0, 1, 3),
        "bq": qkv[:, :D], "bk": qkv[:, D:2 * D], "bv": qkv[:, 2 * D:],
        "bo": i["L1_attn_w_out"].T, "b_out": np.broadcast_to(i["L1_attn_b_out"], (P, D)),
        "wg": i["L1_ffn_Wg"], "b_g": np.broadcast_to(i["L1_ffn_bg"], (P, E)),
        "we": i["L1_ffn_We"].transpose(1, 0, 2).reshape(D, E * D), "be": i["L1_ffn_be"],
    }
    w = {k: np.ascontiguousarray(v) for k, v in w.items()}
    c, ind = _constants()
    x = np.ascontiguousarray(i["L0_attn_x"]).reshape(SEQS * T, D)
    nc = bacc.Bacc("TRN2", target_bir_lowering=False, num_devices=1)
    arrays = {}

    def dram(name, a):
        arrays[name] = a
        return nc.dram_tensor(name, a.shape, mybir.dt.from_np(a.dtype), kind="ExternalInput").ap()

    w_in = {k: dram(f"w_in_{k}", v) for k, v in w.items()}
    c_in = {k: dram(f"c_in_{k}", v) for k, v in c.items()}
    x_in, ind_in = dram("x_dram", x), dram("ind_dram", ind)
    out = nc.dram_tensor("out_dram", x.shape, F32, kind="ExternalOutput").ap()
    model_kernel(nc, x_in, out, w_in, c_in, ind_in)
    r = run_bass_kernel_spmd(nc, [arrays], core_ids=[0])
    return r.results[0]["out_dram"].reshape(SEQS, T, D)
```
